# Optimizing a Trainium2 kernel written in Bass

```python
import numpy as np
import jax
import jax.numpy as jnp

def _softmax(x, axis=-1):
    return jax.nn.softmax(x, axis=axis)

def _gelu(x):
    return jax.nn.gelu(x, approximate=True)

def _silu(x):
    return jax.nn.silu(x)

def _sigmoid(x):
    return jax.nn.sigmoid(x)

def _layernorm(x, axis=-1, eps=1e-05):
    m = jnp.mean(x, axis=axis, keepdims=True)
    v = jnp.var(x, axis=axis, keepdims=True)
    return (x - m) / jnp.sqrt(v + eps)

def _scatter_add(tgt, idx, src, axis=0):
    return tgt.at[idx].add(src)

def _segment_sum(src, seg, n):
    return jax.ops.segment_sum(src, seg, n)
kernel_name = 'mk_gnn_resnorm_d4_gnn_r8_535685'

def setup_inputs(seed: int=0):
    np.random.seed(seed)
    _w = jnp.asarray

    def _rec_inputs():
        import jax
        import jax.numpy as jnp
        _gk = jax.random.key(seed)
        x = -0.0005121 + 1.001 * jax.random.normal(jax.random.fold_in(_gk, 1), (6250, 64), jnp.float32)
        _s = jax.random.randint(jax.random.fold_in(_gk, 2), (100000,), 0, 6250, jnp.int32)
        _d = jax.random.randint(jax.random.fold_in(_gk, 3), (100000,), 0, 6250, jnp.int32)
        _loop = jnp.arange(6250, dtype=jnp.int32)
        src = jnp.concatenate([_s, _d, _loop])
        dst = jnp.concatenate([_d, _s, _loop])
        _o = jnp.argsort(dst, stable=True)
        src = src[_o]
        dst = dst[_o]
        edge_attr_32 = -5.3897e-05 + 0.999841 * jax.random.normal(jax.random.fold_in(_gk, 12), (206250, 32), jnp.float32)
        edge_attr_64 = 7.68618e-05 + 1.00005 * jax.random.normal(jax.random.fold_in(_gk, 13), (206250, 64), jnp.float32)
        return (x, src, dst, edge_attr_32, edge_attr_64)
    x, src, dst, edge_attr_32, edge_attr_64 = _rec_inputs()

    def _L0_gnn_setup():
        import jax, jax.numpy as jnp
        import numpy as np
        N_NODES = 6250
        N_EDGES = 100000
        D_NODE = 64
        D_EDGE = 32
        H_MSG = (2 * D_NODE + D_EDGE) // 2
        H_CMB = 3 * D_NODE // 2

        def _gelu(x):
            return jax.nn.gelu(x, approximate=False)
        key = jax.random.key(seed)
        ks = jax.random.split(key, 11)

        def lin(k, fan_in, fan_out):
            bound = 1.0 / np.sqrt(fan_in)
            k1, k2 = jax.random.split(k)
            W = jax.random.uniform(k1, (fan_in, fan_out), jnp.float32, -bound, bound)
            b = jax.random.uniform(k2, (fan_out,), jnp.float32, -bound, bound)
            return (W, b)
        node_vectors = jax.random.normal(ks[0], (N_NODES, D_NODE), jnp.float32)
        edge_vectors = jax.random.normal(ks[1], (N_EDGES, D_EDGE), jnp.float32)
        edge_indices = jax.random.randint(ks[2], (N_EDGES, 2), 0, N_NODES, jnp.int64 if jax.config.jax_enable_x64 else jnp.int32)
        W_m1, b_m1 = lin(ks[3], 2 * D_NODE + D_EDGE, H_MSG)
        W_m2, b_m2 = lin(ks[4], H_MSG, D_NODE)
        W_c1, b_c1 = lin(ks[5], 2 * D_NODE, H_CMB)
        W_c2, b_c2 = lin(ks[6], H_CMB, D_NODE)
        return {'node_vectors': node_vectors, 'edge_vectors': edge_vectors, 'edge_indices': edge_indices, 'W_m1': W_m1, 'b_m1': b_m1, 'W_m2': W_m2, 'b_m2': b_m2, 'W_c1': W_c1, 'b_c1': b_c1, 'W_c2': W_c2, 'b_c2': b_c2}
    _L0_gnn_all = _L0_gnn_setup()
    _L0_gnn_in = {k: v for k, v in _L0_gnn_all.items() if k in ('W_m1', 'b_m1', 'W_m2', 'b_m2', 'W_c1', 'b_c1', 'W_c2', 'b_c2')}
    del _L0_gnn_all

    def _L1_gnn_setup():
        import jax, jax.numpy as jnp
        import numpy as np
        N_NODES = 12500

        def gcn_conv(x, W, b, src, dst, n):
            h = x @ W
            loop = jnp.arange(n, dtype=src.dtype)
            s = jnp.concatenate([src, loop])
            d = jnp.concatenate([dst, loop])
            deg = jax.ops.segment_sum(jnp.ones_like(d, dtype=h.dtype), d, num_segments=n)
            dinv = jnp.where(deg > 0, jax.lax.rsqrt(deg), 0.0)
            norm = dinv[s] * dinv[d]
            msg = h[s] * norm[:, None]
            out = jax.ops.segment_sum(msg, d, num_segments=n)
            return out + b
        key = jax.random.key(seed)
        k1, k2, k3, k4 = jax.random.split(key, 4)
        n, e = (N_NODES, 200000)
        z = jax.random.normal(k1, (n, 64), dtype=jnp.float32)
        edge_index = jax.random.randint(k2, (2, e), 0, n, dtype=jnp.int64)
        W1 = jax.random.normal(k3, (64, 128), dtype=jnp.float32) * (1.0 / np.sqrt(64))
        b1 = jnp.zeros((128,), dtype=jnp.float32)
        W2 = jax.random.normal(k4, (128, 64), dtype=jnp.float32) * (1.0 / np.sqrt(128))
        b2 = jnp.zeros((64,), dtype=jnp.float32)
        return {'z': z, 'edge_index': edge_index, 'W1': W1, 'b1': b1, 'W2': W2, 'b2': b2}
    _L1_gnn_all = _L1_gnn_setup()
    _L1_gnn_in = {k: v for k, v in _L1_gnn_all.items() if k in ('W1', 'b1', 'W2', 'b2')}
    del _L1_gnn_all

    def _L2_gnn_setup():
        import jax, jax.numpy as jnp
        import numpy as np
        EPS = 1e-05

        def _mlp(h, W, b, gamma, beta):
            h = h @ W + b
            mu = jnp.mean(h, axis=0)
            var = jnp.var(h, axis=0)
            h = (h - mu) * jax.lax.rsqrt(var + EPS) * gamma + beta
            return h * jax.nn.sigmoid(h)
        key = jax.random.key(seed)
        ks = jax.random.split(key, 10)
        N, E, D, G = (12500, 125000, 64, 16)
        x = jax.random.normal(ks[0], (N, D), dtype=jnp.float32)
        edge_index = jax.random.randint(ks[1], (2, E), 0, N, dtype=jnp.int64)
        edge_attr = jax.random.normal(ks[2], (E, D), dtype=jnp.float32)
        u = jax.random.normal(ks[3], (G, D), dtype=jnp.float32)
        batch = jax.random.randint(ks[4], (N,), 0, G, dtype=jnp.int64)
        s1 = 1.0 / np.sqrt(2 * D)
        W1 = jax.random.uniform(ks[5], (2 * D, D), jnp.float32, -s1, s1)
        b1 = jax.random.uniform(ks[6], (D,), jnp.float32, -s1, s1)
        W2 = jax.random.uniform(ks[7], (2 * D, D), jnp.float32, -s1, s1)
        b2 = jax.random.uniform(ks[8], (D,), jnp.float32, -s1, s1)
        g1 = jnp.ones((D,), jnp.float32)
        be1 = jnp.zeros((D,), jnp.float32)
        g2 = jnp.ones((D,), jnp.float32)
        be2 = jnp.zeros((D,), jnp.float32)
        return {'x': x, 'edge_attr': edge_attr, 'u': u, 'W1': W1, 'b1': b1, 'g1': g1, 'be1': be1, 'W2': W2, 'b2': b2, 'g2': g2, 'be2': be2, 'edge_index': edge_index, 'batch': batch}
    _L2_gnn_all = _L2_gnn_setup()
    _L2_gnn_in = {k: v for k, v in _L2_gnn_all.items() if k in ('u', 'W1', 'b1', 'g1', 'be1', 'W2', 'b2', 'g2', 'be2')}
    del _L2_gnn_all

    def _L3_gnn_setup():
        import jax, jax.numpy as jnp
        import numpy as np
        N = 12500
        E = 125000
        IN_DIM = 64
        OUT_DIM = 64
        key = jax.random.key(seed)
        k1, k2, k3, k4 = jax.random.split(key, 4)
        x = jax.random.normal(k1, (N, IN_DIM), dtype=jnp.float32)
        edge_index = jax.random.randint(k2, (2, E), 0, N, dtype=jnp.int64)
        bound = 1.0 / np.sqrt(IN_DIM)
        W = jax.random.uniform(k3, (OUT_DIM, IN_DIM), dtype=jnp.float32, minval=-bound, maxval=bound)
        b = jax.random.uniform(k4, (OUT_DIM,), dtype=jnp.float32, minval=-bound, maxval=bound)
        return {'x': x, 'edge_index': edge_index, 'W': W, 'b': b}
    _L3_gnn_all = _L3_gnn_setup()
    _L3_gnn_in = {k: v for k, v in _L3_gnn_all.items() if k in ('W', 'b')}
    del _L3_gnn_all
    return {'x': x, 'src': src, 'dst': dst, 'edge_attr_32': edge_attr_32, 'edge_attr_64': edge_attr_64, 'L0_gnn_W_m1': _L0_gnn_in['W_m1'], 'L0_gnn_b_m1': _L0_gnn_in['b_m1'], 'L0_gnn_W_m2': _L0_gnn_in['W_m2'], 'L0_gnn_b_m2': _L0_gnn_in['b_m2'], 'L0_gnn_W_c1': _L0_gnn_in['W_c1'], 'L0_gnn_b_c1': _L0_gnn_in['b_c1'], 'L0_gnn_W_c2': _L0_gnn_in['W_c2'], 'L0_gnn_b_c2': _L0_gnn_in['b_c2'], 'L1_gnn_W1': _L1_gnn_in['W1'], 'L1_gnn_b1': _L1_gnn_in['b1'], 'L1_gnn_W2': _L1_gnn_in['W2'], 'L1_gnn_b2': _L1_gnn_in['b2'], 'L2_gnn_u': _L2_gnn_in['u'], 'L2_gnn_W1': _L2_gnn_in['W1'], 'L2_gnn_b1': _L2_gnn_in['b1'], 'L2_gnn_g1': _L2_gnn_in['g1'], 'L2_gnn_be1': _L2_gnn_in['be1'], 'L2_gnn_W2': _L2_gnn_in['W2'], 'L2_gnn_b2': _L2_gnn_in['b2'], 'L2_gnn_g2': _L2_gnn_in['g2'], 'L2_gnn_be2': _L2_gnn_in['be2'], 'L3_gnn_W': _L3_gnn_in['W'], 'L3_gnn_b': _L3_gnn_in['b']}

def reference(x, src, dst, edge_attr_32, edge_attr_64, L0_gnn_W_m1, L0_gnn_b_m1, L0_gnn_W_m2, L0_gnn_b_m2, L0_gnn_W_c1, L0_gnn_b_c1, L0_gnn_W_c2, L0_gnn_b_c2, L1_gnn_W1, L1_gnn_b1, L1_gnn_W2, L1_gnn_b2, L2_gnn_u, L2_gnn_W1, L2_gnn_b1, L2_gnn_g1, L2_gnn_be1, L2_gnn_W2, L2_gnn_b2, L2_gnn_g2, L2_gnn_be2, L3_gnn_W, L3_gnn_b):
    import jax
    import jax.numpy as jnp

    def _L0_gnn_ref(node_vectors, edge_vectors, edge_indices, W_m1, b_m1, W_m2, b_m2, W_c1, b_c1, W_c2, b_c2):
        import jax, jax.numpy as jnp
        import numpy as np
        N_NODES = 6250
        N_EDGES = 100000
        D_NODE = 64
        D_EDGE = 32
        H_MSG = (2 * D_NODE + D_EDGE) // 2
        H_CMB = 3 * D_NODE // 2

        def _gelu(x):
            return jax.nn.gelu(x, approximate=False)
        node_i = node_vectors[edge_indices[:, 0]]
        node_j = node_vectors[edge_indices[:, 1]]
        msg_input = jnp.concatenate([node_i, node_j, edge_vectors], axis=1)
        h = _gelu(msg_input @ W_m1 + b_m1)
        messages = _gelu(h @ W_m2 + b_m2)
        boxes = jax.ops.segment_sum(messages, edge_indices[:, 1], num_segments=node_vectors.shape[0])
        pairs = jnp.concatenate([node_vectors, boxes], axis=1)
        c = _gelu(pairs @ W_c1 + b_c1)
        combined = _gelu(c @ W_c2 + b_c2)
        return node_vectors + combined

    def _L1_gnn_ref(z, edge_index, W1, b1, W2, b2):
        import jax, jax.numpy as jnp
        import numpy as np
        N_NODES = 12500

        def gcn_conv(x, W, b, src, dst, n):
            h = x @ W
            loop = jnp.arange(n, dtype=src.dtype)
            s = jnp.concatenate([src, loop])
            d = jnp.concatenate([dst, loop])
            deg = jax.ops.segment_sum(jnp.ones_like(d, dtype=h.dtype), d, num_segments=n)
            dinv = jnp.where(deg > 0, jax.lax.rsqrt(deg), 0.0)
            norm = dinv[s] * dinv[d]
            msg = h[s] * norm[:, None]
            out = jax.ops.segment_sum(msg, d, num_segments=n)
            return out + b
        n = z.shape[0]
        src, dst = (edge_index[0], edge_index[1])
        h = gcn_conv(z, W1, b1, src, dst, n)
        h = jax.nn.relu(h)
        x_hat = gcn_conv(h, W2, b2, src, dst, n)
        return x_hat

    def _L2_gnn_ref(x, edge_attr, u, W1, b1, g1, be1, W2, b2, g2, be2, edge_index, batch):
        import jax, jax.numpy as jnp
        import numpy as np
        EPS = 1e-05

        def _mlp(h, W, b, gamma, beta):
            h = h @ W + b
            mu = jnp.mean(h, axis=0)
            var = jnp.var(h, axis=0)
            h = (h - mu) * jax.lax.rsqrt(var + EPS) * gamma + beta
            return h * jax.nn.sigmoid(h)
        N = x.shape[0]
        row, col = (edge_index[0], edge_index[1])
        msg = _mlp(jnp.concatenate([x[row], edge_attr], axis=1), W1, b1, g1, be1)
        sums = jax.ops.segment_sum(msg, col, num_segments=N)
        cnt = jax.ops.segment_sum(jnp.ones((msg.shape[0],), msg.dtype), col, num_segments=N)
        agg = sums / jnp.maximum(cnt, 1.0)[:, None]
        return _mlp(jnp.concatenate([x, agg], axis=1), W2, b2, g2, be2)

    def _L3_gnn_ref(x, edge_index, W, b):
        import jax, jax.numpy as jnp
        import numpy as np
        N = 12500
        E = 125000
        IN_DIM = 64
        OUT_DIM = 64
        i = edge_index[0]
        j = edge_index[1]
        msg = x[j] @ W.T + b
        n = x.shape[0]
        out = jax.ops.segment_sum(msg, i, num_segments=n)
        deg = jax.ops.segment_sum(jnp.ones((i.shape[0],), dtype=msg.dtype), i, num_segments=n)
        deg = jnp.maximum(deg, 1.0)[:, None]
        return out / deg
    edge_index = jnp.stack([src, dst])
    edge_index_t = jnp.stack([src, dst], axis=1)
    batch0 = jnp.zeros((6250,), jnp.int32)
    x = _layernorm(x + _L0_gnn_ref(x, edge_attr_32, edge_index_t, L0_gnn_W_m1, L0_gnn_b_m1, L0_gnn_W_m2, L0_gnn_b_m2, L0_gnn_W_c1, L0_gnn_b_c1, L0_gnn_W_c2, L0_gnn_b_c2), axis=-1)
    x = _layernorm(x + _L1_gnn_ref(x, edge_index, L1_gnn_W1, L1_gnn_b1, L1_gnn_W2, L1_gnn_b2), axis=-1)
    x = _layernorm(x + _L2_gnn_ref(x, edge_attr_64, L2_gnn_u, L2_gnn_W1, L2_gnn_b1, L2_gnn_g1, L2_gnn_be1, L2_gnn_W2, L2_gnn_b2, L2_gnn_g2, L2_gnn_be2, edge_index, batch0), axis=-1)
    x = _layernorm(x + _L3_gnn_ref(x, edge_index, L3_gnn_W, L3_gnn_b), axis=-1)
    return x

_drawn_inputs = setup_inputs


def setup_inputs(seed=0):
    import zlib

    import numpy as np

    out = dict(_drawn_inputs(seed))
    spreads = {'L1_gnn_b1': (0.0, 0.1),
     'L1_gnn_b2': (0.0, 0.1),
     'L2_gnn_g1': (1.0, 0.6),
     'L2_gnn_be1': (0.0, 2.0),
     'L2_gnn_g2': (1.0, 0.2),
     'L2_gnn_be2': (0.0, 0.1)}
    factors = {'edge_attr_32': 4.642,
     'L0_gnn_b_m1': 4.173,
     'L0_gnn_b_c1': 7.397,
     'L0_gnn_b_c2': 3.328,
     'L2_gnn_b1': 64.0,
     'L2_gnn_b2': 64.0}
    for name, (base, spread) in spreads.items():
        noise = np.random.default_rng([zlib.crc32(name.encode()), seed]).standard_normal(out[name].shape)
        drawn = base * np.exp(spread * noise) if base else spread * noise
        out[name] = jnp.asarray(drawn.astype(out[name].dtype))
    for name, factor in factors.items():
        out[name] = (out[name] * factor).astype(out[name].dtype)
    return out
```

```python
def build(nc, P, out):
    import concourse.bass as bass
    from concourse import mybir
    from contextlib import ExitStack, contextmanager

    fp32, i32 = mybir.dt.float32, mybir.dt.int32
    ALU, ACT, AX = mybir.AluOpType, mybir.ActivationFunctionType, mybir.AxisListType

    N, D = P["x"].shape
    E, DE = P["edge_attr_32"].shape
    H = P["L0_gnn_W_m1"].shape[1]
    HC = P["L0_gnn_W_c1"].shape[1]
    H1 = P["L1_gnn_W1"].shape[1]
    SUB, LANES = 4, 128
    GE = SUB * LANES
    NG = -(-E // GE)
    NT = -(-(N + 1) // GE)
    NP = NT * GE
    W = 32
    TAIL = E - (NG - 1) * GE
    TROWS = TAIL // SUB
    TLEFT = TAIL - TROWS * SUB
    NFULL = N // GE
    NREST = (N - NFULL * GE) // SUB
    NLEFT = N - NFULL * GE - NREST * SUB
    EPS = 1e-5
    TABLES = 8
    SROWS = NP + 1 + LANES
    CR = 4

    def done(n):
        return n + (1 + CR)

    def rounds(eng, step, total, unroll):
        with eng.Fori(0, total // unroll) as i:
            for k in range(unroll):
                step(i, k)
        for k in range(total % unroll):
            step(total // unroll, k)

    def dram(name, shape, dt=fp32):
        return nc.dram_tensor(name, shape, dt).ap()

    src_pad = dram("src_pad", (NG * GE,), i32)
    dst_pad = dram("dst_pad", (NG * GE,), i32)
    tab_a = dram("tab_a", (NP + 1, H))
    tab_b = dram("tab_b", (NP + W, H))
    tab_y1 = dram("tab_y1", (NP + 1, D))
    tab_y2 = dram("tab_y2", (NP + 1, D))
    tab_t2 = dram("tab_t2", (NP + 1, D))
    tab_x3 = dram("tab_x3", (NP + W, D))
    h_edges = dram("h_edges", (NG * GE, D))
    cnt_dram = dram("cnt_dram", (NP,))
    scat = [dram(f"scat{q}", (SROWS, D + 1)) for q in range(TABLES)]

    def groups(ap):
        return ap.rearrange("(g p s) -> g p s", p=LANES, s=SUB)

    def group_rows(ap, g):
        v = ap[0:(ap.shape[0] // GE) * GE, :].rearrange("(g p s) f -> g p (s f)", p=LANES, s=SUB)
        return v[bass.ds(g, 1)].rearrange("a p f -> (a p) f")

    whole = ExitStack()
    with whole:
        def sb(name, shape, dt=fp32, ctx=whole):
            return ctx.enter_context(nc.sbuf_tensor(name, shape, dt))

        ident = sb("ident", [128, 128])
        iota_w = sb("iota_w", [128, SUB, W])
        rel = sb("rel", [128, NG, SUB])
        src_f = sb("src_f", [128, NG, SUB])
        base = sb("base", [1, NG], i32)
        flag = sb("flag", [1, 1], i32)
        iota_n = sb("iota_n", [128, GE])
        acc = sb("acc", [D + 1, NP])
        x_nm = sb("x_nm", [128, NT, SUB, D])
        z_nm = sb("z_nm", [128, NT, SUB, D])
        cnt_nm = sb("cnt_nm", [128, NT, SUB])
        dinv_nm = sb("dinv_nm", [128, NT, SUB])
        w_ab = sb("w_ab", [D, 2, H])
        w_m2 = sb("w_m2", [H + 1, D])
        b_m1 = sb("b_m1", [H, 1])
        w_c1x = sb("w_c1x", [D, HC])
        w_c1a = sb("w_c1a", [D + 1, HC])
        b_c1 = sb("b_c1", [HC, 1])
        w_c2 = sb("w_c2", [HC + 1, D])
        w_g1 = sb("w_g1", [D, H1])
        b_g1 = sb("b_g1", [H1, 1])
        w_g2 = sb("w_g2", [H1, D])
        b_g2 = sb("b_g2", [128, D])
        w_e1x = sb("w_e1x", [D, D])
        w_e1e = sb("w_e1e", [D, D])
        row_b1 = sb("row_b1", [128, D])
        row_g1 = sb("row_g1", [128, D])
        row_be1 = sb("row_be1", [128, D])
        w_n2x = sb("w_n2x", [D, 2 * D])
        w_n2a = sb("w_n2a", [D, 2 * D])
        col_n2 = sb("col_n2", [D, 3])
        w_3 = sb("w_3", [D + 1, D])
        bn_scale = sb("bn_scale", [128, D])
        bn_shift = sb("bn_shift", [128, D])
        ones_sq = sb("ones_sq", [128, 128])
        lower = sb("lower", [128, 128])
        spare = sb("spare", [128, 1])

        def stage_semaphores(c, prefix):
            own = []

            def sem(name):
                own.append(c.enter_context(nc.semaphore(prefix + name)))
                return own[-1]
            return sem, own

        @contextmanager
        def stage_block(own):
            with nc.Block() as block:
                yield block
            with nc.Block() as after:
                @after.gpsimd
                def _(pool):
                    for s_ in own:
                        pool.sem_clear(s_)

        def gather_sem(name):
            return whole.enter_context(nc.semaphore(name))

        def linker(eng, sem):
            count = [0]

            def link(ins):
                count[0] += 1
                ins.then_inc(sem, 1)
                eng.wait_ge(sem, count[0])
            return link

        def bc_last(ap, n):
            return ap.unsqueeze(len(ap.shape)).to_broadcast(list(ap.shape) + [n])

        with ExitStack() as c, nc.allow_non_contiguous_dma(reason="index columns, once"):
            sem, own = stage_semaphores(c, "")
            pads_set, s_pads, s_load, s_padded = sem("pads_set"), sem("s_pads"), sem("s_load"), sem("s_padded")
            s_idx, consts, vchain, base_ready, base_spread = sem("s_idx"), sem("consts"), sem("vchain"), sem("base_ready"), sem("base_spread")
            s_zero, clears = sem("s_zero"), sem("clears")
            pad_src = sb("pad_src", [1, GE], i32, c)
            pad_dst = sb("pad_dst", [1, GE], i32, c)
            dst_i = sb("dst_i", [128, NG, SUB], i32, c)
            src_i = sb("src_i", [128, NG, SUB], i32, c)
            base_row = sb("base_row", [1, NG], fp32, c)
            base_f = sb("base_f", [128, NG], fp32, c)
            outside = sb("outside", [128, 2], fp32, c)
            outside_ready, outside_all = sem("outside_ready"), sem("outside_all")
            zeros = sb("zeros", [128, GE], fp32, c)
            block = c.enter_context(stage_block(own))
            loads = [
                (w_ab[:, 0, :], P["L0_gnn_W_m1"][0:D, :]), (w_ab[:, 1, :], P["L0_gnn_W_m1"][D:2 * D, :]),
                (w_m2[0:H, :], P["L0_gnn_W_m2"]), (w_m2[H:H + 1, :], P["L0_gnn_b_m2"].unsqueeze(0)),
                (b_m1[:, :], P["L0_gnn_b_m1"].unsqueeze(1)),
                (w_c1x[:, :], P["L0_gnn_W_c1"][0:D, :]), (w_c1a[1:D + 1, :], P["L0_gnn_W_c1"][D:2 * D, :]),
                (b_c1[:, :], P["L0_gnn_b_c1"].unsqueeze(1)),
                (w_c2[0:HC, :], P["L0_gnn_W_c2"]), (w_c2[HC:HC + 1, :], P["L0_gnn_b_c2"].unsqueeze(0)),
                (w_g1[:, :], P["L1_gnn_W1"]), (b_g1[:, :], P["L1_gnn_b1"].unsqueeze(1)), (w_g2[:, :], P["L1_gnn_W2"]),
                (b_g2[:, :], P["L1_gnn_b2"].unsqueeze(0).to_broadcast([128, D])),
                (w_e1x[:, :], P["L2_gnn_W1"][0:D, :]), (w_e1e[:, :], P["L2_gnn_W1"][D:2 * D, :]),
                (row_b1[:, :], P["L2_gnn_b1"].unsqueeze(0).to_broadcast([128, D])),
                (row_g1[:, :], P["L2_gnn_g1"].unsqueeze(0).to_broadcast([128, D])),
                (row_be1[:, :], P["L2_gnn_be1"].unsqueeze(0).to_broadcast([128, D])),
                (w_n2x[:, 0:D], P["L2_gnn_W2"][0:D, :]), (w_n2a[:, 0:D], P["L2_gnn_W2"][D:2 * D, :]),
                (col_n2[:, 0:1], P["L2_gnn_b2"].unsqueeze(1)), (col_n2[:, 1:2], P["L2_gnn_g2"].unsqueeze(1)),
                (col_n2[:, 2:3], P["L2_gnn_be2"].unsqueeze(1)),
                (w_3[0:D, :], P["L3_gnn_W_t"]), (w_3[D:D + 1, :], P["L3_gnn_b"].unsqueeze(0)),
                (x_nm[:, 0:NFULL].rearrange("p t j f -> p t (j f)"),
                 P["x"][0:NFULL * GE, :].rearrange("(t p j) f -> p t (j f)", p=LANES, j=SUB)),
                (x_nm[0:NREST, NFULL].rearrange("p j f -> p (j f)"),
                 P["x"][NFULL * GE:NFULL * GE + NREST * SUB, :].rearrange("(p j) f -> p (j f)", j=SUB)),
                (x_nm[NREST:NREST + 1, NFULL, 0:NLEFT].rearrange("p j f -> p (j f)"),
                 P["x"][N - NLEFT:N, :].rearrange("(p j) f -> p (j f)", j=NLEFT)),
            ]

            @block.sync
            def _(sp):
                sp.dma_start(src_pad[0:E], P["src"]).then_inc(s_padded, 16)
                sp.dma_start(dst_pad[0:E], P["dst"]).then_inc(s_padded, 16)
                sp.wait_ge(pads_set, 2)
                sp.dma_start(src_pad[E:NG * GE].unsqueeze(0), pad_src[:, 0:NG * GE - E]).then_inc(s_padded, 16)
                sp.dma_start(dst_pad[E:NG * GE].unsqueeze(0), pad_dst[:, 0:NG * GE - E]).then_inc(s_padded, 16)
                sp.wait_ge(clears, 5)
                for to, of in loads:
                    sp.dma_start(to, of).then_inc(s_load, 16)
                sp.wait_ge(s_padded, 64)
                sp.dma_start(dst_i[:, :, :], groups(dst_pad).rearrange("g p s -> p g s")).then_inc(s_idx, 16)
                sp.dma_start(src_i[:, :, :], groups(src_pad).rearrange("g p s -> p g s")).then_inc(s_idx, 16)
                sp.dma_start(base[:, :], dst_pad.rearrange("(a g e) -> a g e", a=1, e=GE)[:, :, 0]).then_inc(s_idx, 16)
                sp.wait_ge(consts, 1)
                for tab in (tab_a, tab_y1, tab_y2, tab_t2):
                    sp.dma_start(tab[NP:NP + 1, :], zeros[0:1, 0:tab.shape[1]]).then_inc(s_zero, 16)
                for tab in (tab_b, tab_x3):
                    sp.dma_start(tab[NP:NP + W, :], zeros[0:W, 0:tab.shape[1]]).then_inc(s_zero, 16)
                sp.wait_ge(s_zero, 6 * 16)
                sp.wait_ge(s_load, len(loads) * 16)

            @block.gpsimd
            def _(pool):
                pool.memset(pad_src[:, :], NP).then_inc(pads_set, 1)
                pool.memset(pad_dst[:, :], N).then_inc(pads_set, 1)
                pool.memset(x_nm[:, NT - 1], 0.0).then_inc(clears, 1)
                pool.memset(w_c1a[0:1, :], 0.0).then_inc(clears, 1)
                pool.memset(acc[:, :], 0.0).then_inc(clears, 1)
                pool.memset(w_n2x[:, D:2 * D], 0.0).then_inc(clears, 1)
                pool.memset(w_n2a[:, D:2 * D], 0.0).then_inc(clears, 1)
                pool.memset(zeros[:, :], 0.0).then_inc(consts, 1)
                pool.memset(ones_sq[:, :], 1.0).then_inc(consts, 1)
                pool.memset(ident[:, :], 0.0).then_inc(consts, 1)
                pool.wait_ge(consts, 3)
                pool.affine_select(out=ident[:, :], in_=ident[:, :], compare_op=ALU.not_equal, fill=1.0,
                                   base=0, pattern=[[-1, 128]], channel_multiplier=1).then_inc(consts, 1)
                pool.affine_select(out=lower[:, :], in_=ones_sq[:, :], compare_op=ALU.is_gt, fill=0.0,
                                   base=0, pattern=[[-1, 128]], channel_multiplier=1).then_inc(consts, 1)
                pool.iota(iota_w[:, :, :], pattern=[[0, SUB], [1, W]], base=0, channel_multiplier=0,
                          allow_small_or_imprecise_dtypes=True).then_inc(consts, 1)
                pool.iota(iota_n[:, :], pattern=[[1, GE]], base=0, channel_multiplier=0,
                          allow_small_or_imprecise_dtypes=True).then_inc(consts, 1)
                pool.iota(spare[:, :], pattern=[[0, 1]], base=NP + 1, channel_multiplier=1,
                          allow_small_or_imprecise_dtypes=True).then_inc(consts, 1)
                pool.wait_ge(base_ready, 1)
                pool.partition_broadcast(base_f[:, :], base_row[:, :], 128).then_inc(base_spread, 1)
                pool.wait_ge(outside_ready, 1)
                pool.partition_all_reduce(outside[:, :], outside[:, :], 128, bass.bass_isa.ReduceOp.max).then_inc(outside_all, 1)

            @block.vector
            def _(dve):
                dve.wait_ge(s_idx, 48)
                nc.vector.tensor_copy(base_row[:, :], base[:, :]).then_inc(base_ready, 1)
                nc.vector.tensor_copy(src_f[:, :, :], src_i[:, :, :])
                nc.vector.tensor_copy(rel[:, :, :], dst_i[:, :, :]).then_inc(vchain, 1)
                dve.wait_ge(vchain, 1)
                dve.wait_ge(base_spread, 1)
                nc.vector.tensor_tensor(rel[:, :, :], rel[:, :, :], bc_last(base_f[:, :], SUB), ALU.subtract).then_inc(vchain, 1)
                dve.wait_ge(vchain, 2)
                rel_flat = rel[:, :, :].rearrange("p g s -> p (g s)")
                nc.vector.tensor_reduce(outside[:, 0:1], rel_flat, AX.X, ALU.max)
                nc.vector.tensor_reduce(outside[:, 1:2], rel_flat, AX.X, ALU.min).then_inc(vchain, 1)
                dve.wait_ge(vchain, 3)
                nc.vector.tensor_scalar(outside[:, 0:1], outside[:, 0:1], float(W - 1), None, ALU.subtract)
                nc.vector.tensor_scalar(outside[:, 1:2], outside[:, 1:2], -1.0, None, ALU.mult).then_inc(outside_ready, 1)
                dve.wait_ge(outside_all, 1)
                nc.vector.tensor_tensor(outside[0:1, 0:1], outside[0:1, 0:1], outside[0:1, 1:2], ALU.max).then_inc(vchain, 1)
                dve.wait_ge(vchain, 4)
                nc.vector.tensor_scalar(flag[:, :], outside[0:1, 0:1], 0.0, None, ALU.is_gt)

        def general_path(c, sem, name, width, target, tabs, message_tile, ps, after=()):
            class gen:
                pass
            gen.begun, gen.loaded, gen.message, gen.hot, gen.summed, gen.added, gen.turn, gen.lowered = (
                sem(f"gen_{n}") for n in ("begun", "loaded", "message", "hot", "summed", "added", "turn", "lowered"))
            gen.gathered = gather_sem(f"{name}_gen_gathered") if tabs else gen.loaded
            target_i = sb(f"{name}_gen_target_i", [128, SUB], i32, c)
            target_f = sb(f"{name}_gen_target_f", [128, SUB], ctx=c)
            index = [sb(f"{name}_gen_index{n}", [128, SUB], i32, c) for n in range(len(tabs))]
            onehot = sb(f"{name}_gen_onehot", [128, SUB, GE], ctx=c)
            gen.per_group = (1 + len(tabs)) * 16

            def each_group(eng, step):
                with eng.Fori(0, NG - 1) as g:
                    step(g)
                step(NG - 1)
            gen.each_group = each_group

            def sync(sp, load=None):
                def step(g):
                    g = sp.snap(g) if not isinstance(g, int) else g
                    sp.wait_ge(gen.begun, g + 1)
                    sp.dma_start(target_i[:, :], group_rows(target.unsqueeze(1), g)).then_inc(gen.loaded, 16)
                    for n, (_, indices, _) in enumerate(tabs):
                        sp.dma_start(index[n][:, :], group_rows(indices.unsqueeze(1), g)).then_inc(gen.loaded, 16)
                    if load is not None:
                        load(g)
                each_group(sp, step)
            gen.sync = sync

            def gpsimd(pool):
                def step(g):
                    pool.wait_ge(gen.loaded, (g + 1) * gen.per_group)
                    pool.sem_inc(gen.turn, 1)
                    for n, (tab, _, to) in enumerate(tabs):
                        for s in range(SUB):
                            nc.gpsimd.indirect_dma_start(
                                out=to[:, s, :], out_offset=None, in_=tab,
                                in_offset=bass.IndirectOffsetOnAxis(ap=index[n][:, s:s + 1], axis=0)).then_inc(gen.gathered, 16)
                each_group(pool, step)
            gen.gpsimd = gpsimd
            gen.rows_in = len(tabs) * SUB * 16

            def vector(dve, make=None):
                dve.sem_inc(gen.begun, 1)

                def step(g):
                    dve.wait_ge(gen.loaded, (g + 1) * gen.per_group)
                    nc.vector.tensor_copy(target_f[:, :], target_i[:, :]).then_inc(gen.lowered, 1)
                    if make is not None:
                        make(g)

                    def block(v):
                        dve.wait_ge(gen.lowered, (g * (NT + 1) + v) + 1)
                        nc.vector.tensor_tensor(onehot[:, :, :], iota_n[:, :].unsqueeze(1).to_broadcast([128, SUB, GE]),
                                                bc_last(target_f[:, :], GE), ALU.is_equal).then_inc(gen.hot, 1)
                        dve.wait_ge(gen.hot, (g * NT + v) + 1)
                        nc.vector.tensor_scalar(target_f[:, :], target_f[:, :], float(GE), None, ALU.subtract).then_inc(gen.lowered, 1)
                        dve.wait_ge(gen.summed, (g * NT + v) + 1)
                        nc.vector.tensor_tensor(acc[0:width, bass.ds(v * GE, GE)], acc[0:width, bass.ds(v * GE, GE)], ps[0:width, :], ALU.add).then_inc(gen.added, 1)
                    with dve.Fori(0, NT) as v:
                        block(v)
                    dve.wait_ge(gen.lowered, (g + 1) * (NT + 1))
                    dve.wait_ge(gen.added, (g + 1) * NT)
                    dve.sem_inc(gen.begun, 1)
                each_group(dve, step)
            gen.vector = vector

            def tensor(pe, make=None):
                def step(g):
                    if make is not None:
                        make(g)

                    def block(v):
                        if make is not None or not tabs:
                            pe.wait_ge(gen.message, g + 1)
                        else:
                            pe.wait_ge(gen.gathered, (g + 1) * gen.rows_in)
                        pe.wait_ge(gen.hot, (g * NT + v) + 1)
                        pe.sem_inc(gen.turn_pe, 1)
                        for s in range(SUB):
                            last = nc.tensor.matmul(ps[0:width, :], message_tile[:, s, 0:width], onehot[:, s, :], start=s == 0, stop=s == SUB - 1)
                        last.then_inc(gen.summed, 1)
                    with pe.Fori(0, NT) as v:
                        block(v)
                each_group(pe, step)
            gen.turn_pe = sem("gen_turn_pe")
            gen.tensor = tensor
            return gen

        def by_flag(eng, general, windows):
            outside_some = eng.value_load(flag[0:1, 0:1], min_val=0, max_val=1)
            with eng.If(outside_some):
                general()
            with eng.Else():
                windows()

        with ExitStack() as c:
            sem, own = stage_semaphores(c, "")
            staged, turned, turned_sb, product, tables_sb = (sem(f"ta_{n}") for n in ("staged", "turned", "turned_sb", "product", "tables_sb"))
            s_store = [sem(f"ta_store{k}") for k in range(2)]
            stored, pe_turn = sem("ta_stored"), sem("ta_pe_turn")
            xs = sb("xs", [128, 2, SUB, D], ctx=c)
            xts = sb("xts", [D, 2, GE], ctx=c)
            tabs = sb("tabs", [128, 2, 2, SUB * H], ctx=c)
            ps_t = [c.enter_context(nc.psum_tensor(f"ta_t{k}", [128, 512], fp32)) for k in range(2)]
            ps_p = [c.enter_context(nc.psum_tensor(f"ta_p{k}", [128, 512], fp32)) for k in range(4)]
            block = c.enter_context(stage_block(own))

            @block.vector
            def _(dve):
                dve.sem_inc(staged, CR)
                dve.sem_inc(tables_sb, CR)

                def step(i, k):
                    t = i * 2 + k
                    dve.wait_ge(turned, done(t - 2))
                    nc.vector.tensor_copy(xs[:, k], x_nm[:, bass.ds(t, 1)].rearrange("p a j f -> p (a j) f")).then_inc(staged, 1)
                    dve.wait_ge(stored, done(t - 2))
                    dve.wait_ge(product, done(t))
                    nc.vector.tensor_copy(tabs[:, k, 0, :], ps_p[2 * k][:, 0:SUB * H])
                    nc.vector.tensor_copy(tabs[:, k, 1, :], ps_p[2 * k + 1][:, 0:SUB * H]).then_inc(tables_sb, 1)
                rounds(dve, step, NT, 2)

            @block.tensor
            def _(pe):
                pe.sem_inc(turned, CR)
                pe.sem_inc(product, CR)

                def step(i, k):
                    t = i * 2 + k
                    pe.wait_ge(staged, done(t))
                    pe.wait_ge(turned_sb, done(t - 2))
                    pe.sem_inc(pe_turn, 1)
                    for j in range(SUB):
                        last = nc.tensor.transpose(ps_t[k][0:D, j * 128:(j + 1) * 128], xs[:, k, j, :], ident[:, :])
                    last.then_inc(turned, 1)
                    pe.wait_ge(turned_sb, done(t))
                    pe.wait_ge(tables_sb, done(t - 2))
                    for q in range(2):
                        for j in range(SUB):
                            last = nc.tensor.matmul(ps_p[2 * k + q][:, j * H:(j + 1) * H], xts[:, k, j * 128:(j + 1) * 128],
                                                    w_ab[:, q, :], start=True, stop=True)
                    last.then_inc(product, 1)
                rounds(pe, step, NT, 2)

            @block.scalar
            def _(act):
                act.sem_inc(turned_sb, CR)

                def step(i, k):
                    t = i * 2 + k
                    act.wait_ge(turned, done(t))
                    act.wait_ge(product, done(t - 2))
                    nc.scalar.copy(xts[:, k, :], ps_t[k][0:D, :]).then_inc(turned_sb, 1)
                rounds(act, step, NT, 2)

            @block.sync
            def _(sp):
                sp.sem_inc(stored, CR)

                def step(i, k):
                    t = sp.snap(i * 2 + k) if not isinstance(i, int) else i * 2 + k
                    sp.wait_ge(tables_sb, done(t))
                    sp.dma_start(group_rows(tab_a, t), tabs[:, k, 0, :]).then_inc(s_store[k], 16)
                    sp.dma_start(group_rows(tab_b, t), tabs[:, k, 1, :]).then_inc(s_store[k], 16)
                    sp.wait_ge(s_store[k], (i + 1) * 32)
                    sp.sem_inc(stored, 1)
                rounds(sp, step, NT, 2)

        with ExitStack() as c:
            sem, own = stage_semaphores(c, "")
            s_idx = [sem(f"l0_idx{k}") for k in range(4)]
            s_att = [sem(f"l0_att{k}") for k in range(4)]
            s_win = [sem(f"l0_win{k}") for k in range(4)]
            pe_turn = sem("l0_pe_turn")
            s_rows = [gather_sem(f"l0_rows{k}") for k in range(4)]
            pool_turn = sem("l0_pool_turn")
            combined, turned, turned_sb, hidden, hidden_sb, message, message_sb, summed, added = (
                sem(f"l0_{n}") for n in ("combined", "turned", "turned_sb", "hidden", "hidden_sb", "message", "message_sb", "summed", "added"))
            cleared, w_loaded = sem("l0_cleared"), sem("l0_w_loaded")
            idx = sb("l0_idx_t", [128, 4, SUB], i32, c)
            att = sb("l0_att_t", [128, 4, SUB, DE], ctx=c)
            rows = sb("l0_rows_t", [128, 4, SUB, H], ctx=c)
            comb = sb("l0_comb", [128, 4, SUB, DE + W], ctx=c)
            comb_t = sb("l0_comb_t", [DE + W, 2, GE], ctx=c)
            w_ew = sb("l0_w_ew", [DE + W, 4, H], ctx=c)
            hid = sb("l0_hid", [128, 2, GE], ctx=c)
            msg = sb("l0_msg", [128, 2, SUB, 1 + D], ctx=c)
            ps_t = [c.enter_context(nc.psum_tensor(f"l0_ps_t{k}", [128, 512], fp32)) for k in range(2)]
            ps_h = [c.enter_context(nc.psum_tensor(f"l0_ps_h{k}", [128, 512], fp32)) for k in range(2)]
            ps_m = [c.enter_context(nc.psum_tensor(f"l0_ps_m{k}", [128, 512], fp32)) for k in range(2)]
            ps_s = [c.enter_context(nc.psum_tensor(f"l0_ps_s{k}", [128, 512], fp32)) for k in range(2)]
            gen = general_path(c, sem, "l0", 1 + D, dst_pad, [(tab_a, src_pad, rows[:, 0]), (tab_b, dst_pad, rows[:, 1])], msg[:, 0], ps_s[0])
            gen_att, gen_turned, gen_turned_sb, gen_hidden, gen_hidden_sb, gen_product = (
                sem(f"l0_gen_{n}") for n in ("att", "turned", "turned_sb", "hidden", "hidden_sb", "product"))
            block = c.enter_context(stage_block(own))
            att_dram = P["edge_attr_32"]

            @block.sync
            def _(sp):
                for k in range(4):
                    sp.dma_start(w_ew[0:DE, k, :], P["L0_gnn_W_m1"][2 * D:2 * D + DE, :]).then_inc(w_loaded, 16)

                def general():
                    def load(g):
                        if isinstance(g, int):
                            sp.dma_start(att[0:TROWS, 0], att_dram[(NG - 1) * GE:E - TLEFT, :].rearrange("(p s) f -> p s f", s=SUB)).then_inc(gen_att, 16)
                            sp.dma_start(att[TROWS:TROWS + 1, 0, 0:TLEFT], att_dram[E - TLEFT:E, :].unsqueeze(0)).then_inc(gen_att, 16)
                        else:
                            sp.dma_start(att[:, 0].rearrange("p s f -> p (s f)"), group_rows(att_dram, g)).then_inc(gen_att, 16)
                    gen.sync(sp, load)

                def windows():
                    def step(i, k):
                        g = i * 4 + k
                        start = sp.value_load(base[0:1, bass.ds(g, 1)], min_val=0, max_val=N)
                        g = sp.snap(g) if not isinstance(g, int) else g
                        sp.wait_ge(message_sb, done(g - 4))
                        sp.dma_start(idx[:, k, :], group_rows(src_pad.unsqueeze(1), g)).then_inc(s_idx[k], 16)
                        if isinstance(i, int) and g == NG - 1:
                            sp.dma_start(att[0:TROWS, k], att_dram[(NG - 1) * GE:E - TLEFT, :].rearrange("(p s) f -> p s f", s=SUB)).then_inc(s_att[k], 16)
                            sp.dma_start(att[TROWS:TROWS + 1, k, 0:TLEFT], att_dram[E - TLEFT:E, :].unsqueeze(0)).then_inc(s_att[k], 16)
                        else:
                            sp.dma_start(att[:, k].rearrange("p s f -> p (s f)"), group_rows(att_dram, g)).then_inc(s_att[k], 16)
                        sp.dma_start(w_ew[DE:DE + W, k, :], tab_b[bass.ds(start, W), :]).then_inc(s_win[k], 16)
                    rounds(sp, step, NG, 4)

                by_flag(sp, general, windows)

            @block.gpsimd
            def _(pool):
                def general():
                    gen.gpsimd(pool)

                def windows():
                    def step(i, k):
                        pool.wait_ge(s_idx[k], (i + 1) * 16)
                        pool.sem_inc(pool_turn, 1)
                        for s in range(SUB):
                            nc.gpsimd.indirect_dma_start(
                                out=rows[:, k, s, :], out_offset=None, in_=tab_a,
                                in_offset=bass.IndirectOffsetOnAxis(ap=idx[:, k, s:s + 1], axis=0)).then_inc(s_rows[k], 16)
                    rounds(pool, step, NG, 4)

                by_flag(pool, general, windows)

            @block.vector
            def _(dve):
                nc.vector.memset(msg[:, :, :, 0:1], 1.0)
                nc.vector.memset(hid[64:128, :, :], 1.0).then_inc(cleared, 1)
                def general():
                    gen.vector(dve)

                def windows():
                    dve.sem_inc(combined, CR)
                    dve.sem_inc(added, CR)

                    def combine(i, k):
                        i, k = i + k // 4, k % 4
                        g = i * 4 + k
                        dve.wait_ge(summed, done(g - 4))
                        nc.vector.tensor_tensor(comb[:, k, :, DE:DE + W], iota_w[:, :, :],
                                                bc_last(rel[:, bass.ds(g, 1), :].rearrange("p a s -> p (a s)"), W), ALU.is_equal)
                        last = isinstance(i, int) and g == NG - 1
                        dve.wait_ge(s_att[k], (i + 1 + last) * 16)
                        nc.vector.tensor_copy(comb[:, k, :, 0:DE], att[:, k]).then_inc(combined, 1)

                    for k in range(4):
                        combine(0, k)

                    def step(i, k):
                        g = i * 4 + k
                        if not isinstance(i, int) or g + 4 < NG:
                            combine(i, k + 4) if not isinstance(i, int) or g + 4 < NG else None
                        start = dve.value_load(base[0:1, bass.ds(g, 1)], min_val=0, max_val=N)
                        dve.wait_ge(summed, done(g))
                        dve.wait_ge(added, done(g - 1))
                        nc.vector.tensor_tensor(acc[:, bass.ds(start, W)], acc[:, bass.ds(start, W)], ps_s[k % 2][0:D + 1, 0:W], ALU.add).then_inc(added, 1)

                    with dve.Fori(0, (NG - 4) // 4) as i:
                        for k in range(4):
                            step(i, k)
                    for k in range(NG - (NG - 4) // 4 * 4):
                        step((NG - 4) // 4 + k // 4, k % 4)

                by_flag(dve, general, windows)

            @block.tensor
            def _(pe):
                pe.wait_ge(w_loaded, 64)
                pe.wait_ge(cleared, 1)
                def general():
                    def make(g):
                        pe.wait_ge(gen_att, (g + 1 + isinstance(g, int)) * 16)
                        pe.sem_inc(pe_turn, 1)
                        for s in range(SUB):
                            last = nc.tensor.transpose(ps_t[0][0:DE, s * 128:(s + 1) * 128], att[:, 0, s, :], ident[:, :])
                        last.then_inc(gen_turned, 1)
                        pe.wait_ge(gen_turned_sb, g + 1)
                        pe.wait_ge(gen.gathered, (g + 1) * gen.rows_in)
                        pe.sem_inc(pe_turn, 1)
                        nc.tensor.matmul(ps_h[0][0:H, :], w_ew[0:DE, 0, :], comb_t[0:DE, 0, :], start=True, stop=False)
                        for n in range(2):
                            for s in range(SUB):
                                last = nc.tensor.matmul(ps_h[0][0:H, s * 128:(s + 1) * 128], rows[:, n, s, :], ident[:, :],
                                                        start=False, stop=n == 1 and s == SUB - 1)
                        last.then_inc(gen_hidden, 1)
                        pe.wait_ge(gen_hidden_sb, g + 1)
                        for s in range(SUB):
                            last = nc.tensor.matmul(ps_m[0][:, s * D:(s + 1) * D], hid[0:H + 1, 0, s * 128:(s + 1) * 128],
                                                    w_m2[:, :], start=True, stop=True)
                        last.then_inc(gen_product, 1)
                    gen.tensor(pe, make)

                def windows():
                    for s_ in (turned, hidden, message, summed):
                        pe.sem_inc(s_, CR)

                    def turn(i, k):
                        i, k = i + k // 4, k % 4
                        g = i * 4 + k
                        pe.wait_ge(combined, done(g))
                        pe.wait_ge(turned_sb, done(g - 2))
                        pe.sem_inc(pe_turn, 1)
                        for s in range(SUB):
                            last = nc.tensor.transpose(ps_t[k % 2][0:DE + W, s * 128:(s + 1) * 128], comb[:, k, s, :], ident[:, :])
                        last.then_inc(turned, 1)

                    def hide(i, k):
                        i, k = i + k // 4, k % 4
                        g = i * 4 + k
                        pe.wait_ge(turned_sb, done(g))
                        pe.wait_ge(hidden_sb, done(g - 2))
                        pe.wait_ge(s_win[k], (i + 1) * 16)
                        nc.tensor.matmul(ps_h[k % 2][0:H, :], w_ew[:, k, :], comb_t[:, k % 2, :], start=True, stop=False)
                        pe.wait_ge(s_rows[k], (i + 1) * 64)
                        for s in range(SUB):
                            last = nc.tensor.matmul(ps_h[k % 2][0:H, s * 128:(s + 1) * 128], rows[:, k, s, :], ident[:, :],
                                                    start=False, stop=s == SUB - 1)
                        last.then_inc(hidden, 1)

                    def messages(i, k):
                        i, k = i + k // 4, k % 4
                        g = i * 4 + k
                        pe.wait_ge(hidden_sb, done(g))
                        pe.wait_ge(message_sb, done(g - 2))
                        for s in range(SUB):
                            last = nc.tensor.matmul(ps_m[k % 2][:, s * D:(s + 1) * D], hid[0:H + 1, k % 2, s * 128:(s + 1) * 128],
                                                    w_m2[:, :], start=True, stop=True)
                        last.then_inc(message, 1)

                    def sums(i, k):
                        g = i * 4 + k
                        pe.wait_ge(message_sb, done(g))
                        pe.wait_ge(added, done(g - 2))
                        for s in range(SUB):
                            last = nc.tensor.matmul(ps_s[k % 2][0:D + 1, 0:W], msg[:, k % 2, s, :], comb[:, k, s, DE:DE + W],
                                                    start=s == 0, stop=s == SUB - 1)
                        last.then_inc(summed, 1)

                    for n in range(3):
                        turn(0, n)
                        if n >= 1:
                            hide(0, n - 1)
                        if n >= 2:
                            messages(0, n - 2)

                    def step(i, k):
                        g = i * 4 + k
                        loop = not isinstance(i, int)
                        sums(i, k)
                        if loop or g + 1 < NG:
                            messages(i, k + 1)
                        if loop or g + 2 < NG:
                            hide(i, k + 2)
                        if loop or g + 3 < NG:
                            turn(i, k + 3)
                    rounds(pe, step, NG, 4)

                by_flag(pe, general, windows)

            @block.scalar
            def _(act):
                act.wait_ge(cleared, 1)
                def general():
                    def step(g):
                        act.wait_ge(gen_turned, g + 1)
                        nc.scalar.copy(comb_t[0:DE, 0, :], ps_t[0][0:DE, :]).then_inc(gen_turned_sb, 1)
                        act.wait_ge(gen_hidden, g + 1)
                        nc.scalar.activation(hid[0:H, 0, :], ps_h[0][0:H, :], ACT.Gelu, bias=b_m1[:, :]).then_inc(gen_hidden_sb, 1)
                        act.wait_ge(gen_product, g + 1)
                        nc.scalar.activation(msg[:, 0, :, 1:1 + D], ps_m[0][:, 0:SUB * D].rearrange("p (s f) -> p s f", s=SUB),
                                             ACT.Gelu).then_inc(gen.message, 1)
                    gen.each_group(act, step)

                def windows():
                    for s_ in (turned_sb, hidden_sb, message_sb):
                        act.sem_inc(s_, CR)

                    def copy_turned(i, k):
                        g = i * 4 + k
                        act.wait_ge(turned, done(g))
                        act.wait_ge(hidden, done(g - 2))
                        nc.scalar.copy(comb_t[:, k % 2, :], ps_t[k % 2][0:DE + W, :]).then_inc(turned_sb, 1)

                    def gelu_hidden(i, k):
                        g = i * 4 + k
                        act.wait_ge(hidden, done(g))
                        act.wait_ge(message, done(g - 2))
                        nc.scalar.activation(hid[0:H, k % 2, :], ps_h[k % 2][0:H, :], ACT.Gelu, bias=b_m1[:, :]).then_inc(hidden_sb, 1)

                    def gelu_message(i, k):
                        g = i * 4 + k
                        act.wait_ge(message, done(g))
                        act.wait_ge(summed, done(g - 2))
                        nc.scalar.activation(msg[:, k % 2, :, 1:1 + D], ps_m[k % 2][:, 0:SUB * D].rearrange("p (s f) -> p s f", s=SUB),
                                             ACT.Gelu).then_inc(message_sb, 1)

                    for n in range(3):
                        copy_turned(0, n)
                        if n >= 1:
                            gelu_hidden(0, n - 1)
                        if n >= 2:
                            gelu_message(0, n - 2)

                    def step(i, k):
                        g = i * 4 + k
                        loop = not isinstance(i, int)
                        if loop or g + 1 < NG:
                            gelu_message(i, k + 1)
                        if loop or g + 2 < NG:
                            gelu_hidden(i, k + 2)
                        if loop or g + 3 < NG:
                            copy_turned(i, k + 3)
                    rounds(act, step, NG, 4)

                by_flag(act, general, windows)

        def layer_norm(dve, act_done, act_turn, link, z, mid, sums, squares):
            link(nc.vector.tensor_reduce(sums, z, AX.X, ALU.add))
            link(nc.vector.tensor_scalar(sums, sums, 1.0 / D, None, ALU.mult))
            link(nc.vector.tensor_tensor(z, z, bc_last(sums, D), ALU.subtract))
            link(nc.vector.tensor_tensor(mid, z, z, ALU.mult))
            link(nc.vector.tensor_reduce(squares, mid, AX.X, ALU.add))
            nc.vector.tensor_scalar(squares, squares, 1.0 / D, EPS, ALU.mult, ALU.add).then_inc(act_turn, 1)
            dve.wait_ge(act_done, 1)
            link(nc.vector.reciprocal(squares, squares))
            link(nc.vector.tensor_tensor(z, z, bc_last(squares, D), ALU.mult))

        def flat(ap):
            return ap.rearrange("p t j f -> p (t j) f")

        def block_of(ap, t):
            return ap[:, bass.ds(t, 1)].rearrange("p a j f -> p (a j) f")

        def per_node(ap, t):
            return ap[:, bass.ds(t, 1)].rearrange("p a j -> p (a j)")

        def strided(ap):
            return ap.rearrange("r (p j) -> r j p", j=SUB)

        def halves(ap):
            return ap.rearrange("r (j p) -> r j p", j=SUB)

        with ExitStack() as c:
            sem, own = stage_semaphores(c, "n0_")
            staged, turned, turned_sb, hidden, hidden_sb, product, product_sb, summed = (
                sem(n) for n in ("staged", "turned", "turned_sb", "hidden", "hidden_sb", "product", "product_sb", "summed"))
            pe_turn, ones_set, chain, root_in, root_out, s_cnt = sem("pe_turn"), sem("ones_set"), sem("chain"), sem("root_in"), sem("root_out"), sem("cnt")
            xs = sb("n0_xs", [128, 2, SUB, D], ctx=c)
            xts = sb("n0_xts", [D, 2, GE], ctx=c)
            hid = sb("n0_hid", [HC + 1, 2, GE], ctx=c)
            comb = sb("n0_comb", [128, 2, SUB, D], ctx=c)
            sums, squares = sb("n0_sums", [128, NT * SUB], ctx=c), sb("n0_squares", [128, NT * SUB], ctx=c)
            mid = sb("n0_mid", [128, NT * SUB, D], ctx=c)
            ps_t = [c.enter_context(nc.psum_tensor(f"n0_t{k}", [128, 512], fp32)) for k in range(2)]
            ps_h = [c.enter_context(nc.psum_tensor(f"n0_h{k}", [128, 512], fp32)) for k in range(2)]
            ps_p = [c.enter_context(nc.psum_tensor(f"n0_p{k}", [128, 512], fp32)) for k in range(2)]
            block = c.enter_context(stage_block(own))

            @block.sync
            def _(sp):
                sp.dma_start(cnt_dram.unsqueeze(0), acc[0:1, :]).then_inc(s_cnt, 16)
                sp.wait_ge(s_cnt, 16)
                sp.dma_start(cnt_nm[:, :, :], cnt_dram.rearrange("(t p j) -> p t j", p=LANES, j=SUB)).then_inc(s_cnt, 16)
                sp.wait_ge(s_cnt, 32)

            @block.tensor
            def _(pe):
                for s_ in (turned, hidden, product):
                    pe.sem_inc(s_, CR)
                pe.wait_ge(ones_set, 1)

                def step(i, k):
                    t = i * 2 + k
                    pe.wait_ge(staged, done(t))
                    pe.wait_ge(turned_sb, done(t - 2))
                    pe.sem_inc(pe_turn, 1)
                    for j in range(SUB):
                        last = nc.tensor.transpose(ps_t[k][0:D, j * 128:(j + 1) * 128], xs[:, k, j, :], ident[:, :])
                    last.then_inc(turned, 1)
                    pe.wait_ge(hidden_sb, done(t - 2))
                    nc.tensor.matmul(ps_h[k][0:HC, :], w_c1a[:, :], strided(acc[:, bass.ds(t * GE, GE)]), start=True, stop=False)
                    pe.wait_ge(turned_sb, done(t))
                    nc.tensor.matmul(ps_h[k][0:HC, :], w_c1x[:, :], xts[:, k, :], start=False, stop=True).then_inc(hidden, 1)
                    pe.wait_ge(hidden_sb, done(t))
                    pe.wait_ge(product_sb, done(t - 2))
                    for j in range(SUB):
                        last = nc.tensor.matmul(ps_p[k][:, j * D:(j + 1) * D], hid[:, k, j * 128:(j + 1) * 128], w_c2[:, :], start=True, stop=True)
                    last.then_inc(product, 1)
                rounds(pe, step, NT, 2)

            @block.scalar
            def _(act):
                for s_ in (turned_sb, hidden_sb, product_sb):
                    act.sem_inc(s_, CR)

                def step(i, k):
                    t = i * 2 + k
                    act.wait_ge(turned, done(t))
                    act.wait_ge(hidden, done(t - 2))
                    nc.scalar.copy(xts[:, k, :], ps_t[k][0:D, :]).then_inc(turned_sb, 1)
                    act.wait_ge(hidden, done(t))
                    act.wait_ge(product, done(t - 2))
                    nc.scalar.activation(hid[0:HC, k, :], ps_h[k][0:HC, :], ACT.Gelu, bias=b_c1[:, :]).then_inc(hidden_sb, 1)
                    act.wait_ge(product, done(t))
                    act.wait_ge(summed, done(t - 2))
                    nc.scalar.activation(comb[:, k].rearrange("p j f -> p (j f)"), ps_p[k][:, 0:SUB * D], ACT.Gelu).then_inc(product_sb, 1)
                rounds(act, step, NT, 2)
                act.wait_ge(root_in, 1)
                nc.scalar.activation(squares[:, :], squares[:, :], ACT.Sqrt).then_inc(root_out, 1)
                act.wait_ge(root_in, 2)
                nc.scalar.activation(dinv_nm[:, :, :], dinv_nm[:, :, :], ACT.Sqrt).then_inc(root_out, 1)

            @block.vector
            def _(dve):
                link = linker(dve, chain)
                nc.vector.memset(hid[HC:HC + 1, :, :], 1.0).then_inc(ones_set, 1)
                dve.sem_inc(staged, CR)
                dve.sem_inc(summed, CR)

                def step(i, k):
                    t = i * 2 + k
                    dve.wait_ge(turned, done(t - 2))
                    nc.vector.tensor_copy(xs[:, k], block_of(x_nm, t)).then_inc(staged, 1)
                    dve.wait_ge(product_sb, done(t))
                    nc.vector.scalar_tensor_tensor(out=block_of(z_nm, t), in0=block_of(x_nm, t), scalar=2.0, in1=comb[:, k],
                                                   op0=ALU.mult, op1=ALU.add).then_inc(summed, 1)
                rounds(dve, step, NT, 2)
                dve.wait_ge(summed, done(NT - 1))
                layer_norm(dve, root_out, root_in, link, flat(z_nm), mid[:, :, :], sums[:, :], squares[:, :])
                dve.wait_ge(s_cnt, 32)
                nc.vector.tensor_scalar(dinv_nm[:, :, :], cnt_nm[:, :, :], 1.0, None, ALU.add).then_inc(root_in, 1)
                dve.wait_ge(root_out, 2)
                link(nc.vector.reciprocal(dinv_nm[:, :, :], dinv_nm[:, :, :]))


        dinv_ctx = ExitStack()
        whole.enter_context(dinv_ctx)
        dinv_bc = sb("dinv_bc", [128, NP], ctx=dinv_ctx)
        with ExitStack() as c:
            sem, own = stage_semaphores(c, "g1_")
            made, turned, in_acc, stored, pe_turn = (sem(n) for n in ("made", "turned", "in_acc", "stored", "pe_turn"))
            s_store = [sem(f"store{k}") for k in range(2)]
            s_cnt, deg_ready, root = sem("cnt"), sem("deg_ready"), sem("root")
            ys = sb("g1_ys", [128, 2, SUB, D], ctx=c)
            ps_y = [c.enter_context(nc.psum_tensor(f"g1_y{k}", [128, 512], fp32)) for k in range(2)]
            block = c.enter_context(stage_block(own))

            @block.sync
            def _(sp):
                sp.sem_inc(stored, CR)
                sp.dma_start(dinv_bc[:, :], cnt_dram.unsqueeze(0).to_broadcast([128, NP])).then_inc(s_cnt, 16)

                def step(i, k):
                    t = sp.snap(i * 2 + k) if not isinstance(i, int) else i * 2 + k
                    sp.wait_ge(made, done(t))
                    sp.dma_start(group_rows(tab_y1, t), ys[:, k].rearrange("p j f -> p (j f)")).then_inc(s_store[k], 16)
                    sp.wait_ge(s_store[k], (i + 1) * 16)
                    sp.sem_inc(stored, 1)
                rounds(sp, step, NT, 2)

            @block.vector
            def _(dve):
                dve.sem_inc(made, CR)

                def step(i, k):
                    t = i * 2 + k
                    dve.wait_ge(turned, done(t - 2))
                    dve.wait_ge(stored, done(t - 2))
                    nc.vector.tensor_tensor(ys[:, k], block_of(z_nm, t), bc_last(per_node(dinv_nm, t), D), ALU.mult).then_inc(made, 1)
                rounds(dve, step, NT, 2)
                dve.wait_ge(s_cnt, 16)
                nc.vector.tensor_scalar(dinv_bc[:, :], dinv_bc[:, :], 1.0, None, ALU.add).then_inc(deg_ready, 1)
                dve.wait_ge(root, 1)
                nc.vector.reciprocal(dinv_bc[:, :], dinv_bc[:, :])

            @block.tensor
            def _(pe):
                pe.sem_inc(turned, CR)

                def step(i, k):
                    t = i * 2 + k
                    pe.wait_ge(made, done(t))
                    pe.wait_ge(in_acc, done(t - 2))
                    pe.sem_inc(pe_turn, 1)
                    for j in range(SUB):
                        last = nc.tensor.transpose(ps_y[k][0:D, j * 128:(j + 1) * 128], ys[:, k, j, :], ident[:, :])
                    last.then_inc(turned, 1)
                rounds(pe, step, NT, 2)

            @block.scalar
            def _(act):
                act.sem_inc(in_acc, CR)

                def step(i, k):
                    t = i * 2 + k
                    act.wait_ge(turned, done(t))
                    nc.scalar.copy(strided(acc[0:D, bass.ds(t * GE, GE)]), halves(ps_y[k][0:D, :])).then_inc(in_acc, 1)
                rounds(act, step, NT, 2)
                act.wait_ge(deg_ready, 1)
                nc.scalar.activation(dinv_bc[:, :], dinv_bc[:, :], ACT.Sqrt).then_inc(root, 1)

        def gcn_sums(name, tab):
            with ExitStack() as c:
                sem, own = stage_semaphores(c, f"{name}_")
                s_idx = [sem(f"idx{k}") for k in range(4)]
                s_rows = [gather_sem(f"{name}_rows{k}") for k in range(4)]
                pool_turn, hot, summed, added = (sem(n) for n in ("pool_turn", "hot", "summed", "added"))
                idx = sb(f"{name}_idx", [128, 4, SUB], i32, c)
                rows = sb(f"{name}_rows", [128, 4, SUB, D], ctx=c)
                onehot = sb(f"{name}_onehot", [128, 4, SUB, W], ctx=c)
                ps_s = [c.enter_context(nc.psum_tensor(f"{name}_s{k}", [128, 512], fp32)) for k in range(2)]
                gen = general_path(c, sem, name, D, dst_pad, [(tab, src_pad, rows[:, 0])], rows[:, 0], ps_s[0])
                block = c.enter_context(stage_block(own))

                @block.sync
                def _(sp):
                    def general():
                        gen.sync(sp)

                    def windows():
                        def step(i, k):
                            g = sp.snap(i * 4 + k) if not isinstance(i, int) else i * 4 + k
                            sp.wait_ge(summed, done(g - 4))
                            sp.dma_start(idx[:, k, :], group_rows(src_pad.unsqueeze(1), g)).then_inc(s_idx[k], 16)
                        rounds(sp, step, NG, 4)

                    by_flag(sp, general, windows)

                @block.gpsimd
                def _(pool):
                    def general():
                        gen.gpsimd(pool)

                    def windows():
                        def step(i, k):
                            pool.wait_ge(s_idx[k], (i + 1) * 16)
                            pool.sem_inc(pool_turn, 1)
                            for s in range(SUB):
                                nc.gpsimd.indirect_dma_start(
                                    out=rows[:, k, s, :], out_offset=None, in_=tab,
                                    in_offset=bass.IndirectOffsetOnAxis(ap=idx[:, k, s:s + 1], axis=0)).then_inc(s_rows[k], 16)
                        rounds(pool, step, NG, 4)

                    by_flag(pool, general, windows)

                @block.vector
                def _(dve):
                    def general():
                        gen.vector(dve)

                    def windows():
                        dve.sem_inc(hot, CR)
                        dve.sem_inc(added, CR)

                        def step(i, k):
                            g = i * 4 + k
                            dve.wait_ge(summed, done(g - 4))
                            nc.vector.tensor_tensor(onehot[:, k], iota_w[:, :, :],
                                                    bc_last(rel[:, bass.ds(g, 1), :].rearrange("p a s -> p (a s)"), W), ALU.is_equal).then_inc(hot, 1)
                            start = dve.value_load(base[0:1, bass.ds(g, 1)], min_val=0, max_val=N)
                            dve.wait_ge(summed, done(g))
                            dve.wait_ge(added, done(g - 1))
                            nc.vector.tensor_tensor(acc[0:D, bass.ds(start, W)], acc[0:D, bass.ds(start, W)], ps_s[k % 2][0:D, 0:W], ALU.add).then_inc(added, 1)
                        rounds(dve, step, NG, 4)

                    by_flag(dve, general, windows)

                @block.tensor
                def _(pe):
                    def general():
                        gen.tensor(pe)

                    def windows():
                        pe.sem_inc(summed, CR)

                        def step(i, k):
                            g = i * 4 + k
                            pe.wait_ge(hot, done(g))
                            pe.wait_ge(added, done(g - 2))
                            pe.wait_ge(s_rows[k], (i + 1) * 64)
                            for s in range(SUB):
                                last = nc.tensor.matmul(ps_s[k % 2][0:D, 0:W], rows[:, k, s, :], onehot[:, k, s, :], start=s == 0, stop=s == SUB - 1)
                            last.then_inc(summed, 1)
                        rounds(pe, step, NG, 4)

                    by_flag(pe, general, windows)

        gcn_sums("gs1", tab_y1)

        with ExitStack() as c:
            sem, own = stage_semaphores(c, "g2_")
            wide, scaled, hidden, product, made, turned, in_acc, stored, pe_turn = (
                sem(n) for n in ("wide", "scaled", "hidden", "product", "made", "turned", "in_acc", "stored", "pe_turn"))
            s_store = [sem(f"store{k}") for k in range(2)]
            us = sb("g2_us", [H1, 2, GE], ctx=c)
            hid = sb("g2_hid", [H1, 2, GE], ctx=c)
            ys = sb("g2_ys", [128, 2, SUB, D], ctx=c)
            ps_u = [c.enter_context(nc.psum_tensor(f"g2_u{k}", [128, 512], fp32)) for k in range(2)]
            ps_p = [c.enter_context(nc.psum_tensor(f"g2_p{k}", [128, 512], fp32)) for k in range(2)]
            ps_y = [c.enter_context(nc.psum_tensor(f"g2_y{k}", [128, 512], fp32)) for k in range(2)]
            block = c.enter_context(stage_block(own))

            @block.tensor
            def _(pe):
                for s_ in (wide, product, turned):
                    pe.sem_inc(s_, CR)

                def step(i, k):
                    t = i * 2 + k
                    pe.wait_ge(scaled, done(t - 2))
                    nc.tensor.matmul(ps_u[k][0:H1, :], w_g1[:, :], acc[0:D, bass.ds(t * GE, GE)], start=True, stop=True).then_inc(wide, 1)
                    pe.wait_ge(hidden, done(t))
                    pe.wait_ge(made, done(t - 2))
                    for j in range(SUB):
                        last = nc.tensor.matmul(ps_p[k][:, j * D:(j + 1) * D], strided(hid[:, k, :])[:, j, :], w_g2[:, :], start=True, stop=True)
                    last.then_inc(product, 1)
                    pe.wait_ge(made, done(t))
                    pe.wait_ge(in_acc, done(t - 2))
                    pe.sem_inc(pe_turn, 1)
                    for j in range(SUB):
                        last = nc.tensor.transpose(ps_y[k][0:D, j * 128:(j + 1) * 128], ys[:, k, j, :], ident[:, :])
                    last.then_inc(turned, 1)
                rounds(pe, step, NT, 2)

            @block.vector
            def _(dve):
                dve.sem_inc(scaled, CR)
                dve.sem_inc(made, CR)

                def step(i, k):
                    t = i * 2 + k
                    dve.wait_ge(wide, done(t))
                    dve.wait_ge(hidden, done(t - 2))
                    nc.vector.tensor_tensor(us[:, k, :], ps_u[k][0:H1, :], dinv_bc[0:H1, bass.ds(t * GE, GE)], ALU.mult).then_inc(scaled, 1)
                    dve.wait_ge(product, done(t))
                    dve.wait_ge(turned, done(t - 2))
                    dve.wait_ge(stored, done(t - 2))
                    nc.vector.tensor_tensor(ys[:, k], ps_p[k][:, 0:SUB * D].rearrange("p (j f) -> p j f", j=SUB),
                                            bc_last(per_node(dinv_nm, t), D), ALU.mult).then_inc(made, 1)
                rounds(dve, step, NT, 2)

            @block.scalar
            def _(act):
                act.sem_inc(hidden, CR)
                act.sem_inc(in_acc, CR)

                def step(i, k):
                    t = i * 2 + k
                    act.wait_ge(scaled, done(t))
                    act.wait_ge(product, done(t - 2))
                    nc.scalar.activation(hid[:, k, :], us[:, k, :], ACT.Relu, bias=b_g1[:, :]).then_inc(hidden, 1)
                    act.wait_ge(turned, done(t))
                    nc.scalar.copy(strided(acc[0:D, bass.ds(t * GE, GE)]), halves(ps_y[k][0:D, :])).then_inc(in_acc, 1)
                rounds(act, step, NT, 2)

            @block.sync
            def _(sp):
                sp.sem_inc(stored, CR)

                def step(i, k):
                    t = sp.snap(i * 2 + k) if not isinstance(i, int) else i * 2 + k
                    sp.wait_ge(made, done(t))
                    sp.dma_start(group_rows(tab_y2, t), ys[:, k].rearrange("p j f -> p (j f)")).then_inc(s_store[k], 16)
                    sp.wait_ge(s_store[k], (i + 1) * 16)
                    sp.sem_inc(stored, 1)
                rounds(sp, step, NT, 2)

        gcn_sums("gs2", tab_y2)

        with ExitStack() as c:
            sem, own = stage_semaphores(c, "g3_")
            scaled, turned, summed, pe_turn, chain, root_in, root_out = (
                sem(n) for n in ("scaled", "turned", "summed", "pe_turn", "chain", "root_in", "root_out"))
            us = sb("g3_us", [D, 2, GE], ctx=c)
            sums, squares = sb("g3_sums", [128, NT * SUB], ctx=c), sb("g3_squares", [128, NT * SUB], ctx=c)
            mid = sb("g3_mid", [128, NT * SUB, D], ctx=c)
            ps_z = [c.enter_context(nc.psum_tensor(f"g3_z{k}", [128, 512], fp32)) for k in range(2)]
            block = c.enter_context(stage_block(own))

            @block.vector
            def _(dve):
                link = linker(dve, chain)
                dve.sem_inc(scaled, CR)
                dve.sem_inc(summed, CR)

                def step(i, k):
                    t = i * 2 + k
                    dve.wait_ge(turned, done(t - 2))
                    nc.vector.tensor_tensor(us[:, k, :], acc[0:D, bass.ds(t * GE, GE)], dinv_bc[0:D, bass.ds(t * GE, GE)], ALU.mult).then_inc(scaled, 1)
                    dve.wait_ge(turned, done(t))
                    nc.vector.tensor_tensor(block_of(x_nm, t), ps_z[k][:, 0:SUB * D].rearrange("p (j f) -> p j f", j=SUB), block_of(z_nm, t), ALU.add).then_inc(summed, 1)
                rounds(dve, step, NT, 2)
                dve.wait_ge(summed, done(NT - 1))
                link(nc.vector.tensor_tensor(flat(x_nm), flat(x_nm), b_g2[:, :].unsqueeze(1).to_broadcast([128, NT * SUB, D]), ALU.add))
                layer_norm(dve, root_out, root_in, link, flat(x_nm), mid[:, :, :], sums[:, :], squares[:, :])

            @block.tensor
            def _(pe):
                pe.sem_inc(turned, CR)

                def step(i, k):
                    t = i * 2 + k
                    pe.wait_ge(scaled, done(t))
                    pe.wait_ge(summed, done(t - 2))
                    pe.sem_inc(pe_turn, 1)
                    for j in range(SUB):
                        last = nc.tensor.transpose(ps_z[k][:, j * D:(j + 1) * D], strided(us[:, k, :])[:, j, :], ident[0:D, 0:D])
                    last.then_inc(turned, 1)
                rounds(pe, step, NT, 2)

            @block.scalar
            def _(act):
                act.wait_ge(root_in, 1)
                nc.scalar.activation(squares[:, :], squares[:, :], ACT.Sqrt).then_inc(root_out, 1)
        dinv_ctx.close()

        x_t = sb("x_t", [D, NP])
        with ExitStack() as c:
            sem, own = stage_semaphores(c, "e0_")
            staged, turned, turned_sb, product, made, stored, pe_turn = (
                sem(n) for n in ("staged", "turned", "turned_sb", "product", "made", "stored", "pe_turn"))
            s_store = [sem(f"store{k}") for k in range(2)]
            xs = sb("e0_xs", [128, 2, SUB, D], ctx=c)
            xts = sb("e0_xts", [D, 2, GE], ctx=c)
            ys = sb("e0_ys", [128, 2, SUB, D], ctx=c)
            ps_t = [c.enter_context(nc.psum_tensor(f"e0_t{k}", [128, 512], fp32)) for k in range(2)]
            ps_p = [c.enter_context(nc.psum_tensor(f"e0_p{k}", [128, 512], fp32)) for k in range(2)]
            block = c.enter_context(stage_block(own))

            @block.vector
            def _(dve):
                dve.sem_inc(staged, CR)
                dve.sem_inc(made, CR)
                nc.vector.memset(acc[:, :], 0.0)

                def step(i, k):
                    t = i * 2 + k
                    dve.wait_ge(turned, done(t - 2))
                    nc.vector.tensor_copy(xs[:, k], block_of(x_nm, t)).then_inc(staged, 1)
                    dve.wait_ge(product, done(t))
                    dve.wait_ge(stored, done(t - 2))
                    nc.vector.tensor_copy(ys[:, k].rearrange("p j f -> p (j f)"), ps_p[k][:, 0:SUB * D]).then_inc(made, 1)
                rounds(dve, step, NT, 2)

            @block.tensor
            def _(pe):
                pe.sem_inc(turned, CR)
                pe.sem_inc(product, CR)

                def step(i, k):
                    t = i * 2 + k
                    pe.wait_ge(staged, done(t))
                    pe.wait_ge(turned_sb, done(t - 2))
                    pe.sem_inc(pe_turn, 1)
                    for j in range(SUB):
                        last = nc.tensor.transpose(ps_t[k][0:D, j * 128:(j + 1) * 128], xs[:, k, j, :], ident[:, :])
                    last.then_inc(turned, 1)
                    pe.wait_ge(turned_sb, done(t))
                    pe.wait_ge(made, done(t - 2))
                    for j in range(SUB):
                        last = nc.tensor.matmul(ps_p[k][:, j * D:(j + 1) * D], xts[:, k, j * 128:(j + 1) * 128], w_e1x[:, :], start=True, stop=True)
                    last.then_inc(product, 1)
                rounds(pe, step, NT, 2)

            @block.scalar
            def _(act):
                act.sem_inc(turned_sb, CR)

                def step(i, k):
                    t = i * 2 + k
                    act.wait_ge(turned, done(t))
                    act.wait_ge(product, done(t - 2))
                    nc.scalar.copy(strided(x_t[:, bass.ds(t * GE, GE)]), halves(ps_t[k][0:D, :]))
                    nc.scalar.copy(xts[:, k, :], ps_t[k][0:D, :]).then_inc(turned_sb, 1)
                rounds(act, step, NT, 2)

            @block.sync
            def _(sp):
                sp.sem_inc(stored, CR)

                def step(i, k):
                    t = sp.snap(i * 2 + k) if not isinstance(i, int) else i * 2 + k
                    sp.wait_ge(made, done(t))
                    sp.dma_start(group_rows(tab_t2, t), ys[:, k].rearrange("p j f -> p (j f)")).then_inc(s_store[k], 16)
                    sp.wait_ge(s_store[k], (i + 1) * 16)
                    sp.sem_inc(stored, 1)
                rounds(sp, step, NT, 2)

        with ExitStack() as c:
            sem, own = stage_semaphores(c, "e1_")
            s_idx = [sem(f"idx{k}") for k in range(4)]
            s_att = [sem(f"att{k}") for k in range(4)]
            s_rows = [gather_sem(f"e1_rows{k}") for k in range(4)]
            s_out = [sem(f"out{k}") for k in range(4)]
            turned, turned_sb, product, made, squared, counted, pool_turn, pe_turn, written, cleared, adds, squares_added = (
                sem(n) for n in ("turned", "turned_sb", "product", "made", "squared", "counted", "pool_turn", "pe_turn", "written", "cleared", "adds", "squares_added"))
            chain, moments, root_in, root_out = sem("chain"), sem("moments"), sem("root_in"), sem("root_out")
            idx = sb("e1_idx_t", [128, 4, SUB], i32, c)
            att = sb("e1_att_t", [128, 4, SUB, D], ctx=c)
            att_end = sb("e1_att_end", [128, SUB, D], ctx=c)
            rows = sb("e1_rows_t", [128, 4, SUB, D], ctx=c)
            att_t = sb("e1_att_tt", [D, 2, GE], ctx=c)
            h = sb("e1_h", [128, 4, SUB * D], ctx=c)
            sq = sb("e1_sq", [128, 2, SUB * D], ctx=c)
            sum_h, sum_q = sb("e1_sum_h", [128, SUB * D], ctx=c), sb("e1_sum_q", [128, SUB * D], ctx=c)
            mean, var = sb("e1_mean", [128, D], ctx=c), sb("e1_var", [128, D], ctx=c)
            tmp = sb("e1_tmp", [128, D], ctx=c)
            ps_t = [c.enter_context(nc.psum_tensor(f"e1_t{k}", [128, 512], fp32)) for k in range(2)]
            ps_p = [c.enter_context(nc.psum_tensor(f"e1_p{k}", [128, 512], fp32)) for k in range(2)]
            ps_q = c.enter_context(nc.psum_tensor("e1_q", [128, 512], fp32))
            block = c.enter_context(stage_block(own))
            att_dram = P["edge_attr_64"]

            def att_of(i, k):
                return att_end[:, :, :] if isinstance(i, int) and i * 4 + k == NG - 1 else att[:, k % 4]

            @block.sync
            def _(sp):
                sp.sem_inc(written, CR)

                def load(i, k):
                    i, k = i + k // 4, k % 4
                    g = sp.snap(i * 4 + k) if not isinstance(i, int) else i * 4 + k
                    sp.wait_ge(made, done(g - 4))
                    sp.dma_start(idx[:, k, :], group_rows(src_pad.unsqueeze(1), g)).then_inc(s_idx[k], 16)
                    if isinstance(i, int) and g == NG - 1:
                        sp.wait_ge(cleared, 1)
                        sp.dma_start(att_end[0:TROWS], att_dram[(NG - 1) * GE:E - TLEFT, :].rearrange("(p s) f -> p s f", s=SUB)).then_inc(s_att[k], 16)
                        sp.dma_start(att_end[TROWS:TROWS + 1, 0:TLEFT], att_dram[E - TLEFT:E, :].unsqueeze(0)).then_inc(s_att[k], 16)
                    else:
                        sp.dma_start(att[:, k].rearrange("p s f -> p (s f)"), group_rows(att_dram, g)).then_inc(s_att[k], 16)

                for k in range(2):
                    load(0, k)

                def step(i, k):
                    g = sp.snap(i * 4 + k) if not isinstance(i, int) else i * 4 + k
                    if not isinstance(i, int) or g + 2 < NG:
                        load(i, k + 2)
                    sp.wait_ge(made, done(g))
                    sp.dma_start(group_rows(h_edges, g), h[:, k, :]).then_inc(s_out[k], 16)
                rounds(sp, step, NG, 4)
                for k in range(4):
                    sp.wait_ge(s_out[k], (NG + 3 - k) // 4 * 16)

            @block.gpsimd
            def _(pool):
                pool.memset(att_end[:, :, :], 0.0).then_inc(cleared, 1)

                def step(i, k):
                    pool.wait_ge(s_idx[k], (i + 1) * 16)
                    pool.sem_inc(pool_turn, 1)
                    for s in range(SUB):
                        nc.gpsimd.indirect_dma_start(
                            out=rows[:, k, s, :], out_offset=None, in_=tab_t2,
                            in_offset=bass.IndirectOffsetOnAxis(ap=idx[:, k, s:s + 1], axis=0)).then_inc(s_rows[k], 16)
                rounds(pool, step, NG, 4)

            @block.tensor
            def _(pe):
                pe.sem_inc(turned, CR)
                pe.sem_inc(product, CR)

                def turn(i, k):
                    i, k = i + k // 4, k % 4
                    g = i * 4 + k
                    last_group = isinstance(i, int) and g == NG - 1
                    pe.wait_ge(s_att[k], (i + 1 + last_group) * 16)
                    pe.wait_ge(turned_sb, done(g - 2))
                    pe.sem_inc(pe_turn, 1)
                    for s in range(SUB):
                        last = nc.tensor.transpose(ps_t[k % 2][0:D, s * 128:(s + 1) * 128], att_of(i, k)[:, s, :], ident[:, :])
                    last.then_inc(turned, 1)
                turn(0, 0)

                def step(i, k):
                    g = i * 4 + k
                    if not isinstance(i, int) or g + 1 < NG:
                        turn(i, k + 1)
                    pe.wait_ge(turned_sb, done(g))
                    pe.wait_ge(made, done(g - 2))
                    for s in range(SUB):
                        last = nc.tensor.matmul(ps_p[k % 2][:, s * D:(s + 1) * D], att_t[:, k % 2, s * 128:(s + 1) * 128], w_e1e[:, :], start=True, stop=True)
                    last.then_inc(product, 1)
                rounds(pe, step, NG, 4)
                pe.wait_ge(adds, done(NG - 1))
                pe.wait_ge(squares_added, done(NG - 1))
                nc.tensor.matmul(ps_q[:, 0:SUB * D], ones_sq[:, :], sum_h[:, :], start=True, stop=True)
                nc.tensor.matmul(ps_q[:, SUB * D:2 * SUB * D], ones_sq[:, :], sum_q[:, :], start=True, stop=True).then_inc(moments, 1)

            @block.scalar
            def _(act):
                act.sem_inc(turned_sb, CR)
                act.sem_inc(squared, CR)

                def copy_turned(i, k):
                    i, k = i + k // 4, k % 4
                    g = i * 4 + k
                    act.wait_ge(turned, done(g))
                    act.wait_ge(product, done(g - 2))
                    nc.scalar.copy(att_t[:, k % 2, :], ps_t[k % 2][0:D, :]).then_inc(turned_sb, 1)
                copy_turned(0, 0)

                def step(i, k):
                    g = i * 4 + k
                    if not isinstance(i, int) or g + 1 < NG:
                        copy_turned(i, k + 1)
                    act.wait_ge(made, done(g))
                    act.wait_ge(squares_added, done(g - 2))
                    nc.scalar.activation(sq[:, k % 2, :], h[:, k, :], ACT.Square).then_inc(squared, 1)
                rounds(act, step, NG, 4)
                act.wait_ge(root_in, 1)
                nc.scalar.activation(var[:, :], var[:, :], ACT.Sqrt).then_inc(root_out, 1)

            @block.vector
            def _(dve):
                link = linker(dve, chain)
                link(nc.vector.memset(sum_h[:, :], 0.0))
                link(nc.vector.memset(sum_q[:, :], 0.0))
                for s_ in (made, adds, squares_added):
                    dve.sem_inc(s_, CR)

                def step(i, k, previous=True):
                    g = i * 4 + k
                    dve.wait_ge(product, done(g))
                    dve.wait_ge(squared, done(g - 4))
                    if not isinstance(i, int) or i > 0:
                        dve.wait_ge(s_out[k], i * 16)
                    dve.wait_ge(s_rows[k], (i + 1) * 64)
                    nc.vector.tensor_tensor(h[:, k, :], ps_p[k % 2][:, 0:SUB * D], rows[:, k].rearrange("p s f -> p (s f)"), ALU.add).then_inc(made, 1)
                    if previous:
                        dve.wait_ge(squared, done(g - 1))
                        dve.wait_ge(squares_added, done(g - 2))
                        nc.vector.tensor_tensor(sum_q[:, :], sum_q[:, :], sq[:, (k + 1) % 2, :], ALU.add).then_inc(squares_added, 1)
                    dve.wait_ge(made, done(g))
                    dve.wait_ge(adds, done(g - 1))
                    nc.vector.tensor_tensor(sum_h[:, :], sum_h[:, :], h[:, k, :], ALU.add).then_inc(adds, 1)
                for k in range(4):
                    step(0, k, k > 0)
                with dve.Fori(1, NG // 4) as i:
                    for k in range(4):
                        step(i, k)
                for k in range(NG % 4):
                    step(NG // 4, k)
                dve.wait_ge(squared, done(NG - 1))
                dve.wait_ge(squares_added, done(NG - 2))
                nc.vector.tensor_tensor(sum_q[:, :], sum_q[:, :], sq[:, (NG - 1) % 2, :], ALU.add).then_inc(squares_added, 1)
                dve.wait_ge(moments, 1)
                by_sub = lambda o: ps_q[:, o:o + SUB * D].rearrange("p (s f) -> p f s", s=SUB)
                link(nc.vector.tensor_reduce(mean[:, :], by_sub(0), AX.X, ALU.add))
                link(nc.vector.tensor_reduce(var[:, :], by_sub(SUB * D), AX.X, ALU.add))
                link(nc.vector.tensor_scalar(mean[:, :], mean[:, :], 1.0 / E, None, ALU.mult))
                link(nc.vector.tensor_tensor(tmp[:, :], mean[:, :], mean[:, :], ALU.mult))
                link(nc.vector.tensor_scalar(var[:, :], var[:, :], 1.0 / E, EPS, ALU.mult, ALU.add))
                nc.vector.tensor_tensor(var[:, :], var[:, :], tmp[:, :], ALU.subtract).then_inc(root_in, 1)
                dve.wait_ge(root_out, 1)
                link(nc.vector.reciprocal(var[:, :], var[:, :]))
                link(nc.vector.tensor_tensor(bn_scale[:, :], var[:, :], row_g1[:, :], ALU.mult))
                link(nc.vector.tensor_tensor(mean[:, :], mean[:, :], row_b1[:, :], ALU.add))
                link(nc.vector.tensor_tensor(mean[:, :], row_b1[:, :], mean[:, :], ALU.subtract))
                link(nc.vector.tensor_tensor(mean[:, :], mean[:, :], bn_scale[:, :], ALU.mult))
                nc.vector.tensor_tensor(bn_shift[:, :], mean[:, :], row_be1[:, :], ALU.add)

        with ExitStack() as c:
            sem, own = stage_semaphores(c, "e2_")
            s_h = [sem(f"h{k}") for k in range(4)]
            scaled, shifted, message, hot, summed, added = (sem(n) for n in ("scaled", "shifted", "message", "hot", "summed", "added"))
            h = sb("e2_h", [128, 4, SUB, D], ctx=c)
            hs = sb("e2_hs", [128, 2, SUB, D], ctx=c)
            msg = sb("e2_msg", [128, 2, SUB, D], ctx=c)
            onehot = sb("e2_onehot", [128, 4, SUB, W], ctx=c)
            ps_s = [c.enter_context(nc.psum_tensor(f"e2_s{k}", [128, 512], fp32)) for k in range(2)]
            gen = general_path(c, sem, "e2", D, dst_pad, [], msg[:, 0], ps_s[0])
            gen_h, gen_shifted, gen_scaled = sem("gen_h"), sem("gen_shifted"), sem("gen_scaled")
            block = c.enter_context(stage_block(own))
            scale_bc = bn_scale[:, :].unsqueeze(1).to_broadcast([128, SUB, D])
            shift_bc = bn_shift[:, :].unsqueeze(1).to_broadcast([128, SUB, D])

            @block.sync
            def _(sp):
                def general():
                    gen.sync(sp, lambda g: sp.dma_start(h[:, 0].rearrange("p s f -> p (s f)"), group_rows(h_edges, g)).then_inc(gen_h, 16))

                def windows():
                    def step(i, k):
                        g = sp.snap(i * 4 + k) if not isinstance(i, int) else i * 4 + k
                        sp.wait_ge(scaled, done(g - 4))
                        sp.dma_start(h[:, k].rearrange("p s f -> p (s f)"), group_rows(h_edges, g)).then_inc(s_h[k], 16)
                    rounds(sp, step, NG, 4)

                by_flag(sp, general, windows)

            @block.gpsimd
            def _(pool):
                def general():
                    pool.sem_inc(scaled, 1)

                def windows():
                    pool.sem_inc(scaled, CR)

                    def step(i, k):
                        g = i * 4 + k
                        pool.wait_ge(s_h[k], (i + 1) * 16)
                        pool.wait_ge(message, done(g - 2))
                        nc.gpsimd.tensor_tensor(hs[:, k % 2], h[:, k], scale_bc, ALU.mult).then_inc(scaled, 1)
                    rounds(pool, step, NG, 4)

                by_flag(pool, general, windows)

            @block.vector
            def _(dve):
                def general():
                    def make(g):
                        dve.wait_ge(gen_h, (g + 1) * 16)
                        nc.vector.tensor_tensor(hs[:, 0], h[:, 0], scale_bc, ALU.mult).then_inc(gen_scaled, 1)
                        dve.wait_ge(gen_scaled, g + 1)
                        nc.vector.tensor_tensor(hs[:, 0], hs[:, 0], shift_bc, ALU.add).then_inc(gen_shifted, 1)
                    gen.vector(dve, make)

                def windows():
                    for s_ in (hot, shifted, added):
                        dve.sem_inc(s_, CR)

                    def prepare(i, k):
                        i, k = i + k // 4, k % 4
                        g = i * 4 + k
                        dve.wait_ge(summed, done(g - 4))
                        nc.vector.tensor_tensor(onehot[:, k], iota_w[:, :, :],
                                                bc_last(rel[:, bass.ds(g, 1), :].rearrange("p a s -> p (a s)"), W), ALU.is_equal).then_inc(hot, 1)
                        dve.wait_ge(scaled, done(g))
                        nc.vector.tensor_tensor(hs[:, k % 2], hs[:, k % 2], shift_bc, ALU.add).then_inc(shifted, 1)
                    prepare(0, 0)

                    def step(i, k):
                        g = i * 4 + k
                        if not isinstance(i, int) or g + 1 < NG:
                            prepare(i, k + 1)
                        start = dve.value_load(base[0:1, bass.ds(g, 1)], min_val=0, max_val=N)
                        dve.wait_ge(summed, done(g))
                        dve.wait_ge(added, done(g - 1))
                        nc.vector.tensor_tensor(acc[0:D, bass.ds(start, W)], acc[0:D, bass.ds(start, W)], ps_s[k % 2][0:D, 0:W], ALU.add).then_inc(added, 1)
                    rounds(dve, step, NG, 4)

                by_flag(dve, general, windows)

            @block.scalar
            def _(act):
                def general():
                    def step(g):
                        act.wait_ge(gen_shifted, g + 1)
                        nc.scalar.activation(msg[:, 0], hs[:, 0], ACT.Silu).then_inc(gen.message, 1)
                    gen.each_group(act, step)

                def windows():
                    act.sem_inc(message, CR)

                    def step(i, k):
                        g = i * 4 + k
                        act.wait_ge(shifted, done(g))
                        act.wait_ge(summed, done(g - 2))
                        nc.scalar.activation(msg[:, k % 2], hs[:, k % 2], ACT.Silu).then_inc(message, 1)
                    rounds(act, step, NG, 4)

                by_flag(act, general, windows)

            @block.tensor
            def _(pe):
                def general():
                    gen.tensor(pe)

                def windows():
                    pe.sem_inc(summed, CR)

                    def step(i, k):
                        g = i * 4 + k
                        pe.wait_ge(hot, done(g))
                        pe.wait_ge(added, done(g - 2))
                        pe.wait_ge(message, done(g))
                        for s in range(SUB):
                            last = nc.tensor.matmul(ps_s[k % 2][0:D, 0:W], msg[:, k % 2, s, :], onehot[:, k, s, :], start=s == 0, stop=s == SUB - 1)
                        last.then_inc(summed, 1)
                    rounds(pe, step, NG, 4)

                by_flag(pe, general, windows)

        with ExitStack() as c:
            sem, own = stage_semaphores(c, "e3_")
            ready, product, copied, chain, centre, root_in, root_out, silu_out, staged, turned, summed, pe_turn, s_cnt = (
                sem(n) for n in ("ready", "product", "copied", "chain", "centre", "root_in", "root_out", "silu_out", "staged", "turned", "summed", "pe_turn", "s_cnt"))
            s_tab = sem("tab")
            h_t = sb("e3_h_t", [D, NP], ctx=c)
            sq_t = sb("e3_sq_t", [D, NP], ctx=c)
            hs = sb("e3_hs", [D, 2, GE], ctx=c)
            col = sb("e3_col", [D, 6], ctx=c)
            sums, squares = sb("e3_sums", [128, NT * SUB], ctx=c), sb("e3_squares", [128, NT * SUB], ctx=c)
            mid = sb("e3_mid", [128, NT * SUB, D], ctx=c)
            ps_p = [c.enter_context(nc.psum_tensor(f"e3_p{k}", [128, 512], fp32)) for k in range(2)]
            ps_z = [c.enter_context(nc.psum_tensor(f"e3_z{k}", [128, 512], fp32)) for k in range(2)]
            block = c.enter_context(stage_block(own))

            @block.sync
            def _(sp):
                sp.dma_start(sq_t[:, :], cnt_dram.unsqueeze(0).to_broadcast([D, NP])).then_inc(s_cnt, 16)
                sp.wait_ge(root_in, 4)
                sp.dma_start(tab_x3[0:NP, :].rearrange("(t p j) f -> p t (j f)", p=LANES, j=SUB),
                             z_nm[:, :, :, :].rearrange("p t j f -> p t (j f)")).then_inc(s_tab, 16)
                sp.wait_ge(s_tab, 16)

            @block.tensor
            def _(pe):
                pe.sem_inc(product, CR)
                pe.sem_inc(turned, CR)
                pe.wait_ge(ready, 1)

                def multiply(i, k):
                    t = i * 2 + k
                    pe.wait_ge(copied, done(t - 2))
                    nc.tensor.matmul(ps_p[k][:, :], w_n2x[:, :], x_t[:, bass.ds(t * GE, GE)], start=True, stop=False)
                    nc.tensor.matmul(ps_p[k][:, :], w_n2a[:, :], acc[0:D, bass.ds(t * GE, GE)], start=False, stop=True).then_inc(product, 1)
                rounds(pe, multiply, NT, 2)

                def turn(i, k):
                    t = i * 2 + k
                    pe.wait_ge(staged, done(t))
                    pe.wait_ge(summed, done(t - 2))
                    pe.sem_inc(pe_turn, 1)
                    for j in range(SUB):
                        last = nc.tensor.transpose(ps_z[k][:, j * D:(j + 1) * D], strided(hs[:, k, :])[:, j, :], ident[0:D, 0:D])
                    last.then_inc(turned, 1)
                rounds(pe, turn, NT, 2)

            @block.scalar
            def _(act):
                act.sem_inc(copied, CR)
                act.sem_inc(staged, CR)

                def copy_product(i, k):
                    t = i * 2 + k
                    act.wait_ge(product, done(t))
                    nc.scalar.copy(h_t[:, bass.ds(t * GE, GE)], ps_p[k][0:D, :]).then_inc(copied, 1)
                rounds(act, copy_product, NT, 2)
                act.wait_ge(root_in, 1)
                nc.scalar.activation(col[:, 1:2], col[:, 1:2], ACT.Sqrt).then_inc(root_out, 1)
                act.wait_ge(root_in, 2)

                def finish(i, k):
                    t = i * 2 + k
                    act.wait_ge(turned, done(t - 2))
                    nc.scalar.activation(hs[:, k, :], h_t[:, bass.ds(t * GE, GE)], ACT.Silu, bias=col[:, 3:4], scale=col[:, 2:3]).then_inc(staged, 1)
                rounds(act, finish, NT, 2)
                act.wait_ge(root_in, 3)
                nc.scalar.activation(squares[:, :], squares[:, :], ACT.Sqrt).then_inc(root_out, 1)

            @block.vector
            def _(dve):
                link = linker(dve, chain)
                dve.sem_inc(summed, CR)
                dve.wait_ge(s_cnt, 16)
                link(nc.vector.tensor_scalar(sq_t[:, :], sq_t[:, :], 1.0, None, ALU.max))
                link(nc.vector.reciprocal(sq_t[:, :], sq_t[:, :]))
                nc.vector.tensor_tensor(acc[0:D, :], acc[0:D, :], sq_t[:, :], ALU.mult).then_inc(ready, 1)
                dve.wait_ge(ready, 1)
                dve.wait_ge(copied, done(NT - 1))
                link(nc.vector.tensor_reduce(col[:, 0:1], h_t[:, 0:N], AX.X, ALU.add))
                link(nc.vector.tensor_scalar(col[:, 0:1], col[:, 0:1], 1.0 / N, None, ALU.mult))
                link(nc.vector.tensor_scalar(h_t[:, :], h_t[:, :], col[:, 0:1], None, ALU.subtract))
                link(nc.vector.tensor_tensor(sq_t[:, 0:N], h_t[:, 0:N], h_t[:, 0:N], ALU.mult))
                link(nc.vector.tensor_reduce(col[:, 1:2], sq_t[:, 0:N], AX.X, ALU.add))
                nc.vector.tensor_scalar(col[:, 1:2], col[:, 1:2], 1.0 / N, EPS, ALU.mult, ALU.add).then_inc(root_in, 1)
                dve.wait_ge(root_out, 1)
                link(nc.vector.reciprocal(col[:, 1:2], col[:, 1:2]))
                link(nc.vector.tensor_tensor(col[:, 2:3], col[:, 1:2], col_n2[:, 1:2], ALU.mult))
                link(nc.vector.tensor_tensor(col[:, 4:5], col[:, 0:1], col_n2[:, 0:1], ALU.add))
                link(nc.vector.tensor_tensor(col[:, 5:6], col[:, 0:1], col_n2[:, 0:1], ALU.add))
                link(nc.vector.tensor_tensor(col[:, 4:5], col[:, 4:5], col[:, 5:6], ALU.subtract))
                link(nc.vector.tensor_tensor(col[:, 4:5], col[:, 4:5], col[:, 2:3], ALU.mult))
                nc.vector.tensor_tensor(col[:, 3:4], col[:, 4:5], col_n2[:, 2:3], ALU.add).then_inc(root_in, 1)

                def step(i, k):
                    t = i * 2 + k
                    dve.wait_ge(turned, done(t))
                    nc.vector.tensor_tensor(block_of(z_nm, t), ps_z[k][:, 0:SUB * D].rearrange("p (j f) -> p j f", j=SUB), block_of(x_nm, t), ALU.add).then_inc(summed, 1)
                rounds(dve, step, NT, 2)
                dve.wait_ge(summed, done(NT - 1))
                z, mid_ = flat(z_nm), mid[:, :, :]
                link(nc.vector.tensor_reduce(sums[:, :], z, AX.X, ALU.add))
                link(nc.vector.tensor_scalar(sums[:, :], sums[:, :], 1.0 / D, None, ALU.mult))
                link(nc.vector.tensor_tensor(z, z, bc_last(sums[:, :], D), ALU.subtract))
                link(nc.vector.tensor_tensor(mid_, z, z, ALU.mult))
                link(nc.vector.tensor_reduce(squares[:, :], mid_, AX.X, ALU.add))
                nc.vector.tensor_scalar(squares[:, :], squares[:, :], 1.0 / D, EPS, ALU.mult, ALU.add).then_inc(root_in, 1)
                dve.wait_ge(root_out, 2)
                link(nc.vector.reciprocal(squares[:, :], squares[:, :]))
                nc.vector.tensor_tensor(z, z, bc_last(squares[:, :], D), ALU.mult).then_inc(root_in, 1)

        with ExitStack() as c:
            sem, own = stage_semaphores(c, "r1_")
            s_win = [sem(f"win{k}") for k in range(4)]
            s_scat = [gather_sem(f"r1_scat{k}") for k in range(2)]
            (hot, turned, turned_sb, expanded, rows_sb, spread_in, spread, equal, dup, index, pooled, pooled_sb, taken, pool_turn, pe_turn, s_clear, cleared,
             c1, c2, c3, c4, c5, ones_set) = (
                sem(n) for n in ("hot", "turned", "turned_sb", "expanded", "rows_sb", "spread_in", "spread", "equal", "dup", "index", "pooled", "pooled_sb",
                                 "taken", "pool_turn", "pe_turn", "s_clear", "cleared", "c1", "c2", "c3", "c4", "c5", "ones_set"))
            win = sb("r1_win", [W, 4, D], ctx=c)
            onehot = sb("r1_onehot", [128, 2, SUB, W], ctx=c)
            onehot_t = sb("r1_onehot_t", [W, 2, GE], ctx=c)
            rows = sb("r1_rows", [128, 2, SUB, D + 1], ctx=c)
            diag = sb("r1_diag", [128, 2, SUB, 128], ctx=c)
            eq = sb("r1_eq", [128, 2, SUB, 128], ctx=c)
            eq_low = sb("r1_eq_low", [128, SUB, 128], ctx=c)
            before = sb("r1_before", [128, SUB], ctx=c)
            shift = sb("r1_shift", [128, SUB], ctx=c)
            target = sb("r1_target", [128, 4, SUB], i32, c)
            pooled_rows = sb("r1_pooled", [128, 4, SUB, D + 1], ctx=c)
            zeros = sb("r1_zeros", [128, (NP // 128) * (D + 1)], ctx=c)
            ps_o = [c.enter_context(nc.psum_tensor(f"r1_o{k}", [128, 512], fp32)) for k in range(2)]
            ps_x = [c.enter_context(nc.psum_tensor(f"r1_x{k}", [128, 512], fp32)) for k in range(2)]
            ps_e = [c.enter_context(nc.psum_tensor(f"r1_e{k}", [128, 512], fp32)) for k in range(2)]
            ps_r = [c.enter_context(nc.psum_tensor(f"r1_r{k}", [128, 512], fp32)) for k in range(2)]
            gen = general_path(c, sem, "r1", D + 1, src_pad, [(tab_x3, dst_pad, rows[:, 0, :, 0:D])], rows[:, 0], ps_r[0])
            gen_zero, gen_out = sem("gen_zero"), sem("gen_out")
            block = c.enter_context(stage_block(own))

            @block.sync
            def _(sp):
                sp.wait_ge(cleared, 1)
                for q in range(TABLES):
                    sp.dma_start(scat[q][0:NP, :].rearrange("(p r) f -> p (r f)", p=128), zeros[:, :]).then_inc(s_clear, 16)
                    sp.dma_start(scat[q][NP:NP + 128, :], zeros[:, 0:D + 1]).then_inc(s_clear, 16)
                    sp.dma_start(scat[q][NP + 128:NP + 129, :], zeros[0:1, 0:D + 1]).then_inc(s_clear, 16)

                def general():
                    sp.wait_ge(s_clear, 3 * TABLES * 16)
                    gen.sync(sp)
                    sp.wait_ge(gen.begun, NG + 1)
                    for t in range(NT):
                        sp.dma_start(scat[0][t * GE:(t + 1) * GE, :].rearrange("n f -> f n"), acc[:, t * GE:(t + 1) * GE],
                                     allow_slow_non_contiguous=True).then_inc(gen_out, 16)
                    sp.wait_ge(gen_out, NT * 16)

                def windows():
                    def step(i, k):
                        g = i * 4 + k
                        start = sp.value_load(base[0:1, bass.ds(g, 1)], min_val=0, max_val=N)
                        sp.wait_ge(expanded, done(g - 4))
                        sp.dma_start(win[:, k, :], tab_x3[bass.ds(start, W), :]).then_inc(s_win[k], 16)
                    rounds(sp, step, NG, 4)

                by_flag(sp, general, windows)

            @block.gpsimd
            def _(pool):
                pool.memset(zeros[:, :], 0.0).then_inc(cleared, 1)
                def general():
                    gen.gpsimd(pool)

                def windows():
                    pool.sem_inc(taken, CR)
                    pool.wait_ge(s_clear, 3 * TABLES * 16)

                    def step(i, k):
                        g = i * 4 + k
                        pool.wait_ge(pooled_sb, done(g))
                        pool.wait_ge(index, done(g))
                        if not isinstance(g, int) or g >= 2:
                            pool.wait_ge(s_scat[k % 2], (i * 2 + k // 2) * 64)
                        pool.sem_inc(taken, 1)
                        for s in range(SUB):
                            nc.gpsimd.indirect_dma_start(
                                out=scat[(k % 2) * SUB + s], out_offset=bass.IndirectOffsetOnAxis(ap=target[:, k, s:s + 1], axis=0),
                                in_=pooled_rows[:, k, s, :], in_offset=None, compute_op=ALU.add).then_inc(s_scat[k % 2], 16)
                    for k in range(4):
                        step(0, k)
                    with pool.Fori(1, NG // 4) as i:
                        for k in range(4):
                            step(i, k)
                    for k in range(NG % 4):
                        step(NG // 4, k)
                    for k in range(2):
                        pool.wait_ge(s_scat[k], (NG + 1 - k) // 2 * 64)

                by_flag(pool, general, windows)

            @block.vector
            def _(dve):
                nc.vector.memset(rows[:, :, :, D:D + 1], 1.0).then_inc(ones_set, 1)
                def general():
                    nc.vector.memset(acc[:, :], 0.0).then_inc(gen_zero, 1)
                    dve.wait_ge(gen_zero, 1)
                    gen.vector(dve)

                def windows():
                    for s_ in (hot, spread_in, equal, dup, index, c1, c2, c3, c4, c5):
                        dve.sem_inc(s_, CR)

                    def sources(g):
                        return src_f[:, bass.ds(g, 1), :].rearrange("p a s -> p (a s)")

                    def prepare(i, k):
                        i, k = i + k // 4, k % 4
                        g = i * 4 + k
                        dve.wait_ge(turned, done(g - 2))
                        nc.vector.tensor_tensor(onehot[:, k % 2], iota_w[:, :, :],
                                                bc_last(rel[:, bass.ds(g, 1), :].rearrange("p a s -> p (a s)"), W), ALU.is_equal).then_inc(hot, 1)
                        dve.wait_ge(spread, done(g - 2))
                        nc.vector.tensor_tensor(diag[:, k % 2], ident[:, :].unsqueeze(1).to_broadcast([128, SUB, 128]),
                                                bc_last(sources(g), 128), ALU.mult).then_inc(spread_in, 1)
                    prepare(0, 0)

                    def step(i, k):
                        g = i * 4 + k
                        if not isinstance(i, int) or g + 1 < NG:
                            prepare(i, k + 1)
                        dve.wait_ge(spread, done(g))
                        dve.wait_ge(pooled, done(g - 2))
                        nc.vector.tensor_tensor(eq[:, k % 2], ps_e[k % 2][:, :].rearrange("p (s e) -> p s e", s=SUB),
                                                bc_last(sources(g), 128), ALU.is_equal).then_inc(equal, 1)
                        dve.wait_ge(equal, done(g))
                        dve.wait_ge(dup, done(g - 1))
                        nc.vector.tensor_tensor(eq_low[:, :, :], eq[:, k % 2], lower[:, :].unsqueeze(1).to_broadcast([128, SUB, 128]), ALU.mult).then_inc(c1, 1)
                        dve.wait_ge(c1, done(g))
                        dve.wait_ge(c4, done(g - 1))
                        nc.vector.tensor_reduce(before[:, :], eq_low[:, :, :], AX.X, ALU.max).then_inc(dup, 1)
                        nc.vector.tensor_scalar(shift[:, :], sources(g), spare[:, :], -1.0, ALU.subtract, ALU.mult).then_inc(c2, 1)
                        dve.wait_ge(dup, done(g))
                        dve.wait_ge(c2, done(g))
                        nc.vector.tensor_tensor(shift[:, :], shift[:, :], before[:, :], ALU.mult).then_inc(c4, 1)
                        dve.wait_ge(c4, done(g))
                        dve.wait_ge(taken, done(g - 2))
                        nc.vector.tensor_tensor(target[:, k], shift[:, :], sources(g), ALU.add).then_inc(index, 1)
                        dve.wait_ge(index, done(g))
                    rounds(dve, step, NG, 4)

                by_flag(dve, general, windows)

            @block.tensor
            def _(pe):
                def general():
                    pe.wait_ge(ones_set, 1)
                    gen.tensor(pe)

                def windows():
                    for s_ in (turned, expanded, spread, pooled):
                        pe.sem_inc(s_, CR)

                    def turn(i, k):
                        i, k = i + k // 4, k % 4
                        g = i * 4 + k
                        pe.wait_ge(hot, done(g))
                        pe.wait_ge(turned_sb, done(g - 2))
                        pe.sem_inc(pe_turn, 1)
                        for s in range(SUB):
                            last = nc.tensor.transpose(ps_o[k % 2][0:W, s * 128:(s + 1) * 128], onehot[:, k % 2, s, :], ident[:, :])
                        last.then_inc(turned, 1)
                        pe.wait_ge(spread_in, done(g))
                        pe.wait_ge(equal, done(g - 2))
                        nc.tensor.matmul(ps_e[k % 2][:, :], ones_sq[:, :], diag[:, k % 2].rearrange("p s e -> p (s e)"), start=True, stop=True).then_inc(spread, 1)
                    turn(0, 0)

                    def step(i, k):
                        g = i * 4 + k
                        if not isinstance(i, int) or g + 1 < NG:
                            turn(i, k + 1)
                        pe.wait_ge(turned_sb, done(g))
                        pe.wait_ge(rows_sb, done(g - 2))
                        pe.wait_ge(s_win[k], (i + 1) * 16)
                        pe.sem_inc(pe_turn, 1)
                        for s in range(SUB):
                            last = nc.tensor.matmul(ps_x[k % 2][:, s * D:(s + 1) * D], onehot_t[:, k % 2, s * 128:(s + 1) * 128], win[:, k, :], start=True, stop=True)
                        last.then_inc(expanded, 1)
                        pe.wait_ge(rows_sb, done(g))
                        pe.wait_ge(pooled_sb, done(g - 2))
                        pe.wait_ge(equal, done(g))
                        for s in range(SUB):
                            last = nc.tensor.matmul(ps_r[k % 2][:, s * (D + 1):(s + 1) * (D + 1)], eq[:, k % 2, s, :], rows[:, k % 2, s, :], start=True, stop=True)
                        last.then_inc(pooled, 1)
                    rounds(pe, step, NG, 4)

                by_flag(pe, general, windows)

            @block.scalar
            def _(act):
                def general():
                    act.wait_ge(ones_set, 1)

                def windows():
                    for s_ in (turned_sb, rows_sb, pooled_sb):
                        act.sem_inc(s_, CR)
                    act.wait_ge(ones_set, 1)

                    def copy_turned(i, k):
                        i, k = i + k // 4, k % 4
                        g = i * 4 + k
                        act.wait_ge(turned, done(g))
                        act.wait_ge(expanded, done(g - 2))
                        nc.scalar.copy(onehot_t[:, k % 2, :], ps_o[k % 2][0:W, :]).then_inc(turned_sb, 1)
                    copy_turned(0, 0)

                    def step(i, k):
                        g = i * 4 + k
                        if not isinstance(i, int) or g + 1 < NG:
                            copy_turned(i, k + 1)
                        act.wait_ge(expanded, done(g))
                        act.wait_ge(pooled, done(g - 2))
                        nc.scalar.copy(rows[:, k % 2, :, 0:D], ps_x[k % 2][:, 0:SUB * D].rearrange("p (s f) -> p s f", s=SUB)).then_inc(rows_sb, 1)
                        act.wait_ge(pooled, done(g))
                        act.wait_ge(taken, done(g - 2))
                        nc.scalar.copy(pooled_rows[:, k].rearrange("p s f -> p (s f)"), ps_r[k % 2][:, 0:SUB * (D + 1)]).then_inc(pooled_sb, 1)
                    rounds(act, step, NG, 4)

                by_flag(act, general, windows)

        with ExitStack() as c:
            sem, own = stage_semaphores(c, "r2_")
            s_tab = [sem(f"tab{q}") for q in range(TABLES)]
            added, chain, staged, turned, turned_sb, product, summed, pe_turn, root_in, root_out, s_out = (
                sem(n) for n in ("added", "chain", "staged", "turned", "turned_sb", "product", "summed", "pe_turn", "root_in", "root_out", "s_out"))
            R = D + 1
            part = sb("r2_part", [128, 2, NT, SUB * R], ctx=c)
            total = sb("r2_total", [128, NT, SUB, R], ctx=c)
            rdeg = sb("r2_rdeg", [128, NT, SUB], ctx=c)
            ss = sb("r2_ss", [128, 2, SUB, R], ctx=c)
            sts = sb("r2_sts", [R, 2, GE], ctx=c)
            ps_t = [c.enter_context(nc.psum_tensor(f"r2_t{k}", [128, 512], fp32)) for k in range(2)]
            ps_p = [c.enter_context(nc.psum_tensor(f"r2_p{k}", [128, 512], fp32)) for k in range(2)]
            sums, squares = sb("r2_sums", [128, NT * SUB], ctx=c), sb("r2_squares", [128, NT * SUB], ctx=c)
            mid = sb("r2_mid", [128, NT * SUB, D], ctx=c)
            block = c.enter_context(stage_block(own))

            @block.sync
            def _(sp):
                for q in range(TABLES):
                    if q >= 2:
                        sp.wait_ge(added, q - 1)
                    sp.dma_start(part[:, q % 2], scat[q][0:NP, :].rearrange("(t p j) f -> p t (j f)", p=LANES, j=SUB)).then_inc(s_tab[q], 16)
                sp.wait_ge(root_in, 2)
                sp.dma_start(out[0:NFULL * GE, :].rearrange("(t p j) f -> p t (j f)", p=LANES, j=SUB),
                             x_nm[:, 0:NFULL].rearrange("p t j f -> p t (j f)")).then_inc(s_out, 16)
                sp.dma_start(out[NFULL * GE:NFULL * GE + NREST * SUB, :].rearrange("(p j) f -> p (j f)", j=SUB),
                             x_nm[0:NREST, NFULL].rearrange("p j f -> p (j f)")).then_inc(s_out, 16)
                sp.dma_start(out[N - NLEFT:N, :].rearrange("(p j) f -> p (j f)", j=NLEFT),
                             x_nm[NREST:NREST + 1, NFULL, 0:NLEFT].rearrange("p j f -> p (j f)")).then_inc(s_out, 16)
                sp.wait_ge(s_out, 48)

            @block.vector
            def _(dve):
                link = linker(dve, chain)
                dve.sem_inc(staged, CR)
                dve.sem_inc(summed, CR)
                tot = total[:, :, :, :].rearrange("p t j f -> p t (j f)")
                for q in range(TABLES):
                    dve.wait_ge(s_tab[q], 16)
                    if q == 0:
                        nc.vector.tensor_copy(tot, part[:, 0]).then_inc(added, 1)
                    else:
                        nc.vector.tensor_tensor(tot, tot, part[:, q % 2], ALU.add).then_inc(added, 1)
                    dve.wait_ge(added, q + 1)
                link(nc.vector.tensor_scalar(rdeg[:, :, :], total[:, :, :, D], 1.0, None, ALU.max))
                link(nc.vector.reciprocal(rdeg[:, :, :], rdeg[:, :, :]))

                def step(i, k):
                    t = i * 2 + k
                    dve.wait_ge(turned, done(t - 2))
                    nc.vector.tensor_tensor(ss[:, k], block_of(total, t), bc_last(per_node(rdeg, t), R), ALU.mult).then_inc(staged, 1)
                    dve.wait_ge(product, done(t))
                    nc.vector.tensor_tensor(block_of(x_nm, t), ps_p[k][:, 0:SUB * D].rearrange("p (j f) -> p j f", j=SUB), block_of(z_nm, t), ALU.add).then_inc(summed, 1)
                rounds(dve, step, NT, 2)
                dve.wait_ge(summed, done(NT - 1))
                z, mid_ = flat(x_nm), mid[:, :, :]
                link(nc.vector.tensor_reduce(sums[:, :], z, AX.X, ALU.add))
                link(nc.vector.tensor_scalar(sums[:, :], sums[:, :], 1.0 / D, None, ALU.mult))
                link(nc.vector.tensor_tensor(z, z, bc_last(sums[:, :], D), ALU.subtract))
                link(nc.vector.tensor_tensor(mid_, z, z, ALU.mult))
                link(nc.vector.tensor_reduce(squares[:, :], mid_, AX.X, ALU.add))
                nc.vector.tensor_scalar(squares[:, :], squares[:, :], 1.0 / D, EPS, ALU.mult, ALU.add).then_inc(root_in, 1)
                dve.wait_ge(root_out, 1)
                link(nc.vector.reciprocal(squares[:, :], squares[:, :]))
                nc.vector.tensor_tensor(z, z, bc_last(squares[:, :], D), ALU.mult).then_inc(root_in, 1)

            @block.tensor
            def _(pe):
                pe.sem_inc(turned, CR)
                pe.sem_inc(product, CR)

                def step(i, k):
                    t = i * 2 + k
                    pe.wait_ge(staged, done(t))
                    pe.wait_ge(turned_sb, done(t - 2))
                    pe.sem_inc(pe_turn, 1)
                    for j in range(SUB):
                        last = nc.tensor.transpose(ps_t[k][0:R, j * 128:(j + 1) * 128], ss[:, k, j, :], ident[:, :])
                    last.then_inc(turned, 1)
                    pe.wait_ge(turned_sb, done(t))
                    pe.wait_ge(summed, done(t - 2))
                    for j in range(SUB):
                        last = nc.tensor.matmul(ps_p[k][:, j * D:(j + 1) * D], sts[:, k, j * 128:(j + 1) * 128], w_3[:, :], start=True, stop=True)
                    last.then_inc(product, 1)
                rounds(pe, step, NT, 2)

            @block.scalar
            def _(act):
                act.sem_inc(turned_sb, CR)

                def step(i, k):
                    t = i * 2 + k
                    act.wait_ge(turned, done(t))
                    act.wait_ge(product, done(t - 2))
                    nc.scalar.copy(sts[:, k, :], ps_t[k][0:R, :]).then_inc(turned_sb, 1)
                rounds(act, step, NT, 2)
                act.wait_ge(root_in, 1)
                nc.scalar.activation(squares[:, :], squares[:, :], ACT.Sqrt).then_inc(root_out, 1)


_INS = ["x", "src", "dst", "edge_attr_32", "edge_attr_64", "L0_gnn_W_m1", "L0_gnn_b_m1", "L0_gnn_W_m2", "L0_gnn_b_m2",
        "L0_gnn_W_c1", "L0_gnn_b_c1", "L0_gnn_W_c2", "L0_gnn_b_c2", "L1_gnn_W1", "L1_gnn_b1", "L1_gnn_W2", "L1_gnn_b2",
        "L2_gnn_u", "L2_gnn_W1", "L2_gnn_b1", "L2_gnn_g1", "L2_gnn_be1", "L2_gnn_W2", "L2_gnn_b2", "L2_gnn_g2", "L2_gnn_be2",
        "L3_gnn_W", "L3_gnn_b"]


def kernel(**inputs):
    import numpy as np
    import concourse.bacc as bacc
    from concourse import mybir
    from concourse.bass_utils import run_bass_kernel_spmd

    nc = bacc.Bacc("TRN2", target_bir_lowering=False, num_devices=1)
    arrays = {name: np.ascontiguousarray(inputs[name]) for name in _INS if name not in ("L2_gnn_u", "L3_gnn_W")}
    arrays["L3_gnn_W_t"] = np.ascontiguousarray(np.asarray(inputs["L3_gnn_W"]).T)
    params = {n: nc.dram_tensor(f"in_{n}", a.shape, mybir.dt.from_np(a.dtype), kind="ExternalInput").ap() for n, a in arrays.items()}
    shape = arrays["x"].shape
    out = nc.dram_tensor("out", shape, mybir.dt.float32, kind="ExternalOutput").ap()
    build(nc, params, out)
    r = run_bass_kernel_spmd(nc, [{f"in_{n}": a for n, a in arrays.items()}], core_ids=[0])
    return r.results[0]["out"]
```

```python
def build(nc, P, out):
    import concourse.bass as bass
    from concourse import mybir
    from contextlib import ExitStack, contextmanager

    fp32, i32, bf16, fp16 = mybir.dt.float32, mybir.dt.int32, mybir.dt.bfloat16, mybir.dt.float16
    ALU, ACT, AX = mybir.AluOpType, mybir.ActivationFunctionType, mybir.AxisListType

    N, D = P["x"].shape
    E, DE = P["edge_attr_32"].shape
    H = P["L0_gnn_W_m1"].shape[1]
    HC = P["L0_gnn_W_c1"].shape[1]
    H1 = P["L1_gnn_W1"].shape[1]
    SUB, LANES = 4, 128
    GE = SUB * LANES
    NG = -(-E // GE)
    NT = -(-(N + 1) // GE)
    NP = NT * GE
    W = 24
    HI = NT * SUB
    KEYS = W * HI
    KB = 3
    KW = KEYS // KB
    DB = 256
    NDB = -(-(N + 1) // DB)
    NDL = -(-(N + 1) // LANES)
    DEG_MAX = 256
    TAIL = E - (NG - 1) * GE
    TROWS = TAIL // SUB
    TLEFT = TAIL - TROWS * SUB
    NFULL = N // GE
    NREST = (N - NFULL * GE) // SUB
    NLEFT = N - NFULL * GE - NREST * SUB
    EPS = 1e-5
    CR = 4

    def done(n):
        return n + (1 + CR)

    def rounds(eng, step, total, unroll):
        with eng.Fori(0, total // unroll) as i:
            for k in range(unroll):
                step(i, k)
        for k in range(total % unroll):
            step(total // unroll, k)

    def peeled(eng, step, total, unroll):
        for k in range(unroll):
            step(0, k)
        with eng.Fori(1, total // unroll) as i:
            for k in range(unroll):
                step(i, k)
        for k in range(total % unroll):
            step(total // unroll, k)

    def dram(name, shape, dt=fp32):
        return nc.dram_tensor(name, shape, dt).ap()

    src_pad = dram("src_pad", (NG * GE,), i32)
    dst_pad = dram("dst_pad", (NG * GE,), i32)
    tab_a = dram("tab_a", (NP + 1, H))
    tab_b = dram("tab_b", (NP + W, H))
    tab_y1 = dram("tab_y1", (NP + 1, D))
    tab_y2 = dram("tab_y2", (NP + 1, D))
    tab_t2 = dram("tab_t2", (NP + 1, D))
    tab_x3 = dram("tab_x3", (NP + W, D))
    h_edges = dram("h_edges", (NG * GE, D))
    cnt_dram = dram("cnt_dram", (NP,))
    sums_dram = dram("sums_dram", (NP, D + 1))
    counts = dram("counts", (LANES, NP, HI), bf16)

    def groups(ap):
        return ap.rearrange("(g p s) -> g p s", p=LANES, s=SUB)

    def group_rows(ap, g):
        v = ap[0:(ap.shape[0] // GE) * GE, :].rearrange("(g p s) f -> g p (s f)", p=LANES, s=SUB)
        return v[bass.ds(g, 1)].rearrange("a p f -> (a p) f")

    def destinations(b, n):
        return counts.rearrange("p (b d) h -> b p (d h)", d=n)[bass.ds(b, 1)].rearrange("a p r -> (a p) r")

    whole = ExitStack()
    with whole:
        def sb(name, shape, dt=fp32, ctx=whole):
            return ctx.enter_context(nc.sbuf_tensor(name, shape, dt))

        ident = sb("ident", [128, 128])
        iota_w = sb("iota_w", [128, SUB, W])
        rel = sb("rel", [128, NG, SUB])
        lane_f = sb("lane_f", [128, NG, SUB])
        key_f = sb("key_f", [128, NG, SUB])
        hop = sb("hop", [1, NG], i32)
        flag_f = sb("flag_f", [1, 1])
        deg_nm = sb("deg_nm", [128, HI])
        base = sb("base", [1, NG], i32)
        flag = sb("flag", [1, 1], i32)
        iota_n = sb("iota_n", [128, GE])
        acc = sb("acc", [D + 1, NP])
        x_nm = sb("x_nm", [128, NT, SUB, D])
        z_nm = sb("z_nm", [128, NT, SUB, D])
        cnt_nm = sb("cnt_nm", [128, NT, SUB])
        dinv_nm = sb("dinv_nm", [128, NT, SUB])
        w_ab = sb("w_ab", [D, 2, H])
        w_m2 = sb("w_m2", [H + 1, D])
        b_m1 = sb("b_m1", [H, 1])
        w_c1x = sb("w_c1x", [D, HC])
        w_c1a = sb("w_c1a", [D + 1, HC])
        b_c1 = sb("b_c1", [HC, 1])
        w_c2 = sb("w_c2", [HC + 1, D])
        w_g1 = sb("w_g1", [D, H1])
        b_g1 = sb("b_g1", [H1, 1])
        w_g2 = sb("w_g2", [H1, D])
        b_g2 = sb("b_g2", [128, D])
        w_e1x = sb("w_e1x", [D, D])
        w_e1e = sb("w_e1e", [D, D])
        row_b1 = sb("row_b1", [128, D])
        row_g1 = sb("row_g1", [128, D])
        row_be1 = sb("row_be1", [128, D])
        w_n2x = sb("w_n2x", [D, 2 * D])
        w_n2a = sb("w_n2a", [D, 2 * D])
        col_n2 = sb("col_n2", [D, 3])
        w_3 = sb("w_3", [D + 1, D])
        bn_scale = sb("bn_scale", [128, D])
        bn_shift = sb("bn_shift", [128, D])
        ones_sq = sb("ones_sq", [128, 128])
        ident_b = sb("ident_b", [128, 128], bf16)

        def stage_semaphores(c, prefix):
            own = []

            def sem(name):
                own.append(c.enter_context(nc.semaphore(prefix + name)))
                return own[-1]
            return sem, own

        @contextmanager
        def stage_block(own):
            with nc.Block() as block:
                yield block
            with nc.Block() as after:
                @after.gpsimd
                def _(pool):
                    for s_ in own:
                        pool.sem_clear(s_)

        def gather_sem(name):
            return whole.enter_context(nc.semaphore(name))

        def linker(eng, sem):
            count = [0]

            def link(ins):
                count[0] += 1
                ins.then_inc(sem, 1)
                eng.wait_ge(sem, count[0])
            return link

        def bc_last(ap, n):
            return ap.unsqueeze(len(ap.shape)).to_broadcast(list(ap.shape) + [n])

        with ExitStack() as c, nc.allow_non_contiguous_dma(reason="index columns, once"):
            sem, own = stage_semaphores(c, "")
            pads_set, s_pads, s_load, s_padded = sem("pads_set"), sem("s_pads"), sem("s_load"), sem("s_padded")
            s_idx, consts, vchain, base_ready, base_spread = sem("s_idx"), sem("consts"), sem("vchain"), sem("base_ready"), sem("base_spread")
            s_zero, clears = sem("s_zero"), sem("clears")
            pad_src = sb("pad_src", [1, GE], i32, c)
            pad_dst = sb("pad_dst", [1, GE], i32, c)
            dst_i = sb("dst_i", [128, NG, SUB], i32, c)
            src_i = sb("src_i", [128, NG, SUB], i32, c)
            base_row = sb("base_row", [1, NG], fp32, c)
            base_f = sb("base_f", [128, NG], fp32, c)
            outside = sb("outside", [128, 3], fp32, c)
            hop_f = sb("hop_f", [1, NG], fp32, c)
            later = sb("later", [128, NG, SUB], fp32, c)
            part_i = sb("part_i", [128, NG, SUB], i32, c)
            czero = sb("czero", [128, 64 * HI], bf16, c)
            outside_ready, outside_all = sem("outside_ready"), sem("outside_all")
            zeros = sb("zeros", [128, GE], fp32, c)
            block = c.enter_context(stage_block(own))
            loads = [
                (w_ab[:, 0, :], P["L0_gnn_W_m1"][0:D, :]), (w_ab[:, 1, :], P["L0_gnn_W_m1"][D:2 * D, :]),
                (w_m2[0:H, :], P["L0_gnn_W_m2"]), (w_m2[H:H + 1, :], P["L0_gnn_b_m2"].unsqueeze(0)),
                (b_m1[:, :], P["L0_gnn_b_m1"].unsqueeze(1)),
                (w_c1x[:, :], P["L0_gnn_W_c1"][0:D, :]), (w_c1a[1:D + 1, :], P["L0_gnn_W_c1"][D:2 * D, :]),
                (b_c1[:, :], P["L0_gnn_b_c1"].unsqueeze(1)),
                (w_c2[0:HC, :], P["L0_gnn_W_c2"]), (w_c2[HC:HC + 1, :], P["L0_gnn_b_c2"].unsqueeze(0)),
                (w_g1[:, :], P["L1_gnn_W1"]), (b_g1[:, :], P["L1_gnn_b1"].unsqueeze(1)), (w_g2[:, :], P["L1_gnn_W2"]),
                (b_g2[:, :], P["L1_gnn_b2"].unsqueeze(0).to_broadcast([128, D])),
                (w_e1x[:, :], P["L2_gnn_W1"][0:D, :]), (w_e1e[:, :], P["L2_gnn_W1"][D:2 * D, :]),
                (row_b1[:, :], P["L2_gnn_b1"].unsqueeze(0).to_broadcast([128, D])),
                (row_g1[:, :], P["L2_gnn_g1"].unsqueeze(0).to_broadcast([128, D])),
                (row_be1[:, :], P["L2_gnn_be1"].unsqueeze(0).to_broadcast([128, D])),
                (w_n2x[:, 0:D], P["L2_gnn_W2"][0:D, :]), (w_n2a[:, 0:D], P["L2_gnn_W2"][D:2 * D, :]),
                (col_n2[:, 0:1], P["L2_gnn_b2"].unsqueeze(1)), (col_n2[:, 1:2], P["L2_gnn_g2"].unsqueeze(1)),
                (col_n2[:, 2:3], P["L2_gnn_be2"].unsqueeze(1)),
                (w_3[0:D, :], P["L3_gnn_W_t"]), (w_3[D:D + 1, :], P["L3_gnn_b"].unsqueeze(0)),
                (x_nm[:, 0:NFULL].rearrange("p t j f -> p t (j f)"),
                 P["x"][0:NFULL * GE, :].rearrange("(t p j) f -> p t (j f)", p=LANES, j=SUB)),
                (x_nm[0:NREST, NFULL].rearrange("p j f -> p (j f)"),
                 P["x"][NFULL * GE:NFULL * GE + NREST * SUB, :].rearrange("(p j) f -> p (j f)", j=SUB)),
                (x_nm[NREST:NREST + 1, NFULL, 0:NLEFT].rearrange("p j f -> p (j f)"),
                 P["x"][N - NLEFT:N, :].rearrange("(p j) f -> p (j f)", j=NLEFT)),
            ]

            @block.sync
            def _(sp):
                sp.dma_start(src_pad[0:E], P["src"]).then_inc(s_padded, 16)
                sp.dma_start(dst_pad[0:E], P["dst"]).then_inc(s_padded, 16)
                sp.wait_ge(pads_set, 2)
                sp.dma_start(src_pad[E:NG * GE].unsqueeze(0), pad_src[:, 0:NG * GE - E]).then_inc(s_padded, 16)
                sp.dma_start(dst_pad[E:NG * GE].unsqueeze(0), pad_dst[:, 0:NG * GE - E]).then_inc(s_padded, 16)
                sp.wait_ge(clears, 5)
                for to, of in loads:
                    sp.dma_start(to, of).then_inc(s_load, 16)
                sp.wait_ge(s_padded, 64)
                sp.dma_start(dst_i[:, :, :], groups(dst_pad).rearrange("g p s -> p g s")).then_inc(s_idx, 16)
                sp.dma_start(src_i[:, :, :], groups(src_pad).rearrange("g p s -> p g s")).then_inc(s_idx, 16)
                sp.dma_start(base[:, :], dst_pad.rearrange("(a g e) -> a g e", a=1, e=GE)[:, :, 0]).then_inc(s_idx, 16)
                sp.wait_ge(consts, 2)
                for tab in (tab_a, tab_y1, tab_y2, tab_t2):
                    sp.dma_start(tab[NP:NP + 1, :], zeros[0:1, 0:tab.shape[1]]).then_inc(s_zero, 16)
                for tab in (tab_b, tab_x3):
                    sp.dma_start(tab[NP:NP + W, :], zeros[0:W, 0:tab.shape[1]]).then_inc(s_zero, 16)
                for d in range(N + 1, NDB * DB, 64):
                    rows_ = min(64, NDB * DB - d)
                    sp.dma_start(counts[:, d:d + rows_, :].rearrange("p d h -> p (d h)"), czero[:, 0:rows_ * HI]).then_inc(s_zero, 16)
                sp.wait_ge(s_zero, (6 + -(-(NDB * DB - N - 1) // 64)) * 16)
                sp.wait_ge(s_load, len(loads) * 16)

            @block.gpsimd
            def _(pool):
                pool.memset(pad_src[:, :], NP).then_inc(pads_set, 1)
                pool.memset(pad_dst[:, :], N).then_inc(pads_set, 1)
                pool.memset(x_nm[:, NT - 1], 0.0).then_inc(clears, 1)
                pool.memset(w_c1a[0:1, :], 0.0).then_inc(clears, 1)
                pool.memset(acc[:, :], 0.0).then_inc(clears, 1)
                pool.memset(w_n2x[:, D:2 * D], 0.0).then_inc(clears, 1)
                pool.memset(w_n2a[:, D:2 * D], 0.0).then_inc(clears, 1)
                pool.memset(zeros[:, :], 0.0).then_inc(consts, 1)
                pool.memset(czero[:, :], 0.0).then_inc(consts, 1)
                pool.memset(ones_sq[:, :], 1.0).then_inc(consts, 1)
                pool.memset(ident[:, :], 0.0).then_inc(consts, 1)
                pool.wait_ge(consts, 4)
                pool.affine_select(out=ident[:, :], in_=ident[:, :], compare_op=ALU.not_equal, fill=1.0,
                                   base=0, pattern=[[-1, 128]], channel_multiplier=1).then_inc(consts, 1)
                pool.wait_ge(consts, 5)
                pool.tensor_copy(ident_b[:, :], ident[:, :]).then_inc(consts, 1)
                pool.iota(iota_w[:, :, :], pattern=[[0, SUB], [1, W]], base=0, channel_multiplier=0,
                          allow_small_or_imprecise_dtypes=True).then_inc(consts, 1)
                pool.iota(iota_n[:, :], pattern=[[1, GE]], base=0, channel_multiplier=0,
                          allow_small_or_imprecise_dtypes=True).then_inc(consts, 1)
                pool.wait_ge(base_ready, 1)
                pool.partition_broadcast(base_f[:, :], base_row[:, :], 128).then_inc(base_spread, 1)
                pool.wait_ge(outside_ready, 1)
                pool.partition_all_reduce(outside[:, :], outside[:, :], 128, bass.bass_isa.ReduceOp.max).then_inc(outside_all, 1)

            @block.vector
            def _(dve):
                dve.wait_ge(s_idx, 48)
                nc.vector.tensor_copy(base_row[:, :], base[:, :]).then_inc(base_ready, 1)
                link = linker(dve, vchain)
                link(nc.vector.tensor_scalar(part_i[:, :, :], src_i[:, :, :], 2, 127, ALU.logical_shift_right, ALU.bitwise_and))
                link(nc.vector.tensor_copy(lane_f[:, :, :], part_i[:, :, :]))
                link(nc.vector.tensor_scalar(part_i[:, :, :], src_i[:, :, :], 3, None, ALU.bitwise_and))
                link(nc.vector.tensor_copy(key_f[:, :, :], part_i[:, :, :]))
                link(nc.vector.tensor_scalar(part_i[:, :, :], src_i[:, :, :], 7, 124, ALU.logical_shift_right, ALU.bitwise_and))
                link(nc.vector.tensor_copy(later[:, :, :], part_i[:, :, :]))
                link(nc.vector.tensor_tensor(key_f[:, :, :], key_f[:, :, :], later[:, :, :], ALU.add))
                link(nc.vector.tensor_scalar(later[:, :, :], key_f[:, :, :], HI - 0.5, 4096.0, ALU.is_gt, ALU.mult))
                link(nc.vector.tensor_tensor(key_f[:, :, :], key_f[:, :, :], later[:, :, :], ALU.add))
                link(nc.vector.tensor_copy(rel[:, :, :], dst_i[:, :, :]))
                dve.wait_ge(base_spread, 1)
                link(nc.vector.tensor_tensor(later[:, 0:NG - 1, :], rel[:, 0:NG - 1, :], bc_last(base_f[:, 1:NG], SUB), ALU.subtract))
                link(nc.vector.tensor_tensor(rel[:, :, :], rel[:, :, :], bc_last(base_f[:, :], SUB), ALU.subtract))
                link(nc.vector.scalar_tensor_tensor(out=key_f[:, :, :], in0=rel[:, :, :], scalar=float(HI), in1=key_f[:, :, :], op0=ALU.mult, op1=ALU.add))
                rel_flat = rel[:, :, :].rearrange("p g s -> p (g s)")
                link(nc.vector.tensor_reduce(outside[:, 0:1], rel_flat, AX.X, ALU.max))
                link(nc.vector.tensor_reduce(outside[:, 1:2], rel_flat, AX.X, ALU.min))
                link(nc.vector.tensor_reduce(outside[:, 2:3], later[:, 0:NG - 1, :].rearrange("p g s -> p (g s)"), AX.X, ALU.max))
                link(nc.vector.tensor_scalar(outside[:, 0:1], outside[:, 0:1], float(W - 1), None, ALU.subtract))
                link(nc.vector.tensor_scalar(outside[:, 1:2], outside[:, 1:2], -1.0, None, ALU.mult))
                link(nc.vector.tensor_copy(hop_f[:, 0:1], base_row[:, 0:1]))
                link(nc.vector.tensor_tensor(hop_f[:, 1:NG], base_row[:, 1:NG], base_row[:, 0:NG - 1], ALU.subtract))
                link(nc.vector.tensor_reduce(flag_f[:, :], hop_f[:, :], AX.X, ALU.max))
                link(nc.vector.tensor_scalar(flag_f[:, :], flag_f[:, :], float(W - 1), None, ALU.subtract))
                link(nc.vector.tensor_tensor(flag_f[:, :], flag_f[:, :], base_row[:, 0:1], ALU.max))
                link(nc.vector.tensor_scalar(hop_f[:, :], hop_f[:, :], float(HI), None, ALU.mult))
                link(nc.vector.tensor_copy(hop[:, :], hop_f[:, :]))
                nc.vector.tensor_tensor(outside[:, 0:1], outside[:, 0:1], outside[:, 2:3], ALU.max).then_inc(outside_ready, 1)
                dve.wait_ge(outside_all, 1)
                link(nc.vector.tensor_tensor(outside[0:1, 0:1], outside[0:1, 0:1], outside[0:1, 1:2], ALU.max))
                link(nc.vector.tensor_tensor(flag_f[:, :], flag_f[:, :], outside[0:1, 0:1], ALU.max))
                link(nc.vector.tensor_scalar(flag_f[:, :], flag_f[:, :], 0.0, None, ALU.is_gt))
                nc.vector.tensor_copy(flag[:, :], flag_f[:, :])

        def general_path(c, sem, name, width, target, tabs, message_tile, ps, after=()):
            class gen:
                pass
            gen.begun, gen.loaded, gen.message, gen.hot, gen.summed, gen.added, gen.turn, gen.lowered = (
                sem(f"gen_{n}") for n in ("begun", "loaded", "message", "hot", "summed", "added", "turn", "lowered"))
            gen.gathered = gather_sem(f"{name}_gen_gathered") if tabs else gen.loaded
            target_i = sb(f"{name}_gen_target_i", [128, SUB], i32, c)
            target_f = sb(f"{name}_gen_target_f", [128, SUB], ctx=c)
            index = [sb(f"{name}_gen_index{n}", [128, SUB], i32, c) for n in range(len(tabs))]
            onehot = sb(f"{name}_gen_onehot", [128, SUB, GE], ctx=c)
            gen.per_group = (1 + len(tabs)) * 16

            def each_group(eng, step):
                with eng.Fori(0, NG - 1) as g:
                    step(g)
                step(NG - 1)
            gen.each_group = each_group

            def sync(sp, load=None):
                def step(g):
                    g = sp.snap(g) if not isinstance(g, int) else g
                    sp.wait_ge(gen.begun, g + 1)
                    sp.dma_start(target_i[:, :], group_rows(target.unsqueeze(1), g)).then_inc(gen.loaded, 16)
                    for n, (_, indices, _) in enumerate(tabs):
                        sp.dma_start(index[n][:, :], group_rows(indices.unsqueeze(1), g)).then_inc(gen.loaded, 16)
                    if load is not None:
                        load(g)
                each_group(sp, step)
            gen.sync = sync

            def gpsimd(pool):
                def step(g):
                    pool.wait_ge(gen.loaded, (g + 1) * gen.per_group)
                    pool.sem_inc(gen.turn, 1)
                    for n, (tab, _, to) in enumerate(tabs):
                        for s in range(SUB):
                            nc.gpsimd.indirect_dma_start(
                                out=to[:, s, :], out_offset=None, in_=tab,
                                in_offset=bass.IndirectOffsetOnAxis(ap=index[n][:, s:s + 1], axis=0)).then_inc(gen.gathered, 16)
                each_group(pool, step)
            gen.gpsimd = gpsimd
            gen.rows_in = len(tabs) * SUB * 16

            def vector(dve, make=None):
                dve.sem_inc(gen.begun, 1)

                def step(g):
                    dve.wait_ge(gen.loaded, (g + 1) * gen.per_group)
                    nc.vector.tensor_copy(target_f[:, :], target_i[:, :]).then_inc(gen.lowered, 1)
                    if make is not None:
                        make(g)

                    def block(v):
                        dve.wait_ge(gen.lowered, (g * (NT + 1) + v) + 1)
                        nc.vector.tensor_tensor(onehot[:, :, :], iota_n[:, :].unsqueeze(1).to_broadcast([128, SUB, GE]),
                                                bc_last(target_f[:, :], GE), ALU.is_equal).then_inc(gen.hot, 1)
                        dve.wait_ge(gen.hot, (g * NT + v) + 1)
                        nc.vector.tensor_scalar(target_f[:, :], target_f[:, :], float(GE), None, ALU.subtract).then_inc(gen.lowered, 1)
                        dve.wait_ge(gen.summed, (g * NT + v) + 1)
                        nc.vector.tensor_tensor(acc[0:width, bass.ds(v * GE, GE)], acc[0:width, bass.ds(v * GE, GE)], ps[0:width, :], ALU.add).then_inc(gen.added, 1)
                    with dve.Fori(0, NT) as v:
                        block(v)
                    dve.wait_ge(gen.lowered, (g + 1) * (NT + 1))
                    dve.wait_ge(gen.added, (g + 1) * NT)
                    dve.sem_inc(gen.begun, 1)
                each_group(dve, step)
            gen.vector = vector

            def tensor(pe, make=None):
                def step(g):
                    if make is not None:
                        make(g)

                    def block(v):
                        if make is not None or not tabs:
                            pe.wait_ge(gen.message, g + 1)
                        else:
                            pe.wait_ge(gen.gathered, (g + 1) * gen.rows_in)
                        pe.wait_ge(gen.hot, (g * NT + v) + 1)
                        pe.sem_inc(gen.turn_pe, 1)
                        for s in range(SUB):
                            last = nc.tensor.matmul(ps[0:width, :], message_tile[:, s, 0:width], onehot[:, s, :], start=s == 0, stop=s == SUB - 1)
                        last.then_inc(gen.summed, 1)
                    with pe.Fori(0, NT) as v:
                        block(v)
                each_group(pe, step)
            gen.turn_pe = sem("gen_turn_pe")
            gen.tensor = tensor
            return gen

        def by_flag(eng, general, windows):
            outside_some = eng.value_load(flag[0:1, 0:1], min_val=0, max_val=1)
            with eng.If(outside_some):
                general()
            with eng.Else():
                windows()

        with ExitStack() as c:
            sem, own = stage_semaphores(c, "")
            staged, turned, turned_sb, product, tables_sb = (sem(f"ta_{n}") for n in ("staged", "turned", "turned_sb", "product", "tables_sb"))
            s_store = [sem(f"ta_store{k}") for k in range(2)]
            stored, pe_turn = sem("ta_stored"), sem("ta_pe_turn")
            xs = sb("xs", [128, 2, SUB, D], ctx=c)
            xts = sb("xts", [D, 2, GE], ctx=c)
            tabs = sb("tabs", [128, 2, 2, SUB * H], ctx=c)
            ps_t = [c.enter_context(nc.psum_tensor(f"ta_t{k}", [128, 512], fp32)) for k in range(2)]
            ps_p = [c.enter_context(nc.psum_tensor(f"ta_p{k}", [128, 512], fp32)) for k in range(4)]
            block = c.enter_context(stage_block(own))

            @block.vector
            def _(dve):
                dve.sem_inc(staged, CR)
                dve.sem_inc(tables_sb, CR)

                def step(i, k):
                    t = i * 2 + k
                    dve.wait_ge(turned, done(t - 2))
                    nc.vector.tensor_copy(xs[:, k], x_nm[:, bass.ds(t, 1)].rearrange("p a j f -> p (a j) f")).then_inc(staged, 1)
                    dve.wait_ge(stored, done(t - 2))
                    dve.wait_ge(product, done(t))
                    nc.vector.tensor_copy(tabs[:, k, 0, :], ps_p[2 * k][:, 0:SUB * H])
                    nc.vector.tensor_copy(tabs[:, k, 1, :], ps_p[2 * k + 1][:, 0:SUB * H]).then_inc(tables_sb, 1)
                rounds(dve, step, NT, 2)

            @block.tensor
            def _(pe):
                pe.sem_inc(turned, CR)
                pe.sem_inc(product, CR)

                def step(i, k):
                    t = i * 2 + k
                    pe.wait_ge(staged, done(t))
                    pe.wait_ge(turned_sb, done(t - 2))
                    pe.sem_inc(pe_turn, 1)
                    for j in range(SUB):
                        last = nc.tensor.transpose(ps_t[k][0:D, j * 128:(j + 1) * 128], xs[:, k, j, :], ident[:, :])
                    last.then_inc(turned, 1)
                    pe.wait_ge(turned_sb, done(t))
                    pe.wait_ge(tables_sb, done(t - 2))
                    for q in range(2):
                        for j in range(SUB):
                            last = nc.tensor.matmul(ps_p[2 * k + q][:, j * H:(j + 1) * H], xts[:, k, j * 128:(j + 1) * 128],
                                                    w_ab[:, q, :], start=True, stop=True)
                    last.then_inc(product, 1)
                rounds(pe, step, NT, 2)

            @block.scalar
            def _(act):
                act.sem_inc(turned_sb, CR)

                def step(i, k):
                    t = i * 2 + k
                    act.wait_ge(turned, done(t))
                    act.wait_ge(product, done(t - 2))
                    nc.scalar.copy(xts[:, k, :], ps_t[k][0:D, :]).then_inc(turned_sb, 1)
                rounds(act, step, NT, 2)

            @block.sync
            def _(sp):
                sp.sem_inc(stored, CR)

                def step(i, k):
                    t = sp.snap(i * 2 + k) if not isinstance(i, int) else i * 2 + k
                    sp.wait_ge(tables_sb, done(t))
                    sp.dma_start(group_rows(tab_a, t), tabs[:, k, 0, :]).then_inc(s_store[k], 16)
                    sp.dma_start(group_rows(tab_b, t), tabs[:, k, 1, :]).then_inc(s_store[k], 16)
                    sp.wait_ge(s_store[k], (i + 1) * 32)
                    sp.sem_inc(stored, 1)
                rounds(sp, step, NT, 2)

        with ExitStack() as c:
            sem, own = stage_semaphores(c, "")
            s_idx = [sem(f"l0_idx{k}") for k in range(4)]
            s_att = [sem(f"l0_att{k}") for k in range(4)]
            s_win = [sem(f"l0_win{k}") for k in range(4)]
            pe_turn = sem("l0_pe_turn")
            s_rows = [gather_sem(f"l0_rows{k}") for k in range(4)]
            pool_turn = sem("l0_pool_turn")
            combined, turned, turned_sb, hidden, hidden_sb, message, message_sb, summed, added = (
                sem(f"l0_{n}") for n in ("combined", "turned", "turned_sb", "hidden", "hidden_sb", "message", "message_sb", "summed", "added"))
            cleared, w_loaded = sem("l0_cleared"), sem("l0_w_loaded")
            idx = sb("l0_idx_t", [128, 4, SUB], i32, c)
            att = sb("l0_att_t", [128, 4, SUB, DE], ctx=c)
            rows = sb("l0_rows_t", [128, 4, SUB, H], ctx=c)
            comb = sb("l0_comb", [128, 4, SUB, DE + W], ctx=c)
            comb_t = sb("l0_comb_t", [DE + W, 2, GE], ctx=c)
            w_ew = sb("l0_w_ew", [DE + W, 4, H], ctx=c)
            hid = sb("l0_hid", [128, 2, GE], ctx=c)
            msg = sb("l0_msg", [128, 2, SUB, 1 + D], ctx=c)
            ps_t = [c.enter_context(nc.psum_tensor(f"l0_ps_t{k}", [128, 512], fp32)) for k in range(2)]
            ps_h = [c.enter_context(nc.psum_tensor(f"l0_ps_h{k}", [128, 512], fp32)) for k in range(2)]
            ps_m = [c.enter_context(nc.psum_tensor(f"l0_ps_m{k}", [128, 512], fp32)) for k in range(2)]
            ps_s = [c.enter_context(nc.psum_tensor(f"l0_ps_s{k}", [128, 512], fp32)) for k in range(2)]
            gen = general_path(c, sem, "l0", 1 + D, dst_pad, [(tab_a, src_pad, rows[:, 0]), (tab_b, dst_pad, rows[:, 1])], msg[:, 0], ps_s[0])
            gen_att, gen_turned, gen_turned_sb, gen_hidden, gen_hidden_sb, gen_product = (
                sem(f"l0_gen_{n}") for n in ("att", "turned", "turned_sb", "hidden", "hidden_sb", "product"))
            block = c.enter_context(stage_block(own))
            att_dram = P["edge_attr_32"]

            @block.sync
            def _(sp):
                for k in range(4):
                    sp.dma_start(w_ew[0:DE, k, :], P["L0_gnn_W_m1"][2 * D:2 * D + DE, :]).then_inc(w_loaded, 16)

                def general():
                    def load(g):
                        if isinstance(g, int):
                            sp.dma_start(att[0:TROWS, 0], att_dram[(NG - 1) * GE:E - TLEFT, :].rearrange("(p s) f -> p s f", s=SUB)).then_inc(gen_att, 16)
                            sp.dma_start(att[TROWS:TROWS + 1, 0, 0:TLEFT], att_dram[E - TLEFT:E, :].unsqueeze(0)).then_inc(gen_att, 16)
                        else:
                            sp.dma_start(att[:, 0].rearrange("p s f -> p (s f)"), group_rows(att_dram, g)).then_inc(gen_att, 16)
                    gen.sync(sp, load)

                def windows():
                    def step(i, k):
                        g = i * 4 + k
                        start = sp.value_load(base[0:1, bass.ds(g, 1)], min_val=0, max_val=N)
                        g = sp.snap(g) if not isinstance(g, int) else g
                        sp.wait_ge(message_sb, done(g - 4))
                        sp.dma_start(idx[:, k, :], group_rows(src_pad.unsqueeze(1), g)).then_inc(s_idx[k], 16)
                        if isinstance(i, int) and g == NG - 1:
                            sp.dma_start(att[0:TROWS, k], att_dram[(NG - 1) * GE:E - TLEFT, :].rearrange("(p s) f -> p s f", s=SUB)).then_inc(s_att[k], 16)
                            sp.dma_start(att[TROWS:TROWS + 1, k, 0:TLEFT], att_dram[E - TLEFT:E, :].unsqueeze(0)).then_inc(s_att[k], 16)
                        else:
                            sp.dma_start(att[:, k].rearrange("p s f -> p (s f)"), group_rows(att_dram, g)).then_inc(s_att[k], 16)
                        sp.dma_start(w_ew[DE:DE + W, k, :], tab_b[bass.ds(start, W), :]).then_inc(s_win[k], 16)
                    rounds(sp, step, NG, 4)

                by_flag(sp, general, windows)

            @block.gpsimd
            def _(pool):
                def general():
                    gen.gpsimd(pool)

                def windows():
                    def step(i, k):
                        pool.wait_ge(s_idx[k], (i + 1) * 16)
                        pool.sem_inc(pool_turn, 1)
                        for s in range(SUB):
                            nc.gpsimd.indirect_dma_start(
                                out=rows[:, k, s, :], out_offset=None, in_=tab_a,
                                in_offset=bass.IndirectOffsetOnAxis(ap=idx[:, k, s:s + 1], axis=0)).then_inc(s_rows[k], 16)
                    rounds(pool, step, NG, 4)

                by_flag(pool, general, windows)

            @block.vector
            def _(dve):
                nc.vector.memset(msg[:, :, :, 0:1], 1.0)
                nc.vector.memset(hid[64:128, :, :], 1.0).then_inc(cleared, 1)
                def general():
                    gen.vector(dve)

                def windows():
                    dve.sem_inc(combined, CR)
                    dve.sem_inc(added, CR)

                    def combine(i, k):
                        i, k = i + k // 4, k % 4
                        g = i * 4 + k
                        dve.wait_ge(summed, done(g - 4))
                        nc.vector.tensor_tensor(comb[:, k, :, DE:DE + W], iota_w[:, :, :],
                                                bc_last(rel[:, bass.ds(g, 1), :].rearrange("p a s -> p (a s)"), W), ALU.is_equal)
                        last = isinstance(i, int) and g == NG - 1
                        dve.wait_ge(s_att[k], (i + 1 + last) * 16)
                        nc.vector.tensor_copy(comb[:, k, :, 0:DE], att[:, k]).then_inc(combined, 1)

                    for k in range(4):
                        combine(0, k)

                    def step(i, k):
                        g = i * 4 + k
                        if not isinstance(i, int) or g + 4 < NG:
                            combine(i, k + 4) if not isinstance(i, int) or g + 4 < NG else None
                        start = dve.value_load(base[0:1, bass.ds(g, 1)], min_val=0, max_val=N)
                        dve.wait_ge(summed, done(g))
                        dve.wait_ge(added, done(g - 1))
                        nc.vector.tensor_tensor(acc[:, bass.ds(start, W)], acc[:, bass.ds(start, W)], ps_s[k % 2][0:D + 1, 0:W], ALU.add).then_inc(added, 1)

                    with dve.Fori(0, (NG - 4) // 4) as i:
                        for k in range(4):
                            step(i, k)
                    for k in range(NG - (NG - 4) // 4 * 4):
                        step((NG - 4) // 4 + k // 4, k % 4)

                by_flag(dve, general, windows)

            @block.tensor
            def _(pe):
                pe.wait_ge(w_loaded, 64)
                pe.wait_ge(cleared, 1)
                def general():
                    def make(g):
                        pe.wait_ge(gen_att, (g + 1 + isinstance(g, int)) * 16)
                        pe.sem_inc(pe_turn, 1)
                        for s in range(SUB):
                            last = nc.tensor.transpose(ps_t[0][0:DE, s * 128:(s + 1) * 128], att[:, 0, s, :], ident[:, :])
                        last.then_inc(gen_turned, 1)
                        pe.wait_ge(gen_turned_sb, g + 1)
                        pe.wait_ge(gen.gathered, (g + 1) * gen.rows_in)
                        pe.sem_inc(pe_turn, 1)
                        nc.tensor.matmul(ps_h[0][0:H, :], w_ew[0:DE, 0, :], comb_t[0:DE, 0, :], start=True, stop=False)
                        for n in range(2):
                            for s in range(SUB):
                                last = nc.tensor.matmul(ps_h[0][0:H, s * 128:(s + 1) * 128], rows[:, n, s, :], ident[:, :],
                                                        start=False, stop=n == 1 and s == SUB - 1)
                        last.then_inc(gen_hidden, 1)
                        pe.wait_ge(gen_hidden_sb, g + 1)
                        for s in range(SUB):
                            last = nc.tensor.matmul(ps_m[0][:, s * D:(s + 1) * D], hid[0:H + 1, 0, s * 128:(s + 1) * 128],
                                                    w_m2[:, :], start=True, stop=True)
                        last.then_inc(gen_product, 1)
                    gen.tensor(pe, make)

                def windows():
                    for s_ in (turned, hidden, message, summed):
                        pe.sem_inc(s_, CR)

                    def turn(i, k):
                        i, k = i + k // 4, k % 4
                        g = i * 4 + k
                        pe.wait_ge(combined, done(g))
                        pe.wait_ge(turned_sb, done(g - 2))
                        pe.sem_inc(pe_turn, 1)
                        for s in range(SUB):
                            last = nc.tensor.transpose(ps_t[k % 2][0:DE + W, s * 128:(s + 1) * 128], comb[:, k, s, :], ident[:, :])
                        last.then_inc(turned, 1)

                    def hide(i, k):
                        i, k = i + k // 4, k % 4
                        g = i * 4 + k
                        pe.wait_ge(turned_sb, done(g))
                        pe.wait_ge(hidden_sb, done(g - 2))
                        pe.wait_ge(s_win[k], (i + 1) * 16)
                        nc.tensor.matmul(ps_h[k % 2][0:H, :], w_ew[:, k, :], comb_t[:, k % 2, :], start=True, stop=False)
                        pe.wait_ge(s_rows[k], (i + 1) * 64)
                        for s in range(SUB):
                            last = nc.tensor.matmul(ps_h[k % 2][0:H, s * 128:(s + 1) * 128], rows[:, k, s, :], ident[:, :],
                                                    start=False, stop=s == SUB - 1)
                        last.then_inc(hidden, 1)

                    def messages(i, k):
                        i, k = i + k // 4, k % 4
                        g = i * 4 + k
                        pe.wait_ge(hidden_sb, done(g))
                        pe.wait_ge(message_sb, done(g - 2))
                        for s in range(SUB):
                            last = nc.tensor.matmul(ps_m[k % 2][:, s * D:(s + 1) * D], hid[0:H + 1, k % 2, s * 128:(s + 1) * 128],
                                                    w_m2[:, :], start=True, stop=True)
                        last.then_inc(message, 1)

                    def sums(i, k):
                        g = i * 4 + k
                        pe.wait_ge(message_sb, done(g))
                        pe.wait_ge(added, done(g - 2))
                        for s in range(SUB):
                            last = nc.tensor.matmul(ps_s[k % 2][0:D + 1, 0:W], msg[:, k % 2, s, :], comb[:, k, s, DE:DE + W],
                                                    start=s == 0, stop=s == SUB - 1)
                        last.then_inc(summed, 1)

                    for n in range(3):
                        turn(0, n)
                        if n >= 1:
                            hide(0, n - 1)
                        if n >= 2:
                            messages(0, n - 2)

                    def step(i, k):
                        g = i * 4 + k
                        loop = not isinstance(i, int)
                        sums(i, k)
                        if loop or g + 1 < NG:
                            messages(i, k + 1)
                        if loop or g + 2 < NG:
                            hide(i, k + 2)
                        if loop or g + 3 < NG:
                            turn(i, k + 3)
                    rounds(pe, step, NG, 4)

                by_flag(pe, general, windows)

            @block.scalar
            def _(act):
                act.wait_ge(cleared, 1)
                def general():
                    def step(g):
                        act.wait_ge(gen_turned, g + 1)
                        nc.scalar.copy(comb_t[0:DE, 0, :], ps_t[0][0:DE, :]).then_inc(gen_turned_sb, 1)
                        act.wait_ge(gen_hidden, g + 1)
                        nc.scalar.activation(hid[0:H, 0, :], ps_h[0][0:H, :], ACT.Gelu, bias=b_m1[:, :]).then_inc(gen_hidden_sb, 1)
                        act.wait_ge(gen_product, g + 1)
                        nc.scalar.activation(msg[:, 0, :, 1:1 + D], ps_m[0][:, 0:SUB * D].rearrange("p (s f) -> p s f", s=SUB),
                                             ACT.Gelu).then_inc(gen.message, 1)
                    gen.each_group(act, step)

                def windows():
                    for s_ in (turned_sb, hidden_sb, message_sb):
                        act.sem_inc(s_, CR)

                    def copy_turned(i, k):
                        g = i * 4 + k
                        act.wait_ge(turned, done(g))
                        act.wait_ge(hidden, done(g - 2))
                        nc.scalar.copy(comb_t[:, k % 2, :], ps_t[k % 2][0:DE + W, :]).then_inc(turned_sb, 1)

                    def gelu_hidden(i, k):
                        g = i * 4 + k
                        act.wait_ge(hidden, done(g))
                        act.wait_ge(message, done(g - 2))
                        nc.scalar.activation(hid[0:H, k % 2, :], ps_h[k % 2][0:H, :], ACT.Gelu, bias=b_m1[:, :]).then_inc(hidden_sb, 1)

                    def gelu_message(i, k):
                        g = i * 4 + k
                        act.wait_ge(message, done(g))
                        act.wait_ge(summed, done(g - 2))
                        nc.scalar.activation(msg[:, k % 2, :, 1:1 + D], ps_m[k % 2][:, 0:SUB * D].rearrange("p (s f) -> p s f", s=SUB),
                                             ACT.Gelu).then_inc(message_sb, 1)

                    for n in range(3):
                        copy_turned(0, n)
                        if n >= 1:
                            gelu_hidden(0, n - 1)
                        if n >= 2:
                            gelu_message(0, n - 2)

                    def step(i, k):
                        g = i * 4 + k
                        loop = not isinstance(i, int)
                        if loop or g + 1 < NG:
                            gelu_message(i, k + 1)
                        if loop or g + 2 < NG:
                            gelu_hidden(i, k + 2)
                        if loop or g + 3 < NG:
                            copy_turned(i, k + 3)
                    rounds(act, step, NG, 4)

                by_flag(act, general, windows)

        def layer_norm(dve, act_done, act_turn, link, z, mid, sums, squares):
            link(nc.vector.tensor_reduce(sums, z, AX.X, ALU.add))
            link(nc.vector.tensor_scalar(sums, sums, 1.0 / D, None, ALU.mult))
            link(nc.vector.tensor_tensor(z, z, bc_last(sums, D), ALU.subtract))
            link(nc.vector.tensor_tensor(mid, z, z, ALU.mult))
            link(nc.vector.tensor_reduce(squares, mid, AX.X, ALU.add))
            nc.vector.tensor_scalar(squares, squares, 1.0 / D, EPS, ALU.mult, ALU.add).then_inc(act_turn, 1)
            dve.wait_ge(act_done, 1)
            link(nc.vector.reciprocal(squares, squares))
            link(nc.vector.tensor_tensor(z, z, bc_last(squares, D), ALU.mult))

        def flat(ap):
            return ap.rearrange("p t j f -> p (t j) f")

        def block_of(ap, t):
            return ap[:, bass.ds(t, 1)].rearrange("p a j f -> p (a j) f")

        def per_node(ap, t):
            return ap[:, bass.ds(t, 1)].rearrange("p a j -> p (a j)")

        def strided(ap):
            return ap.rearrange("r (p j) -> r j p", j=SUB)

        def halves(ap):
            return ap.rearrange("r (j p) -> r j p", j=SUB)

        with ExitStack() as c:
            sem, own = stage_semaphores(c, "n0_")
            staged, turned, turned_sb, hidden, hidden_sb, product, product_sb, summed = (
                sem(n) for n in ("staged", "turned", "turned_sb", "hidden", "hidden_sb", "product", "product_sb", "summed"))
            pe_turn, ones_set, chain, root_in, root_out, s_cnt = sem("pe_turn"), sem("ones_set"), sem("chain"), sem("root_in"), sem("root_out"), sem("cnt")
            top_lanes, top_all = sem("top_lanes"), sem("top_all")
            top = sb("n0_top", [128, 1], ctx=c)
            xs = sb("n0_xs", [128, 2, SUB, D], ctx=c)
            xts = sb("n0_xts", [D, 2, GE], ctx=c)
            hid = sb("n0_hid", [HC + 1, 2, GE], ctx=c)
            comb = sb("n0_comb", [128, 2, SUB, D], ctx=c)
            sums, squares = sb("n0_sums", [128, NT * SUB], ctx=c), sb("n0_squares", [128, NT * SUB], ctx=c)
            mid = sb("n0_mid", [128, NT * SUB, D], ctx=c)
            ps_t = [c.enter_context(nc.psum_tensor(f"n0_t{k}", [128, 512], fp32)) for k in range(2)]
            ps_h = [c.enter_context(nc.psum_tensor(f"n0_h{k}", [128, 512], fp32)) for k in range(2)]
            ps_p = [c.enter_context(nc.psum_tensor(f"n0_p{k}", [128, 512], fp32)) for k in range(2)]
            block = c.enter_context(stage_block(own))

            @block.sync
            def _(sp):
                sp.dma_start(cnt_dram.unsqueeze(0), acc[0:1, :]).then_inc(s_cnt, 16)
                sp.wait_ge(s_cnt, 16)
                sp.dma_start(cnt_nm[:, :, :], cnt_dram.rearrange("(t p j) -> p t j", p=LANES, j=SUB)).then_inc(s_cnt, 16)
                sp.wait_ge(s_cnt, 32)

            @block.tensor
            def _(pe):
                for s_ in (turned, hidden, product):
                    pe.sem_inc(s_, CR)
                pe.wait_ge(ones_set, 1)

                def step(i, k):
                    t = i * 2 + k
                    pe.wait_ge(staged, done(t))
                    pe.wait_ge(turned_sb, done(t - 2))
                    pe.sem_inc(pe_turn, 1)
                    for j in range(SUB):
                        last = nc.tensor.transpose(ps_t[k][0:D, j * 128:(j + 1) * 128], xs[:, k, j, :], ident[:, :])
                    last.then_inc(turned, 1)
                    pe.wait_ge(hidden_sb, done(t - 2))
                    nc.tensor.matmul(ps_h[k][0:HC, :], w_c1a[:, :], strided(acc[:, bass.ds(t * GE, GE)]), start=True, stop=False)
                    pe.wait_ge(turned_sb, done(t))
                    nc.tensor.matmul(ps_h[k][0:HC, :], w_c1x[:, :], xts[:, k, :], start=False, stop=True).then_inc(hidden, 1)
                    pe.wait_ge(hidden_sb, done(t))
                    pe.wait_ge(product_sb, done(t - 2))
                    for j in range(SUB):
                        last = nc.tensor.matmul(ps_p[k][:, j * D:(j + 1) * D], hid[:, k, j * 128:(j + 1) * 128], w_c2[:, :], start=True, stop=True)
                    last.then_inc(product, 1)
                rounds(pe, step, NT, 2)

            @block.scalar
            def _(act):
                for s_ in (turned_sb, hidden_sb, product_sb):
                    act.sem_inc(s_, CR)

                def step(i, k):
                    t = i * 2 + k
                    act.wait_ge(turned, done(t))
                    act.wait_ge(hidden, done(t - 2))
                    nc.scalar.copy(xts[:, k, :], ps_t[k][0:D, :]).then_inc(turned_sb, 1)
                    act.wait_ge(hidden, done(t))
                    act.wait_ge(product, done(t - 2))
                    nc.scalar.activation(hid[0:HC, k, :], ps_h[k][0:HC, :], ACT.Gelu, bias=b_c1[:, :]).then_inc(hidden_sb, 1)
                    act.wait_ge(product, done(t))
                    act.wait_ge(summed, done(t - 2))
                    nc.scalar.activation(comb[:, k].rearrange("p j f -> p (j f)"), ps_p[k][:, 0:SUB * D], ACT.Gelu).then_inc(product_sb, 1)
                rounds(act, step, NT, 2)
                act.wait_ge(root_in, 1)
                nc.scalar.activation(squares[:, :], squares[:, :], ACT.Sqrt).then_inc(root_out, 1)
                act.wait_ge(root_in, 2)
                nc.scalar.activation(dinv_nm[:, :, :], dinv_nm[:, :, :], ACT.Sqrt).then_inc(root_out, 1)

            @block.vector
            def _(dve):
                link = linker(dve, chain)
                nc.vector.memset(hid[HC:HC + 1, :, :], 1.0).then_inc(ones_set, 1)
                dve.sem_inc(staged, CR)
                dve.sem_inc(summed, CR)

                def step(i, k):
                    t = i * 2 + k
                    dve.wait_ge(turned, done(t - 2))
                    nc.vector.tensor_copy(xs[:, k], block_of(x_nm, t)).then_inc(staged, 1)
                    dve.wait_ge(product_sb, done(t))
                    nc.vector.scalar_tensor_tensor(out=block_of(z_nm, t), in0=block_of(x_nm, t), scalar=2.0, in1=comb[:, k],
                                                   op0=ALU.mult, op1=ALU.add).then_inc(summed, 1)
                rounds(dve, step, NT, 2)
                dve.wait_ge(summed, done(NT - 1))
                layer_norm(dve, root_out, root_in, link, flat(z_nm), mid[:, :, :], sums[:, :], squares[:, :])
                dve.wait_ge(s_cnt, 32)
                nc.vector.tensor_scalar(dinv_nm[:, :, :], cnt_nm[:, :, :], 1.0, None, ALU.add).then_inc(root_in, 1)
                dve.wait_ge(root_out, 2)
                link(nc.vector.reciprocal(dinv_nm[:, :, :], dinv_nm[:, :, :]))
                nc.vector.tensor_reduce(top[:, :], cnt_nm[:, :, :].rearrange("p t j -> p (t j)"), AX.X, ALU.max).then_inc(top_lanes, 1)
                dve.wait_ge(top_all, 1)
                link(nc.vector.tensor_scalar(top[:, :], top[:, :], float(DEG_MAX), None, ALU.is_gt))
                link(nc.vector.tensor_tensor(flag_f[:, :], flag_f[:, :], top[0:1, :], ALU.max))
                nc.vector.tensor_copy(flag[:, :], flag_f[:, :])

            @block.gpsimd
            def _(pool):
                pool.wait_ge(top_lanes, 1)
                pool.partition_all_reduce(top[:, :], top[:, :], 128, bass.bass_isa.ReduceOp.max).then_inc(top_all, 1)

        dinv_ctx = ExitStack()
        whole.enter_context(dinv_ctx)
        dinv_bc = sb("dinv_bc", [128, NP], ctx=dinv_ctx)
        with ExitStack() as c:
            sem, own = stage_semaphores(c, "g1_")
            made, turned, in_acc, stored, pe_turn = (sem(n) for n in ("made", "turned", "in_acc", "stored", "pe_turn"))
            s_store = [sem(f"store{k}") for k in range(2)]
            s_cnt, deg_ready, root = sem("cnt"), sem("deg_ready"), sem("root")
            ys = sb("g1_ys", [128, 2, SUB, D], ctx=c)
            ps_y = [c.enter_context(nc.psum_tensor(f"g1_y{k}", [128, 512], fp32)) for k in range(2)]
            block = c.enter_context(stage_block(own))

            @block.sync
            def _(sp):
                sp.sem_inc(stored, CR)
                sp.dma_start(dinv_bc[:, :], cnt_dram.unsqueeze(0).to_broadcast([128, NP])).then_inc(s_cnt, 16)

                def step(i, k):
                    t = sp.snap(i * 2 + k) if not isinstance(i, int) else i * 2 + k
                    sp.wait_ge(made, done(t))
                    sp.dma_start(group_rows(tab_y1, t), ys[:, k].rearrange("p j f -> p (j f)")).then_inc(s_store[k], 16)
                    sp.wait_ge(s_store[k], (i + 1) * 16)
                    sp.sem_inc(stored, 1)
                rounds(sp, step, NT, 2)

            @block.vector
            def _(dve):
                dve.sem_inc(made, CR)

                def step(i, k):
                    t = i * 2 + k
                    dve.wait_ge(turned, done(t - 2))
                    dve.wait_ge(stored, done(t - 2))
                    nc.vector.tensor_tensor(ys[:, k], block_of(z_nm, t), bc_last(per_node(dinv_nm, t), D), ALU.mult).then_inc(made, 1)
                rounds(dve, step, NT, 2)
                dve.wait_ge(s_cnt, 16)
                nc.vector.tensor_scalar(dinv_bc[:, :], dinv_bc[:, :], 1.0, None, ALU.add).then_inc(deg_ready, 1)
                dve.wait_ge(root, 1)
                nc.vector.reciprocal(dinv_bc[:, :], dinv_bc[:, :])

            @block.tensor
            def _(pe):
                pe.sem_inc(turned, CR)

                def step(i, k):
                    t = i * 2 + k
                    pe.wait_ge(made, done(t))
                    pe.wait_ge(in_acc, done(t - 2))
                    pe.sem_inc(pe_turn, 1)
                    for j in range(SUB):
                        last = nc.tensor.transpose(ps_y[k][0:D, j * 128:(j + 1) * 128], ys[:, k, j, :], ident[:, :])
                    last.then_inc(turned, 1)
                rounds(pe, step, NT, 2)

            @block.scalar
            def _(act):
                act.sem_inc(in_acc, CR)

                def step(i, k):
                    t = i * 2 + k
                    act.wait_ge(turned, done(t))
                    nc.scalar.copy(strided(acc[0:D, bass.ds(t * GE, GE)]), halves(ps_y[k][0:D, :])).then_inc(in_acc, 1)
                rounds(act, step, NT, 2)
                act.wait_ge(deg_ready, 1)
                nc.scalar.activation(dinv_bc[:, :], dinv_bc[:, :], ACT.Sqrt).then_inc(root, 1)

        def gcn_sums(name, tab):
            with ExitStack() as c:
                sem, own = stage_semaphores(c, f"{name}_")
                s_idx = [sem(f"idx{k}") for k in range(4)]
                s_rows = [gather_sem(f"{name}_rows{k}") for k in range(4)]
                pool_turn, hot, summed, added = (sem(n) for n in ("pool_turn", "hot", "summed", "added"))
                idx = sb(f"{name}_idx", [128, 4, SUB], i32, c)
                rows = sb(f"{name}_rows", [128, 4, SUB, D], ctx=c)
                onehot = sb(f"{name}_onehot", [128, 4, SUB, W], ctx=c)
                ps_s = [c.enter_context(nc.psum_tensor(f"{name}_s{k}", [128, 512], fp32)) for k in range(2)]
                gen = general_path(c, sem, name, D, dst_pad, [(tab, src_pad, rows[:, 0])], rows[:, 0], ps_s[0])
                s_counts = [sem(f"counts{k}") for k in range(4)]
                keys_set, keys_hot, counted, counted_sb, carried, iota_set, sp_turn = (
                    sem(n) for n in ("keys_set", "keys_hot", "counted", "counted_sb", "carried", "iota_set", "sp_turn"))
                iota_k = sb(f"{name}_iota_k", [128, KEYS], fp16, c)
                keys = sb(f"{name}_keys", [128, 2, 2, SUB], ctx=c)
                hot_lane = sb(f"{name}_hot_lane", [128, 2, SUB, LANES], fp16, c)
                hot_key = sb(f"{name}_hot_key", [128, 2, SUB, KEYS], fp16, c)
                win_counts = sb(f"{name}_win_counts", [128, 4, KEYS], bf16, c)
                ps_c = [c.enter_context(nc.psum_tensor(f"{name}_c{k}", [128, KB, 512], fp32)) for k in range(2)]
                block = c.enter_context(stage_block(own))

                @block.sync
                def _(sp):
                    def general():
                        gen.sync(sp)

                    def windows():
                        def step(i, k):
                            g = sp.snap(i * 4 + k) if not isinstance(i, int) else i * 4 + k
                            sp.wait_ge(summed, done(g - 4))
                            sp.dma_start(idx[:, k, :], group_rows(src_pad.unsqueeze(1), g)).then_inc(s_idx[k], 16)
                            if isinstance(g, int) and g == 0:
                                return
                            write(i, k - 1) if k else write(i - 1, 3)

                        def write(i, k):
                            start = sp.snap(sp.value_load(base[0:1, bass.ds(i * 4 + k, 1)], min_val=0, max_val=N))
                            at = sp.snap(i * 4 + k) if not isinstance(i, int) else i * 4 + k
                            sp.wait_ge(carried, done(at))
                            if not isinstance(at, int) or at:
                                sp.sem_inc(sp_turn, 1)
                                sp.wait_ge(s_counts[(k - 1) % 4], (i + 1 if k else i) * 16)
                            sp.dma_start(counts[:, bass.ds(start, W), :].rearrange("p d h -> p (d h)"), win_counts[:, k, :]).then_inc(s_counts[k], 16)

                        peeled(sp, step, NG, 4)
                        write(NG // 4, NG % 4 - 1)
                        sp.wait_ge(s_counts[NG % 4 - 1], (NG // 4 + 1) * 16)

                    by_flag(sp, general, windows)

                @block.gpsimd
                def _(pool):
                    pool.iota(iota_k[:, :], pattern=[[1, KEYS]], base=0, channel_multiplier=0,
                              allow_small_or_imprecise_dtypes=True).then_inc(iota_set, 1)

                    def general():
                        gen.gpsimd(pool)

                    def windows():
                        def step(i, k):
                            pool.wait_ge(s_idx[k], (i + 1) * 16)
                            pool.sem_inc(pool_turn, 1)
                            for s in range(SUB):
                                nc.gpsimd.indirect_dma_start(
                                    out=rows[:, k, s, :], out_offset=None, in_=tab,
                                    in_offset=bass.IndirectOffsetOnAxis(ap=idx[:, k, s:s + 1], axis=0)).then_inc(s_rows[k], 16)
                        rounds(pool, step, NG, 4)

                    by_flag(pool, general, windows)

                @block.vector
                def _(dve):
                    def general():
                        gen.vector(dve)

                    def windows():
                        for s_ in (hot, added, keys_set, keys_hot, carried):
                            dve.sem_inc(s_, CR)
                        dve.wait_ge(iota_set, 1)

                        def prepare(i, k):
                            i, k = i + k // 4, k % 4
                            g = i * 4 + k
                            here = rel[:, bass.ds(g, 1), :].rearrange("p a s -> p (a s)")
                            dve.wait_ge(summed, done(g - 4))
                            nc.vector.tensor_tensor(onehot[:, k], iota_w[:, :, :], bc_last(here, W), ALU.is_equal).then_inc(hot, 1)
                            dve.wait_ge(keys_hot, done(g - 2))
                            nc.vector.tensor_copy(keys[:, k % 2, 0, :], lane_f[:, bass.ds(g, 1), :].rearrange("p a s -> p (a s)"))
                            nc.vector.tensor_copy(keys[:, k % 2, 1, :], key_f[:, bass.ds(g, 1), :].rearrange("p a s -> p (a s)")).then_inc(keys_set, 1)
                            dve.wait_ge(counted, done(g - 2))
                            dve.wait_ge(keys_set, done(g))
                            for s in range(SUB):
                                nc.vector.tensor_scalar(hot_lane[:, k % 2, s, :], iota_k[:, 0:LANES], keys[:, k % 2, 0, s:s + 1], None, ALU.is_equal)
                                last = nc.vector.tensor_scalar(hot_key[:, k % 2, s, :], iota_k[:, :], keys[:, k % 2, 1, s:s + 1], None, ALU.is_equal)
                            last.then_inc(keys_hot, 1)
                        prepare(0, 0)

                        def step(i, k):
                            g = i * 4 + k
                            if not isinstance(i, int) or g + 1 < NG:
                                prepare(i, k + 1)
                            if isinstance(g, int) and g == 0:
                                dve.wait_ge(counted_sb, done(0))
                                dve.sem_inc(carried, 1)
                            else:
                                before = dve.value_load(hop[0:1, bass.ds(g, 1)], min_val=0, max_val=(W - 1) * HI)
                                dve.wait_ge(counted_sb, done(g))
                                dve.wait_ge(carried, done(g - 1))
                                nc.vector.tensor_tensor(win_counts[:, k, 0:HI], win_counts[:, k, 0:HI],
                                                        win_counts[:, (k - 1) % 4, bass.ds(before, HI)], ALU.add).then_inc(carried, 1)
                            start = dve.value_load(base[0:1, bass.ds(g, 1)], min_val=0, max_val=N)
                            dve.wait_ge(summed, done(g))
                            dve.wait_ge(added, done(g - 1))
                            nc.vector.tensor_tensor(acc[0:D, bass.ds(start, W)], acc[0:D, bass.ds(start, W)], ps_s[k % 2][0:D, 0:W], ALU.add).then_inc(added, 1)
                        peeled(dve, step, NG, 4)

                    by_flag(dve, general, windows)

                @block.scalar
                def _(act):
                    def general():
                        act.sem_inc(counted_sb, 1)

                    def windows():
                        act.sem_inc(counted_sb, CR)

                        def step(i, k):
                            g = i * 4 + k
                            act.wait_ge(counted, done(g))
                            act.wait_ge(carried, done(g - 3))
                            if not isinstance(g, int) or g >= 4:
                                act.wait_ge(s_counts[k], i * 16)
                            nc.scalar.copy(win_counts[:, k, :].rearrange("p (b w) -> p b w", b=KB), ps_c[k % 2][:, :, 0:KW]).then_inc(counted_sb, 1)
                        peeled(act, step, NG, 4)

                    by_flag(act, general, windows)

                @block.tensor
                def _(pe):
                    def general():
                        gen.tensor(pe)

                    def windows():
                        pe.sem_inc(summed, CR)
                        pe.sem_inc(counted, CR)

                        def step(i, k):
                            g = i * 4 + k
                            pe.wait_ge(keys_hot, done(g))
                            pe.wait_ge(counted_sb, done(g - 2))
                            for s in range(SUB):
                                for b in range(KB):
                                    last = nc.tensor.matmul(ps_c[k % 2][:, b, 0:KW], hot_lane[:, k % 2, s, :],
                                                            hot_key[:, k % 2, s, b * KW:(b + 1) * KW], start=s == 0, stop=s == SUB - 1)
                            last.then_inc(counted, 1)
                            pe.wait_ge(hot, done(g))
                            pe.wait_ge(added, done(g - 2))
                            pe.wait_ge(s_rows[k], (i + 1) * 64)
                            for s in range(SUB):
                                last = nc.tensor.matmul(ps_s[k % 2][0:D, 0:W], rows[:, k, s, :], onehot[:, k, s, :], start=s == 0, stop=s == SUB - 1)
                            last.then_inc(summed, 1)
                        rounds(pe, step, NG, 4)

                    by_flag(pe, general, windows)

        gcn_sums("gs1", tab_y1)

        with ExitStack() as c:
            sem, own = stage_semaphores(c, "g2_")
            wide, scaled, hidden, product, made, turned, in_acc, stored, pe_turn = (
                sem(n) for n in ("wide", "scaled", "hidden", "product", "made", "turned", "in_acc", "stored", "pe_turn"))
            s_store = [sem(f"store{k}") for k in range(2)]
            us = sb("g2_us", [H1, 2, GE], ctx=c)
            hid = sb("g2_hid", [H1, 2, GE], ctx=c)
            ys = sb("g2_ys", [128, 2, SUB, D], ctx=c)
            ps_u = [c.enter_context(nc.psum_tensor(f"g2_u{k}", [128, 512], fp32)) for k in range(2)]
            ps_p = [c.enter_context(nc.psum_tensor(f"g2_p{k}", [128, 512], fp32)) for k in range(2)]
            ps_y = [c.enter_context(nc.psum_tensor(f"g2_y{k}", [128, 512], fp32)) for k in range(2)]
            block = c.enter_context(stage_block(own))

            @block.tensor
            def _(pe):
                for s_ in (wide, product, turned):
                    pe.sem_inc(s_, CR)

                def step(i, k):
                    t = i * 2 + k
                    pe.wait_ge(scaled, done(t - 2))
                    nc.tensor.matmul(ps_u[k][0:H1, :], w_g1[:, :], acc[0:D, bass.ds(t * GE, GE)], start=True, stop=True).then_inc(wide, 1)
                    pe.wait_ge(hidden, done(t))
                    pe.wait_ge(made, done(t - 2))
                    for j in range(SUB):
                        last = nc.tensor.matmul(ps_p[k][:, j * D:(j + 1) * D], strided(hid[:, k, :])[:, j, :], w_g2[:, :], start=True, stop=True)
                    last.then_inc(product, 1)
                    pe.wait_ge(made, done(t))
                    pe.wait_ge(in_acc, done(t - 2))
                    pe.sem_inc(pe_turn, 1)
                    for j in range(SUB):
                        last = nc.tensor.transpose(ps_y[k][0:D, j * 128:(j + 1) * 128], ys[:, k, j, :], ident[:, :])
                    last.then_inc(turned, 1)
                rounds(pe, step, NT, 2)

            @block.vector
            def _(dve):
                dve.sem_inc(scaled, CR)
                dve.sem_inc(made, CR)

                def step(i, k):
                    t = i * 2 + k
                    dve.wait_ge(wide, done(t))
                    dve.wait_ge(hidden, done(t - 2))
                    nc.vector.tensor_tensor(us[:, k, :], ps_u[k][0:H1, :], dinv_bc[0:H1, bass.ds(t * GE, GE)], ALU.mult).then_inc(scaled, 1)
                    dve.wait_ge(product, done(t))
                    dve.wait_ge(turned, done(t - 2))
                    dve.wait_ge(stored, done(t - 2))
                    nc.vector.tensor_tensor(ys[:, k], ps_p[k][:, 0:SUB * D].rearrange("p (j f) -> p j f", j=SUB),
                                            bc_last(per_node(dinv_nm, t), D), ALU.mult).then_inc(made, 1)
                rounds(dve, step, NT, 2)

            @block.scalar
            def _(act):
                act.sem_inc(hidden, CR)
                act.sem_inc(in_acc, CR)

                def step(i, k):
                    t = i * 2 + k
                    act.wait_ge(scaled, done(t))
                    act.wait_ge(product, done(t - 2))
                    nc.scalar.activation(hid[:, k, :], us[:, k, :], ACT.Relu, bias=b_g1[:, :]).then_inc(hidden, 1)
                    act.wait_ge(turned, done(t))
                    nc.scalar.copy(strided(acc[0:D, bass.ds(t * GE, GE)]), halves(ps_y[k][0:D, :])).then_inc(in_acc, 1)
                rounds(act, step, NT, 2)

            @block.sync
            def _(sp):
                sp.sem_inc(stored, CR)

                def step(i, k):
                    t = sp.snap(i * 2 + k) if not isinstance(i, int) else i * 2 + k
                    sp.wait_ge(made, done(t))
                    sp.dma_start(group_rows(tab_y2, t), ys[:, k].rearrange("p j f -> p (j f)")).then_inc(s_store[k], 16)
                    sp.wait_ge(s_store[k], (i + 1) * 16)
                    sp.sem_inc(stored, 1)
                rounds(sp, step, NT, 2)

        def split(link, whole_, parts, rest):
            link(nc.vector.tensor_copy(parts[0], whole_))
            link(nc.vector.tensor_tensor(rest, whole_, parts[0], ALU.subtract))
            link(nc.vector.tensor_copy(parts[1], rest))
            link(nc.vector.tensor_tensor(rest, rest, parts[1], ALU.subtract))
            link(nc.vector.tensor_copy(parts[2], rest))

        with ExitStack() as c:
            sem, own = stage_semaphores(c, "gs2_")
            s_y, split_done, chain, summed, added, reduced = (sem(n) for n in ("s_y", "split_done", "chain", "summed", "added", "reduced"))
            s_block = [sem(f"block{k}") for k in range(2)]
            y_parts = sb("gs2_y_parts", [128, 3, HI, D], bf16, c)
            block_counts = sb("gs2_block_counts", [128, 2, DB, HI], bf16, c)
            block_deg = sb("gs2_block_deg", [128, HI], ctx=c)
            rows = sb("gs2_rows", [128, SUB, D], ctx=c)
            ps = [c.enter_context(nc.psum_tensor(f"gs2_ps{k}", [128, 512], fp32)) for k in range(2)]
            gen = general_path(c, sem, "gs2", D, dst_pad, [(tab_y2, src_pad, rows[:, :, :])], rows, ps[0])
            block = c.enter_context(stage_block(own))

            @block.sync
            def _(sp):
                def general():
                    gen.sync(sp)

                def dense():
                    sp.sem_inc(s_y, 1)
                    sp.dma_start(x_nm[:, :, :, :].rearrange("p t j f -> p t (j f)"),
                                 tab_y2[0:NP, :].rearrange("(t p j) f -> p t (j f)", p=LANES, j=SUB)).then_inc(s_y, 16)

                    def step(i, k):
                        b = sp.snap(i * 2 + k) if not isinstance(i, int) else i * 2 + k
                        sp.wait_ge(summed, done(b - 2))
                        sp.wait_ge(reduced, done(b - 2))
                        sp.dma_start(block_counts[:, k].rearrange("p d h -> p (d h)"),
                                     destinations(b, DB)).then_inc(s_block[k], 16)
                    rounds(sp, step, NDB, 2)

                by_flag(sp, general, dense)

            @block.gpsimd
            def _(pool):
                by_flag(pool, lambda: gen.gpsimd(pool), lambda: pool.sem_inc(gen.turn, 1))

            @block.vector
            def _(dve):
                def general():
                    gen.vector(dve)

                def dense():
                    link = linker(dve, chain)
                    for s_ in (added, reduced):
                        dve.sem_inc(s_, CR)
                    link(nc.vector.memset(deg_nm[:, :], 0.0))
                    dve.wait_ge(s_y, 17)
                    y = flat(x_nm)
                    split(link, y, [y_parts[:, q] for q in range(3)], y)
                    dve.sem_inc(split_done, 1)

                    def step(i, k):
                        b = i * 2 + k
                        dve.wait_ge(s_block[k], (i + 1) * 16)
                        nc.vector.tensor_reduce(block_deg[:, :], block_counts[:, k].rearrange("p d h -> p h d"), AX.X, ALU.add).then_inc(reduced, 1)
                        dve.wait_ge(reduced, done(b))
                        nc.vector.tensor_tensor(deg_nm[:, :], deg_nm[:, :], block_deg[:, :], ALU.add)
                        dve.wait_ge(summed, done(b))
                        at = acc[0:D, bass.ds(b * DB, DB)]
                        nc.vector.tensor_tensor(at, at, ps[k][0:D, 0:DB], ALU.add).then_inc(added, 1)
                        dve.wait_ge(added, done(b))
                    rounds(dve, step, NDB, 2)

                by_flag(dve, general, dense)

            @block.tensor
            def _(pe):
                def general():
                    gen.tensor(pe)

                def dense():
                    pe.sem_inc(summed, CR)
                    pe.wait_ge(split_done, 1)

                    def step(i, k):
                        b = i * 2 + k
                        pe.wait_ge(added, done(b - 2))
                        pe.wait_ge(s_block[k], (i + 1) * 16)
                        for h in range(HI):
                            for q in range(3):
                                last = nc.tensor.matmul(ps[k][0:D, 0:DB], y_parts[:, q, h, :], block_counts[:, k, :, h],
                                                        start=h == 0 and q == 0, stop=h == HI - 1 and q == 2)
                        last.then_inc(summed, 1)
                    rounds(pe, step, NDB, 2)

                by_flag(pe, general, dense)

        with ExitStack() as c:
            sem, own = stage_semaphores(c, "g3_")
            scaled, turned, summed, pe_turn, chain, root_in, root_out = (
                sem(n) for n in ("scaled", "turned", "summed", "pe_turn", "chain", "root_in", "root_out"))
            us = sb("g3_us", [D, 2, GE], ctx=c)
            sums, squares = sb("g3_sums", [128, NT * SUB], ctx=c), sb("g3_squares", [128, NT * SUB], ctx=c)
            mid = sb("g3_mid", [128, NT * SUB, D], ctx=c)
            ps_z = [c.enter_context(nc.psum_tensor(f"g3_z{k}", [128, 512], fp32)) for k in range(2)]
            block = c.enter_context(stage_block(own))

            @block.vector
            def _(dve):
                link = linker(dve, chain)
                dve.sem_inc(scaled, CR)
                dve.sem_inc(summed, CR)

                def step(i, k):
                    t = i * 2 + k
                    dve.wait_ge(turned, done(t - 2))
                    nc.vector.tensor_tensor(us[:, k, :], acc[0:D, bass.ds(t * GE, GE)], dinv_bc[0:D, bass.ds(t * GE, GE)], ALU.mult).then_inc(scaled, 1)
                    dve.wait_ge(turned, done(t))
                    nc.vector.tensor_tensor(block_of(x_nm, t), ps_z[k][:, 0:SUB * D].rearrange("p (j f) -> p j f", j=SUB), block_of(z_nm, t), ALU.add).then_inc(summed, 1)
                rounds(dve, step, NT, 2)
                dve.wait_ge(summed, done(NT - 1))
                link(nc.vector.tensor_tensor(flat(x_nm), flat(x_nm), b_g2[:, :].unsqueeze(1).to_broadcast([128, NT * SUB, D]), ALU.add))
                layer_norm(dve, root_out, root_in, link, flat(x_nm), mid[:, :, :], sums[:, :], squares[:, :])

            @block.tensor
            def _(pe):
                pe.sem_inc(turned, CR)

                def step(i, k):
                    t = i * 2 + k
                    pe.wait_ge(scaled, done(t))
                    pe.wait_ge(summed, done(t - 2))
                    pe.sem_inc(pe_turn, 1)
                    for j in range(SUB):
                        last = nc.tensor.transpose(ps_z[k][:, j * D:(j + 1) * D], strided(us[:, k, :])[:, j, :], ident[0:D, 0:D])
                    last.then_inc(turned, 1)
                rounds(pe, step, NT, 2)

            @block.scalar
            def _(act):
                act.wait_ge(root_in, 1)
                nc.scalar.activation(squares[:, :], squares[:, :], ACT.Sqrt).then_inc(root_out, 1)
        dinv_ctx.close()

        x_t = sb("x_t", [D, NP])
        with ExitStack() as c:
            sem, own = stage_semaphores(c, "e0_")
            staged, turned, turned_sb, product, made, stored, pe_turn = (
                sem(n) for n in ("staged", "turned", "turned_sb", "product", "made", "stored", "pe_turn"))
            s_store = [sem(f"store{k}") for k in range(2)]
            xs = sb("e0_xs", [128, 2, SUB, D], ctx=c)
            xts = sb("e0_xts", [D, 2, GE], ctx=c)
            ys = sb("e0_ys", [128, 2, SUB, D], ctx=c)
            ps_t = [c.enter_context(nc.psum_tensor(f"e0_t{k}", [128, 512], fp32)) for k in range(2)]
            ps_p = [c.enter_context(nc.psum_tensor(f"e0_p{k}", [128, 512], fp32)) for k in range(2)]
            block = c.enter_context(stage_block(own))

            @block.vector
            def _(dve):
                dve.sem_inc(staged, CR)
                dve.sem_inc(made, CR)
                nc.vector.memset(acc[:, :], 0.0)

                def step(i, k):
                    t = i * 2 + k
                    dve.wait_ge(turned, done(t - 2))
                    nc.vector.tensor_copy(xs[:, k], block_of(x_nm, t)).then_inc(staged, 1)
                    dve.wait_ge(product, done(t))
                    dve.wait_ge(stored, done(t - 2))
                    nc.vector.tensor_copy(ys[:, k].rearrange("p j f -> p (j f)"), ps_p[k][:, 0:SUB * D]).then_inc(made, 1)
                rounds(dve, step, NT, 2)

            @block.tensor
            def _(pe):
                pe.sem_inc(turned, CR)
                pe.sem_inc(product, CR)

                def step(i, k):
                    t = i * 2 + k
                    pe.wait_ge(staged, done(t))
                    pe.wait_ge(turned_sb, done(t - 2))
                    pe.sem_inc(pe_turn, 1)
                    for j in range(SUB):
                        last = nc.tensor.transpose(ps_t[k][0:D, j * 128:(j + 1) * 128], xs[:, k, j, :], ident[:, :])
                    last.then_inc(turned, 1)
                    pe.wait_ge(turned_sb, done(t))
                    pe.wait_ge(made, done(t - 2))
                    for j in range(SUB):
                        last = nc.tensor.matmul(ps_p[k][:, j * D:(j + 1) * D], xts[:, k, j * 128:(j + 1) * 128], w_e1x[:, :], start=True, stop=True)
                    last.then_inc(product, 1)
                rounds(pe, step, NT, 2)

            @block.scalar
            def _(act):
                act.sem_inc(turned_sb, CR)

                def step(i, k):
                    t = i * 2 + k
                    act.wait_ge(turned, done(t))
                    act.wait_ge(product, done(t - 2))
                    nc.scalar.copy(strided(x_t[:, bass.ds(t * GE, GE)]), halves(ps_t[k][0:D, :]))
                    nc.scalar.copy(xts[:, k, :], ps_t[k][0:D, :]).then_inc(turned_sb, 1)
                rounds(act, step, NT, 2)

            @block.sync
            def _(sp):
                sp.sem_inc(stored, CR)

                def step(i, k):
                    t = sp.snap(i * 2 + k) if not isinstance(i, int) else i * 2 + k
                    sp.wait_ge(made, done(t))
                    sp.dma_start(group_rows(tab_t2, t), ys[:, k].rearrange("p j f -> p (j f)")).then_inc(s_store[k], 16)
                    sp.wait_ge(s_store[k], (i + 1) * 16)
                    sp.sem_inc(stored, 1)
                rounds(sp, step, NT, 2)

        with ExitStack() as c:
            sem, own = stage_semaphores(c, "e1_")
            s_idx = [sem(f"idx{k}") for k in range(4)]
            s_att = [sem(f"att{k}") for k in range(4)]
            s_rows = [gather_sem(f"e1_rows{k}") for k in range(4)]
            s_out = [sem(f"out{k}") for k in range(4)]
            turned, turned_sb, product, made, squared, counted, pool_turn, pe_turn, written, cleared, adds, squares_added = (
                sem(n) for n in ("turned", "turned_sb", "product", "made", "squared", "counted", "pool_turn", "pe_turn", "written", "cleared", "adds", "squares_added"))
            chain, moments, root_in, root_out = sem("chain"), sem("moments"), sem("root_in"), sem("root_out")
            idx = sb("e1_idx_t", [128, 4, SUB], i32, c)
            att = sb("e1_att_t", [128, 4, SUB, D], ctx=c)
            att_end = sb("e1_att_end", [128, SUB, D], ctx=c)
            rows = sb("e1_rows_t", [128, 4, SUB, D], ctx=c)
            att_t = sb("e1_att_tt", [D, 2, GE], ctx=c)
            h = sb("e1_h", [128, 4, SUB * D], ctx=c)
            sq = sb("e1_sq", [128, 2, SUB * D], ctx=c)
            sum_h, sum_q = sb("e1_sum_h", [128, SUB * D], ctx=c), sb("e1_sum_q", [128, SUB * D], ctx=c)
            mean, var = sb("e1_mean", [128, D], ctx=c), sb("e1_var", [128, D], ctx=c)
            tmp = sb("e1_tmp", [128, D], ctx=c)
            ps_t = [c.enter_context(nc.psum_tensor(f"e1_t{k}", [128, 512], fp32)) for k in range(2)]
            ps_p = [c.enter_context(nc.psum_tensor(f"e1_p{k}", [128, 512], fp32)) for k in range(2)]
            ps_q = c.enter_context(nc.psum_tensor("e1_q", [128, 512], fp32))
            block = c.enter_context(stage_block(own))
            att_dram = P["edge_attr_64"]

            def att_of(i, k):
                return att_end[:, :, :] if isinstance(i, int) and i * 4 + k == NG - 1 else att[:, k % 4]

            @block.sync
            def _(sp):
                sp.sem_inc(written, CR)

                def load(i, k):
                    i, k = i + k // 4, k % 4
                    g = sp.snap(i * 4 + k) if not isinstance(i, int) else i * 4 + k
                    sp.wait_ge(made, done(g - 4))
                    sp.dma_start(idx[:, k, :], group_rows(src_pad.unsqueeze(1), g)).then_inc(s_idx[k], 16)
                    if isinstance(i, int) and g == NG - 1:
                        sp.wait_ge(cleared, 1)
                        sp.dma_start(att_end[0:TROWS], att_dram[(NG - 1) * GE:E - TLEFT, :].rearrange("(p s) f -> p s f", s=SUB)).then_inc(s_att[k], 16)
                        sp.dma_start(att_end[TROWS:TROWS + 1, 0:TLEFT], att_dram[E - TLEFT:E, :].unsqueeze(0)).then_inc(s_att[k], 16)
                    else:
                        sp.dma_start(att[:, k].rearrange("p s f -> p (s f)"), group_rows(att_dram, g)).then_inc(s_att[k], 16)

                for k in range(2):
                    load(0, k)

                def step(i, k):
                    g = sp.snap(i * 4 + k) if not isinstance(i, int) else i * 4 + k
                    if not isinstance(i, int) or g + 2 < NG:
                        load(i, k + 2)
                    sp.wait_ge(made, done(g))
                    sp.dma_start(group_rows(h_edges, g), h[:, k, :]).then_inc(s_out[k], 16)
                rounds(sp, step, NG, 4)
                for k in range(4):
                    sp.wait_ge(s_out[k], (NG + 3 - k) // 4 * 16)

            @block.gpsimd
            def _(pool):
                pool.memset(att_end[:, :, :], 0.0).then_inc(cleared, 1)

                def step(i, k):
                    pool.wait_ge(s_idx[k], (i + 1) * 16)
                    pool.sem_inc(pool_turn, 1)
                    for s in range(SUB):
                        nc.gpsimd.indirect_dma_start(
                            out=rows[:, k, s, :], out_offset=None, in_=tab_t2,
                            in_offset=bass.IndirectOffsetOnAxis(ap=idx[:, k, s:s + 1], axis=0)).then_inc(s_rows[k], 16)
                rounds(pool, step, NG, 4)

            @block.tensor
            def _(pe):
                pe.sem_inc(turned, CR)
                pe.sem_inc(product, CR)

                def turn(i, k):
                    i, k = i + k // 4, k % 4
                    g = i * 4 + k
                    last_group = isinstance(i, int) and g == NG - 1
                    pe.wait_ge(s_att[k], (i + 1 + last_group) * 16)
                    pe.wait_ge(turned_sb, done(g - 2))
                    pe.sem_inc(pe_turn, 1)
                    for s in range(SUB):
                        last = nc.tensor.transpose(ps_t[k % 2][0:D, s * 128:(s + 1) * 128], att_of(i, k)[:, s, :], ident[:, :])
                    last.then_inc(turned, 1)
                turn(0, 0)

                def step(i, k):
                    g = i * 4 + k
                    if not isinstance(i, int) or g + 1 < NG:
                        turn(i, k + 1)
                    pe.wait_ge(turned_sb, done(g))
                    pe.wait_ge(made, done(g - 2))
                    for s in range(SUB):
                        last = nc.tensor.matmul(ps_p[k % 2][:, s * D:(s + 1) * D], att_t[:, k % 2, s * 128:(s + 1) * 128], w_e1e[:, :], start=True, stop=True)
                    last.then_inc(product, 1)
                rounds(pe, step, NG, 4)
                pe.wait_ge(adds, done(NG - 1))
                pe.wait_ge(squares_added, done(NG - 1))
                nc.tensor.matmul(ps_q[:, 0:SUB * D], ones_sq[:, :], sum_h[:, :], start=True, stop=True)
                nc.tensor.matmul(ps_q[:, SUB * D:2 * SUB * D], ones_sq[:, :], sum_q[:, :], start=True, stop=True).then_inc(moments, 1)

            @block.scalar
            def _(act):
                act.sem_inc(turned_sb, CR)
                act.sem_inc(squared, CR)

                def copy_turned(i, k):
                    i, k = i + k // 4, k % 4
                    g = i * 4 + k
                    act.wait_ge(turned, done(g))
                    act.wait_ge(product, done(g - 2))
                    nc.scalar.copy(att_t[:, k % 2, :], ps_t[k % 2][0:D, :]).then_inc(turned_sb, 1)
                copy_turned(0, 0)

                def step(i, k):
                    g = i * 4 + k
                    if not isinstance(i, int) or g + 1 < NG:
                        copy_turned(i, k + 1)
                    act.wait_ge(made, done(g))
                    act.wait_ge(squares_added, done(g - 2))
                    nc.scalar.activation(sq[:, k % 2, :], h[:, k, :], ACT.Square).then_inc(squared, 1)
                rounds(act, step, NG, 4)
                act.wait_ge(root_in, 1)
                nc.scalar.activation(var[:, :], var[:, :], ACT.Sqrt).then_inc(root_out, 1)

            @block.vector
            def _(dve):
                link = linker(dve, chain)
                link(nc.vector.memset(sum_h[:, :], 0.0))
                link(nc.vector.memset(sum_q[:, :], 0.0))
                for s_ in (made, adds, squares_added):
                    dve.sem_inc(s_, CR)

                def step(i, k, previous=True):
                    g = i * 4 + k
                    dve.wait_ge(product, done(g))
                    dve.wait_ge(squared, done(g - 4))
                    if not isinstance(i, int) or i > 0:
                        dve.wait_ge(s_out[k], i * 16)
                    dve.wait_ge(s_rows[k], (i + 1) * 64)
                    nc.vector.tensor_tensor(h[:, k, :], ps_p[k % 2][:, 0:SUB * D], rows[:, k].rearrange("p s f -> p (s f)"), ALU.add).then_inc(made, 1)
                    if previous:
                        dve.wait_ge(squared, done(g - 1))
                        dve.wait_ge(squares_added, done(g - 2))
                        nc.vector.tensor_tensor(sum_q[:, :], sum_q[:, :], sq[:, (k + 1) % 2, :], ALU.add).then_inc(squares_added, 1)
                    dve.wait_ge(made, done(g))
                    dve.wait_ge(adds, done(g - 1))
                    nc.vector.tensor_tensor(sum_h[:, :], sum_h[:, :], h[:, k, :], ALU.add).then_inc(adds, 1)
                for k in range(4):
                    step(0, k, k > 0)
                with dve.Fori(1, NG // 4) as i:
                    for k in range(4):
                        step(i, k)
                for k in range(NG % 4):
                    step(NG // 4, k)
                dve.wait_ge(squared, done(NG - 1))
                dve.wait_ge(squares_added, done(NG - 2))
                nc.vector.tensor_tensor(sum_q[:, :], sum_q[:, :], sq[:, (NG - 1) % 2, :], ALU.add).then_inc(squares_added, 1)
                dve.wait_ge(moments, 1)
                by_sub = lambda o: ps_q[:, o:o + SUB * D].rearrange("p (s f) -> p f s", s=SUB)
                link(nc.vector.tensor_reduce(mean[:, :], by_sub(0), AX.X, ALU.add))
                link(nc.vector.tensor_reduce(var[:, :], by_sub(SUB * D), AX.X, ALU.add))
                link(nc.vector.tensor_scalar(mean[:, :], mean[:, :], 1.0 / E, None, ALU.mult))
                link(nc.vector.tensor_tensor(tmp[:, :], mean[:, :], mean[:, :], ALU.mult))
                link(nc.vector.tensor_scalar(var[:, :], var[:, :], 1.0 / E, EPS, ALU.mult, ALU.add))
                nc.vector.tensor_tensor(var[:, :], var[:, :], tmp[:, :], ALU.subtract).then_inc(root_in, 1)
                dve.wait_ge(root_out, 1)
                link(nc.vector.reciprocal(var[:, :], var[:, :]))
                link(nc.vector.tensor_tensor(bn_scale[:, :], var[:, :], row_g1[:, :], ALU.mult))
                link(nc.vector.tensor_tensor(mean[:, :], mean[:, :], row_b1[:, :], ALU.add))
                link(nc.vector.tensor_tensor(mean[:, :], row_b1[:, :], mean[:, :], ALU.subtract))
                link(nc.vector.tensor_tensor(mean[:, :], mean[:, :], bn_scale[:, :], ALU.mult))
                nc.vector.tensor_tensor(bn_shift[:, :], mean[:, :], row_be1[:, :], ALU.add)

        with ExitStack() as c:
            sem, own = stage_semaphores(c, "e2_")
            s_h = [sem(f"h{k}") for k in range(4)]
            scaled, shifted, message, hot, summed, added = (sem(n) for n in ("scaled", "shifted", "message", "hot", "summed", "added"))
            h = sb("e2_h", [128, 4, SUB, D], ctx=c)
            hs = sb("e2_hs", [128, 2, SUB, D], ctx=c)
            msg = sb("e2_msg", [128, 2, SUB, D], ctx=c)
            onehot = sb("e2_onehot", [128, 4, SUB, W], ctx=c)
            ps_s = [c.enter_context(nc.psum_tensor(f"e2_s{k}", [128, 512], fp32)) for k in range(2)]
            gen = general_path(c, sem, "e2", D, dst_pad, [], msg[:, 0], ps_s[0])
            gen_h, gen_shifted, gen_scaled = sem("gen_h"), sem("gen_shifted"), sem("gen_scaled")
            block = c.enter_context(stage_block(own))
            scale_bc = bn_scale[:, :].unsqueeze(1).to_broadcast([128, SUB, D])
            shift_bc = bn_shift[:, :].unsqueeze(1).to_broadcast([128, SUB, D])

            @block.sync
            def _(sp):
                def general():
                    gen.sync(sp, lambda g: sp.dma_start(h[:, 0].rearrange("p s f -> p (s f)"), group_rows(h_edges, g)).then_inc(gen_h, 16))

                def windows():
                    def step(i, k):
                        g = sp.snap(i * 4 + k) if not isinstance(i, int) else i * 4 + k
                        sp.wait_ge(scaled, done(g - 4))
                        sp.dma_start(h[:, k].rearrange("p s f -> p (s f)"), group_rows(h_edges, g)).then_inc(s_h[k], 16)
                    rounds(sp, step, NG, 4)

                by_flag(sp, general, windows)

            @block.gpsimd
            def _(pool):
                def general():
                    pool.sem_inc(scaled, 1)

                def windows():
                    pool.sem_inc(scaled, CR)

                    def step(i, k):
                        g = i * 4 + k
                        pool.wait_ge(s_h[k], (i + 1) * 16)
                        pool.wait_ge(message, done(g - 2))
                        nc.gpsimd.tensor_tensor(hs[:, k % 2], h[:, k], scale_bc, ALU.mult).then_inc(scaled, 1)
                    rounds(pool, step, NG, 4)

                by_flag(pool, general, windows)

            @block.vector
            def _(dve):
                def general():
                    def make(g):
                        dve.wait_ge(gen_h, (g + 1) * 16)
                        nc.vector.tensor_tensor(hs[:, 0], h[:, 0], scale_bc, ALU.mult).then_inc(gen_scaled, 1)
                        dve.wait_ge(gen_scaled, g + 1)
                        nc.vector.tensor_tensor(hs[:, 0], hs[:, 0], shift_bc, ALU.add).then_inc(gen_shifted, 1)
                    gen.vector(dve, make)

                def windows():
                    for s_ in (hot, shifted, added):
                        dve.sem_inc(s_, CR)

                    def prepare(i, k):
                        i, k = i + k // 4, k % 4
                        g = i * 4 + k
                        dve.wait_ge(summed, done(g - 4))
                        nc.vector.tensor_tensor(onehot[:, k], iota_w[:, :, :],
                                                bc_last(rel[:, bass.ds(g, 1), :].rearrange("p a s -> p (a s)"), W), ALU.is_equal).then_inc(hot, 1)
                        dve.wait_ge(scaled, done(g))
                        nc.vector.tensor_tensor(hs[:, k % 2], hs[:, k % 2], shift_bc, ALU.add).then_inc(shifted, 1)
                    prepare(0, 0)

                    def step(i, k):
                        g = i * 4 + k
                        if not isinstance(i, int) or g + 1 < NG:
                            prepare(i, k + 1)
                        start = dve.value_load(base[0:1, bass.ds(g, 1)], min_val=0, max_val=N)
                        dve.wait_ge(summed, done(g))
                        dve.wait_ge(added, done(g - 1))
                        nc.vector.tensor_tensor(acc[0:D, bass.ds(start, W)], acc[0:D, bass.ds(start, W)], ps_s[k % 2][0:D, 0:W], ALU.add).then_inc(added, 1)
                    rounds(dve, step, NG, 4)

                by_flag(dve, general, windows)

            @block.scalar
            def _(act):
                def general():
                    def step(g):
                        act.wait_ge(gen_shifted, g + 1)
                        nc.scalar.activation(msg[:, 0], hs[:, 0], ACT.Silu).then_inc(gen.message, 1)
                    gen.each_group(act, step)

                def windows():
                    act.sem_inc(message, CR)

                    def step(i, k):
                        g = i * 4 + k
                        act.wait_ge(shifted, done(g))
                        act.wait_ge(summed, done(g - 2))
                        nc.scalar.activation(msg[:, k % 2], hs[:, k % 2], ACT.Silu).then_inc(message, 1)
                    rounds(act, step, NG, 4)

                by_flag(act, general, windows)

            @block.tensor
            def _(pe):
                def general():
                    gen.tensor(pe)

                def windows():
                    pe.sem_inc(summed, CR)

                    def step(i, k):
                        g = i * 4 + k
                        pe.wait_ge(hot, done(g))
                        pe.wait_ge(added, done(g - 2))
                        pe.wait_ge(message, done(g))
                        for s in range(SUB):
                            last = nc.tensor.matmul(ps_s[k % 2][0:D, 0:W], msg[:, k % 2, s, :], onehot[:, k, s, :], start=s == 0, stop=s == SUB - 1)
                        last.then_inc(summed, 1)
                    rounds(pe, step, NG, 4)

                by_flag(pe, general, windows)

        with ExitStack() as c:
            sem, own = stage_semaphores(c, "e3_")
            ready, product, copied, chain, centre, root_in, root_out, silu_out, staged, turned, summed, pe_turn, s_cnt = (
                sem(n) for n in ("ready", "product", "copied", "chain", "centre", "root_in", "root_out", "silu_out", "staged", "turned", "summed", "pe_turn", "s_cnt"))
            s_tab = sem("tab")
            h_t = sb("e3_h_t", [D, NP], ctx=c)
            sq_t = sb("e3_sq_t", [D, NP], ctx=c)
            hs = sb("e3_hs", [D, 2, GE], ctx=c)
            col = sb("e3_col", [D, 6], ctx=c)
            sums, squares = sb("e3_sums", [128, NT * SUB], ctx=c), sb("e3_squares", [128, NT * SUB], ctx=c)
            mid = sb("e3_mid", [128, NT * SUB, D], ctx=c)
            ps_p = [c.enter_context(nc.psum_tensor(f"e3_p{k}", [128, 512], fp32)) for k in range(2)]
            ps_z = [c.enter_context(nc.psum_tensor(f"e3_z{k}", [128, 512], fp32)) for k in range(2)]
            block = c.enter_context(stage_block(own))

            @block.sync
            def _(sp):
                sp.dma_start(sq_t[:, :], cnt_dram.unsqueeze(0).to_broadcast([D, NP])).then_inc(s_cnt, 16)
                sp.wait_ge(root_in, 4)
                sp.dma_start(tab_x3[0:NP, :].rearrange("(t p j) f -> p t (j f)", p=LANES, j=SUB),
                             z_nm[:, :, :, :].rearrange("p t j f -> p t (j f)")).then_inc(s_tab, 16)
                sp.wait_ge(s_tab, 16)

            @block.tensor
            def _(pe):
                pe.sem_inc(product, CR)
                pe.sem_inc(turned, CR)
                pe.wait_ge(ready, 1)

                def multiply(i, k):
                    t = i * 2 + k
                    pe.wait_ge(copied, done(t - 2))
                    nc.tensor.matmul(ps_p[k][:, :], w_n2x[:, :], x_t[:, bass.ds(t * GE, GE)], start=True, stop=False)
                    nc.tensor.matmul(ps_p[k][:, :], w_n2a[:, :], acc[0:D, bass.ds(t * GE, GE)], start=False, stop=True).then_inc(product, 1)
                rounds(pe, multiply, NT, 2)

                def turn(i, k):
                    t = i * 2 + k
                    pe.wait_ge(staged, done(t))
                    pe.wait_ge(summed, done(t - 2))
                    pe.sem_inc(pe_turn, 1)
                    for j in range(SUB):
                        last = nc.tensor.transpose(ps_z[k][:, j * D:(j + 1) * D], strided(hs[:, k, :])[:, j, :], ident[0:D, 0:D])
                    last.then_inc(turned, 1)
                rounds(pe, turn, NT, 2)

            @block.scalar
            def _(act):
                act.sem_inc(copied, CR)
                act.sem_inc(staged, CR)

                def copy_product(i, k):
                    t = i * 2 + k
                    act.wait_ge(product, done(t))
                    nc.scalar.copy(h_t[:, bass.ds(t * GE, GE)], ps_p[k][0:D, :]).then_inc(copied, 1)
                rounds(act, copy_product, NT, 2)
                act.wait_ge(root_in, 1)
                nc.scalar.activation(col[:, 1:2], col[:, 1:2], ACT.Sqrt).then_inc(root_out, 1)
                act.wait_ge(root_in, 2)

                def finish(i, k):
                    t = i * 2 + k
                    act.wait_ge(turned, done(t - 2))
                    nc.scalar.activation(hs[:, k, :], h_t[:, bass.ds(t * GE, GE)], ACT.Silu, bias=col[:, 3:4], scale=col[:, 2:3]).then_inc(staged, 1)
                rounds(act, finish, NT, 2)
                act.wait_ge(root_in, 3)
                nc.scalar.activation(squares[:, :], squares[:, :], ACT.Sqrt).then_inc(root_out, 1)

            @block.vector
            def _(dve):
                link = linker(dve, chain)
                dve.sem_inc(summed, CR)
                dve.wait_ge(s_cnt, 16)
                link(nc.vector.tensor_scalar(sq_t[:, :], sq_t[:, :], 1.0, None, ALU.max))
                link(nc.vector.reciprocal(sq_t[:, :], sq_t[:, :]))
                nc.vector.tensor_tensor(acc[0:D, :], acc[0:D, :], sq_t[:, :], ALU.mult).then_inc(ready, 1)
                dve.wait_ge(ready, 1)
                dve.wait_ge(copied, done(NT - 1))
                link(nc.vector.tensor_reduce(col[:, 0:1], h_t[:, 0:N], AX.X, ALU.add))
                link(nc.vector.tensor_scalar(col[:, 0:1], col[:, 0:1], 1.0 / N, None, ALU.mult))
                link(nc.vector.tensor_scalar(h_t[:, :], h_t[:, :], col[:, 0:1], None, ALU.subtract))
                link(nc.vector.tensor_tensor(sq_t[:, 0:N], h_t[:, 0:N], h_t[:, 0:N], ALU.mult))
                link(nc.vector.tensor_reduce(col[:, 1:2], sq_t[:, 0:N], AX.X, ALU.add))
                nc.vector.tensor_scalar(col[:, 1:2], col[:, 1:2], 1.0 / N, EPS, ALU.mult, ALU.add).then_inc(root_in, 1)
                dve.wait_ge(root_out, 1)
                link(nc.vector.reciprocal(col[:, 1:2], col[:, 1:2]))
                link(nc.vector.tensor_tensor(col[:, 2:3], col[:, 1:2], col_n2[:, 1:2], ALU.mult))
                link(nc.vector.tensor_tensor(col[:, 4:5], col[:, 0:1], col_n2[:, 0:1], ALU.add))
                link(nc.vector.tensor_tensor(col[:, 5:6], col[:, 0:1], col_n2[:, 0:1], ALU.add))
                link(nc.vector.tensor_tensor(col[:, 4:5], col[:, 4:5], col[:, 5:6], ALU.subtract))
                link(nc.vector.tensor_tensor(col[:, 4:5], col[:, 4:5], col[:, 2:3], ALU.mult))
                nc.vector.tensor_tensor(col[:, 3:4], col[:, 4:5], col_n2[:, 2:3], ALU.add).then_inc(root_in, 1)

                def step(i, k):
                    t = i * 2 + k
                    dve.wait_ge(turned, done(t))
                    nc.vector.tensor_tensor(block_of(z_nm, t), ps_z[k][:, 0:SUB * D].rearrange("p (j f) -> p j f", j=SUB), block_of(x_nm, t), ALU.add).then_inc(summed, 1)
                rounds(dve, step, NT, 2)
                dve.wait_ge(summed, done(NT - 1))
                z, mid_ = flat(z_nm), mid[:, :, :]
                link(nc.vector.tensor_reduce(sums[:, :], z, AX.X, ALU.add))
                link(nc.vector.tensor_scalar(sums[:, :], sums[:, :], 1.0 / D, None, ALU.mult))
                link(nc.vector.tensor_tensor(z, z, bc_last(sums[:, :], D), ALU.subtract))
                link(nc.vector.tensor_tensor(mid_, z, z, ALU.mult))
                link(nc.vector.tensor_reduce(squares[:, :], mid_, AX.X, ALU.add))
                nc.vector.tensor_scalar(squares[:, :], squares[:, :], 1.0 / D, EPS, ALU.mult, ALU.add).then_inc(root_in, 1)
                dve.wait_ge(root_out, 2)
                link(nc.vector.reciprocal(squares[:, :], squares[:, :]))
                nc.vector.tensor_tensor(z, z, bc_last(squares[:, :], D), ALU.mult).then_inc(root_in, 1)

        total = sb("total", [128, NT, SUB, D + 1])
        with ExitStack() as c:
            sem, own = stage_semaphores(c, "r1_")
            s_x, chain, split_done, zero_set, turned, turned_sb, multiplied, ones_set, gen_zero, gen_out, pe_turn = (
                sem(n) for n in ("s_x", "chain", "split_done", "zero_set", "turned", "turned_sb", "multiplied", "ones_set", "gen_zero", "gen_out", "pe_turn"))
            SLOTS = 2
            s_block = [sem(f"block{k}") for k in range(SLOTS)]
            BATCH = 8
            BATCHES = -(-HI // BATCH)
            cuts = [HI * n // BATCHES for n in range(BATCHES + 1)]
            x_rows = sb("r1_x_rows", [128, NDL, D], ctx=c)
            x_parts = sb("r1_x_parts", [128, 3, NDL, D], bf16, c)
            block_counts = sb("r1_block_counts", [128, SLOTS, LANES, HI], bf16, c)
            turned_counts = sb("r1_turned_counts", [128, 2, BATCH, LANES], bf16, c)
            zero_b = sb("r1_zero_b", [128, 512], bf16, c)
            rows = sb("r1_rows", [128, SUB, D + 1], ctx=c)
            PER_BANK = 512 // D
            BANKS = -(-HI // PER_BANK)
            x_now = sb("r1_x_now", [128, SLOTS, 3, D], bf16, c)
            x_set = sem("x_set")
            ps_sum = [c.enter_context(nc.psum_tensor(f"r1_sum{k}", [128, 512], fp32)) for k in range(BANKS)]
            ps_t = c.enter_context(nc.psum_tensor("r1_t", [128, BATCH, LANES], bf16))
            gen = general_path(c, sem, "r1", D + 1, src_pad, [(tab_x3, dst_pad, rows[:, :, 0:D])], rows, ps_sum[0])
            block = c.enter_context(stage_block(own))

            @block.sync
            def _(sp):
                def general():
                    gen.sync(sp)
                    sp.wait_ge(gen.begun, NG + 1)
                    for t in range(NT):
                        sp.dma_start(sums_dram[t * GE:(t + 1) * GE, :].rearrange("n f -> f n"), acc[:, t * GE:(t + 1) * GE],
                                     allow_slow_non_contiguous=True).then_inc(gen_out, 16)
                    sp.wait_ge(gen_out, NT * 16)
                    sp.dma_start(total[:, :, :, :].rearrange("p t j f -> p t (j f)"),
                                 sums_dram.rearrange("(t p j) f -> p t (j f)", p=LANES, j=SUB)).then_inc(gen_out, 16)
                    sp.wait_ge(gen_out, (NT + 1) * 16)

                def dense():
                    sp.sem_inc(s_x, 1)
                    sp.dma_start(x_rows[:, :, :], tab_x3[0:NDL * LANES, :].rearrange("(b p) f -> p b f", p=LANES)).then_inc(s_x, 16)

                    def step(i, k):
                        b = sp.snap(i * 2 + k) if not isinstance(i, int) else i * 2 + k
                        if not isinstance(b, int) or b >= 2:
                            sp.wait_ge(turned, done((b - 1) * BATCHES - 1))
                        sp.dma_start(block_counts[:, k].rearrange("p d h -> p (d h)"),
                                     destinations(b, LANES)).then_inc(s_block[k], 16)
                    peeled(sp, step, NDL, 2)

                by_flag(sp, general, dense)

            @block.gpsimd
            def _(pool):
                by_flag(pool, lambda: gen.gpsimd(pool), lambda: pool.sem_inc(gen.turn, 1))

            @block.vector
            def _(dve):
                nc.vector.memset(rows[:, :, D:D + 1], 1.0).then_inc(ones_set, 1)

                def general():
                    nc.vector.memset(acc[:, :], 0.0).then_inc(gen_zero, 1)
                    dve.wait_ge(gen_zero, 1)
                    gen.vector(dve)

                def dense():
                    link = linker(dve, chain)
                    nc.vector.memset(zero_b[:, :], 0.0).then_inc(zero_set, 1)
                    dve.sem_inc(x_set, CR)
                    dve.wait_ge(s_x, 17)
                    split(link, x_rows[:, :, :], [x_parts[:, q] for q in range(3)], x_rows[:, :, :])

                    def step(i, k):
                        b = i * 2 + k
                        if not isinstance(b, int) or b >= 2:
                            dve.wait_ge(multiplied, done((b - 1) * BATCHES - 1))
                        nc.vector.tensor_copy(x_now[:, k], x_parts[:, :, bass.ds(b, 1), :].rearrange("p q a f -> p (q a) f")).then_inc(x_set, 1)
                    peeled(dve, step, NDL, 2)
                    dve.wait_ge(multiplied, done(NDL * BATCHES - 1))
                    tot = total[:, :, :, :].rearrange("p t j f -> p (t j) f")
                    nc.vector.tensor_copy(tot[:, :, D], deg_nm[:, :])
                    for n in range(0, BANKS, 2):
                        cols = min(PER_BANK, HI - n * PER_BANK)
                        nc.vector.tensor_copy(tot[:, n * PER_BANK:n * PER_BANK + cols, 0:D],
                                              ps_sum[n][:, 0:cols * D].rearrange("p (h f) -> p h f", f=D))

                by_flag(dve, general, dense)

            @block.tensor
            def _(pe):
                def general():
                    pe.wait_ge(ones_set, 1)
                    gen.tensor(pe)

                def dense():
                    for s_ in (turned, multiplied):
                        pe.sem_inc(s_, CR)
                    pe.wait_ge(zero_set, 1)
                    for n in range(BANKS):
                        nc.tensor.matmul(ps_sum[n][:, :], zero_b[:, 0:128], zero_b[:, :], start=True, stop=True)

                    def turn(b, q):
                        if q % BATCHES == 0:
                            pe.wait_ge(s_block[q // BATCHES], (b + 1) * 16)
                        pe.wait_ge(turned_sb, done(b * 2 * BATCHES + q - 1))
                        pe.sem_inc(pe_turn, 1)
                        for n, h in enumerate(range(cuts[q % BATCHES], cuts[q % BATCHES + 1])):
                            last = nc.tensor.transpose(ps_t[:, n, :], block_counts[:, q // BATCHES, :, h], ident_b[:, :])
                        last.then_inc(turned, 1)

                    def multiply(b, q):
                        k = q // BATCHES
                        if q % BATCHES == 0:
                            pe.wait_ge(x_set, done(b * 2 + k))
                        pe.wait_ge(turned_sb, done(b * 2 * BATCHES + q))
                        for n, h in enumerate(range(cuts[q % BATCHES], cuts[q % BATCHES + 1])):
                            for part in range(3):
                                last = nc.tensor.matmul(ps_sum[h // PER_BANK][:, h % PER_BANK * D:(h % PER_BANK + 1) * D],
                                                        turned_counts[:, q % 2, n, :], x_now[:, k, part, :], start=False, stop=True, skip_group_check=True)
                        last.then_inc(multiplied, 1)

                    def pair(i, blocks=2):
                        for q in range(blocks * BATCHES + 1):
                            if q < blocks * BATCHES:
                                turn(i, q)
                            if q >= 1:
                                multiply(i, q - 1)
                    with pe.Fori(0, NDL // 2) as i:
                        pair(i)
                    if NDL % 2:
                        pair(NDL // 2, 1)

                by_flag(pe, general, dense)

            @block.scalar
            def _(act):
                def general():
                    act.wait_ge(ones_set, 1)

                def dense():
                    act.sem_inc(turned_sb, CR)

                    def pair(i, blocks=2):
                        for q in range(blocks * BATCHES):
                            at = i * (2 * BATCHES) + q
                            size = cuts[q % BATCHES + 1] - cuts[q % BATCHES]
                            act.wait_ge(turned, done(at))
                            act.wait_ge(multiplied, done(at - 2))
                            nc.scalar.copy(turned_counts[:, q % 2, 0:size], ps_t[:, 0:size]).then_inc(turned_sb, 1)
                    with act.Fori(0, NDL // 2) as i:
                        pair(i)
                    if NDL % 2:
                        pair(NDL // 2, 1)
                    act.wait_ge(multiplied, done(NDL * BATCHES - 1))
                    tot = total[:, :, :, :].rearrange("p t j f -> p (t j) f")
                    for n in range(1, BANKS, 2):
                        cols = min(PER_BANK, HI - n * PER_BANK)
                        nc.scalar.copy(tot[:, n * PER_BANK:n * PER_BANK + cols, 0:D],
                                       ps_sum[n][:, 0:cols * D].rearrange("p (h f) -> p h f", f=D))

                by_flag(act, general, dense)

        with ExitStack() as c:
            sem, own = stage_semaphores(c, "r2_")
            chain, staged, turned, turned_sb, product, summed, pe_turn, root_in, root_out, s_out = (
                sem(n) for n in ("chain", "staged", "turned", "turned_sb", "product", "summed", "pe_turn", "root_in", "root_out", "s_out"))
            R = D + 1
            rdeg = sb("r2_rdeg", [128, NT, SUB], ctx=c)
            ss = sb("r2_ss", [128, 2, SUB, R], ctx=c)
            sts = sb("r2_sts", [R, 2, GE], ctx=c)
            ps_t = [c.enter_context(nc.psum_tensor(f"r2_t{k}", [128, 512], fp32)) for k in range(2)]
            ps_p = [c.enter_context(nc.psum_tensor(f"r2_p{k}", [128, 512], fp32)) for k in range(2)]
            sums, squares = sb("r2_sums", [128, NT * SUB], ctx=c), sb("r2_squares", [128, NT * SUB], ctx=c)
            mid = sb("r2_mid", [128, NT * SUB, D], ctx=c)
            block = c.enter_context(stage_block(own))

            @block.sync
            def _(sp):
                sp.wait_ge(root_in, 2)
                sp.dma_start(out[0:NFULL * GE, :].rearrange("(t p j) f -> p t (j f)", p=LANES, j=SUB),
                             x_nm[:, 0:NFULL].rearrange("p t j f -> p t (j f)")).then_inc(s_out, 16)
                sp.dma_start(out[NFULL * GE:NFULL * GE + NREST * SUB, :].rearrange("(p j) f -> p (j f)", j=SUB),
                             x_nm[0:NREST, NFULL].rearrange("p j f -> p (j f)")).then_inc(s_out, 16)
                sp.dma_start(out[N - NLEFT:N, :].rearrange("(p j) f -> p (j f)", j=NLEFT),
                             x_nm[NREST:NREST + 1, NFULL, 0:NLEFT].rearrange("p j f -> p (j f)")).then_inc(s_out, 16)
                sp.wait_ge(s_out, 48)

            @block.vector
            def _(dve):
                link = linker(dve, chain)
                dve.sem_inc(staged, CR)
                dve.sem_inc(summed, CR)
                link(nc.vector.tensor_scalar(rdeg[:, :, :], total[:, :, :, D], 1.0, None, ALU.max))
                link(nc.vector.reciprocal(rdeg[:, :, :], rdeg[:, :, :]))

                def step(i, k):
                    t = i * 2 + k
                    dve.wait_ge(turned, done(t - 2))
                    nc.vector.tensor_tensor(ss[:, k], block_of(total, t), bc_last(per_node(rdeg, t), R), ALU.mult).then_inc(staged, 1)
                    dve.wait_ge(product, done(t))
                    nc.vector.tensor_tensor(block_of(x_nm, t), ps_p[k][:, 0:SUB * D].rearrange("p (j f) -> p j f", j=SUB), block_of(z_nm, t), ALU.add).then_inc(summed, 1)
                rounds(dve, step, NT, 2)
                dve.wait_ge(summed, done(NT - 1))
                z, mid_ = flat(x_nm), mid[:, :, :]
                link(nc.vector.tensor_reduce(sums[:, :], z, AX.X, ALU.add))
                link(nc.vector.tensor_scalar(sums[:, :], sums[:, :], 1.0 / D, None, ALU.mult))
                link(nc.vector.tensor_tensor(z, z, bc_last(sums[:, :], D), ALU.subtract))
                link(nc.vector.tensor_tensor(mid_, z, z, ALU.mult))
                link(nc.vector.tensor_reduce(squares[:, :], mid_, AX.X, ALU.add))
                nc.vector.tensor_scalar(squares[:, :], squares[:, :], 1.0 / D, EPS, ALU.mult, ALU.add).then_inc(root_in, 1)
                dve.wait_ge(root_out, 1)
                link(nc.vector.reciprocal(squares[:, :], squares[:, :]))
                nc.vector.tensor_tensor(z, z, bc_last(squares[:, :], D), ALU.mult).then_inc(root_in, 1)

            @block.tensor
            def _(pe):
                pe.sem_inc(turned, CR)
                pe.sem_inc(product, CR)

                def step(i, k):
                    t = i * 2 + k
                    pe.wait_ge(staged, done(t))
                    pe.wait_ge(turned_sb, done(t - 2))
                    pe.sem_inc(pe_turn, 1)
                    for j in range(SUB):
                        last = nc.tensor.transpose(ps_t[k][0:R, j * 128:(j + 1) * 128], ss[:, k, j, :], ident[:, :])
                    last.then_inc(turned, 1)
                    pe.wait_ge(turned_sb, done(t))
                    pe.wait_ge(summed, done(t - 2))
                    for j in range(SUB):
                        last = nc.tensor.matmul(ps_p[k][:, j * D:(j + 1) * D], sts[:, k, j * 128:(j + 1) * 128], w_3[:, :], start=True, stop=True)
                    last.then_inc(product, 1)
                rounds(pe, step, NT, 2)

            @block.scalar
            def _(act):
                act.sem_inc(turned_sb, CR)

                def step(i, k):
                    t = i * 2 + k
                    act.wait_ge(turned, done(t))
                    act.wait_ge(product, done(t - 2))
                    nc.scalar.copy(sts[:, k, :], ps_t[k][0:R, :]).then_inc(turned_sb, 1)
                rounds(act, step, NT, 2)
                act.wait_ge(root_in, 1)
                nc.scalar.activation(squares[:, :], squares[:, :], ACT.Sqrt).then_inc(root_out, 1)


_INS = ["x", "src", "dst", "edge_attr_32", "edge_attr_64", "L0_gnn_W_m1", "L0_gnn_b_m1", "L0_gnn_W_m2", "L0_gnn_b_m2",
        "L0_gnn_W_c1", "L0_gnn_b_c1", "L0_gnn_W_c2", "L0_gnn_b_c2", "L1_gnn_W1", "L1_gnn_b1", "L1_gnn_W2", "L1_gnn_b2",
        "L2_gnn_u", "L2_gnn_W1", "L2_gnn_b1", "L2_gnn_g1", "L2_gnn_be1", "L2_gnn_W2", "L2_gnn_b2", "L2_gnn_g2", "L2_gnn_be2",
        "L3_gnn_W", "L3_gnn_b"]


def kernel(**inputs):
    import numpy as np
    import concourse.bacc as bacc
    from concourse import mybir
    from concourse.bass_utils import run_bass_kernel_spmd

    nc = bacc.Bacc("TRN2", target_bir_lowering=False, num_devices=1)
    arrays = {name: np.ascontiguousarray(inputs[name]) for name in _INS if name not in ("L2_gnn_u", "L3_gnn_W")}
    arrays["L3_gnn_W_t"] = np.ascontiguousarray(np.asarray(inputs["L3_gnn_W"]).T)
    params = {n: nc.dram_tensor(f"in_{n}", a.shape, mybir.dt.from_np(a.dtype), kind="ExternalInput").ap() for n, a in arrays.items()}
    shape = arrays["x"].shape
    out = nc.dram_tensor("out", shape, mybir.dt.float32, kind="ExternalOutput").ap()
    build(nc, params, out)
    r = run_bass_kernel_spmd(nc, [{f"in_{n}": a for n, a in arrays.items()}], core_ids=[0])
    return r.results[0]["out"]
```

```python
def build(nc, P, out):
    import concourse.bass as bass
    from concourse import mybir
    from contextlib import ExitStack, contextmanager

    fp32, i32, bf16, fp16 = mybir.dt.float32, mybir.dt.int32, mybir.dt.bfloat16, mybir.dt.float16
    ALU, ACT, AX = mybir.AluOpType, mybir.ActivationFunctionType, mybir.AxisListType

    N, D = P["x"].shape
    E, DE = P["edge_attr_32"].shape
    H = P["L0_gnn_W_m1"].shape[1]
    HC = P["L0_gnn_W_c1"].shape[1]
    H1 = P["L1_gnn_W1"].shape[1]
    SUB, LANES = 4, 128
    GE = SUB * LANES
    NG = -(-E // GE)
    NT = -(-(N + 1) // GE)
    NP = NT * GE
    W = 24
    HI = NT * SUB
    NC = NG * SUB
    NCT = -(-NC // LANES)
    CREST = NC - (NCT - 1) * LANES
    WC = 8
    KEYS = WC * HI
    DB = 256
    NDB = -(-(N + 1) // DB)
    NDL = -(-(N + 1) // LANES)
    DEG_MAX = 256
    TAIL = E - (NG - 1) * GE
    TROWS = TAIL // SUB
    TLEFT = TAIL - TROWS * SUB
    NFULL = N // GE
    NREST = (N - NFULL * GE) // SUB
    NLEFT = N - NFULL * GE - NREST * SUB
    EPS = 1e-5
    LAG = 8
    SAFE = "`flag` leaves only starts inside the windows and the nodes to this path"
    CR = 4

    def done(n):
        return n + (1 + CR)

    def rounds(eng, step, total, unroll):
        with eng.Fori(0, total // unroll) as i:
            for k in range(unroll):
                step(i, k)
        for k in range(total % unroll):
            step(total // unroll, k)

    def peeled(eng, step, total, unroll):
        for k in range(unroll):
            step(0, k)
        with eng.Fori(1, total // unroll) as i:
            for k in range(unroll):
                step(i, k)
        for k in range(total % unroll):
            step(total // unroll, k)

    def dram(name, shape, dt=fp32):
        return nc.dram_tensor(name, shape, dt).ap()

    src_pad = dram("src_pad", (NG * GE,), i32)
    dst_pad = dram("dst_pad", (NG * GE,), i32)
    tab_a = dram("tab_a", (NP + 1, H))
    tab_b = dram("tab_b", (NP + W, H))
    tab_y1 = dram("tab_y1", (NP + 1, D))
    tab_y2 = dram("tab_y2", (NP + 1, D))
    tab_t2 = dram("tab_t2", (NP + 1, D))
    tab_x3 = dram("tab_x3", (NP + W, D))
    h_edges = dram("h_edges", (NG * GE, D))
    cnt_dram = dram("cnt_dram", (NP,))
    sums_dram = dram("sums_dram", (NP, D + 1))
    counts = dram("counts", (LANES, NP, HI), bf16)

    def groups(ap):
        return ap.rearrange("(g p s) -> g p s", p=LANES, s=SUB)

    def group_rows(ap, g):
        v = ap[0:(ap.shape[0] // GE) * GE, :].rearrange("(g p s) f -> g p (s f)", p=LANES, s=SUB)
        return v[bass.ds(g, 1)].rearrange("a p f -> (a p) f")

    def destinations(b, n):
        return counts.rearrange("p (b d) h -> b p (d h)", d=n)[bass.ds(b, 1)].rearrange("a p r -> (a p) r")

    whole = ExitStack()
    with whole:
        def sb(name, shape, dt=fp32, ctx=whole):
            return ctx.enter_context(nc.sbuf_tensor(name, shape, dt))

        ident = sb("ident", [128, 128])
        iota_w = sb("iota_w", [128, SUB, W])
        rel = sb("rel", [128, NG, SUB])
        lane_key = sb("lane_key", [128, 2, NCT * LANES])
        moves = sb("moves", [1, NG, SUB + 1], i32)
        starts_2 = sb("starts_2", [1, NG, 2], i32)
        flag_f = sb("flag_f", [1, 1])
        deg_nm = sb("deg_nm", [128, HI])
        base = sb("base", [1, NG], i32)
        flag = sb("flag", [1, 1], i32)
        iota_n = sb("iota_n", [128, GE])
        acc = sb("acc", [D + 1, NP])
        x_nm = sb("x_nm", [128, NT, SUB, D])
        z_nm = sb("z_nm", [128, NT, SUB, D])
        cnt_nm = sb("cnt_nm", [128, NT, SUB])
        dinv_nm = sb("dinv_nm", [128, NT, SUB])
        w_ab = sb("w_ab", [D, 2, H])
        w_m2 = sb("w_m2", [H + 1, D])
        b_m1 = sb("b_m1", [H, 1])
        w_c1x = sb("w_c1x", [D, HC])
        w_c1a = sb("w_c1a", [D + 1, HC])
        b_c1 = sb("b_c1", [HC, 1])
        w_c2 = sb("w_c2", [HC + 1, D])
        w_g1 = sb("w_g1", [D, H1])
        b_g1 = sb("b_g1", [H1, 1])
        w_g2 = sb("w_g2", [H1, D])
        b_g2 = sb("b_g2", [128, D])
        w_e1x = sb("w_e1x", [D, D])
        w_e1e = sb("w_e1e", [D, D])
        row_b1 = sb("row_b1", [128, D])
        row_g1 = sb("row_g1", [128, D])
        row_be1 = sb("row_be1", [128, D])
        w_n2x = sb("w_n2x", [D, 2 * D])
        w_n2a = sb("w_n2a", [D, 2 * D])
        col_n2 = sb("col_n2", [D, 3])
        w_3 = sb("w_3", [D + 1, D])
        bn_scale = sb("bn_scale", [128, D])
        bn_shift = sb("bn_shift", [128, D])
        ones_sq = sb("ones_sq", [128, 128])
        ident_b = sb("ident_b", [128, 128], bf16)

        def stage_semaphores(c, prefix):
            own = []

            def sem(name):
                own.append(c.enter_context(nc.semaphore(prefix + name)))
                return own[-1]
            return sem, own

        @contextmanager
        def stage_block(own):
            with nc.Block() as block:
                yield block
            with nc.Block() as after:
                @after.gpsimd
                def _(pool):
                    for s_ in own:
                        pool.sem_clear(s_)

        def gather_sem(name):
            return whole.enter_context(nc.semaphore(name))

        def linker(eng, sem):
            count = [0]

            def link(ins):
                count[0] += 1
                ins.then_inc(sem, 1)
                eng.wait_ge(sem, count[0])
            return link

        def bc_last(ap, n):
            return ap.unsqueeze(len(ap.shape)).to_broadcast(list(ap.shape) + [n])

        with ExitStack() as c, nc.allow_non_contiguous_dma(reason="index columns, once"):
            sem, own = stage_semaphores(c, "")
            pads_set, s_load, s_padded = sem("pads_set"), sem("s_load"), sem("s_padded")
            s_idx, consts, vchain, base_ready, base_spread = sem("s_idx"), sem("consts"), sem("vchain"), sem("base_ready"), sem("base_spread")
            s_zero, clears = sem("s_zero"), sem("clears")
            pad_src = sb("pad_src", [1, GE], i32, c)
            pad_dst = sb("pad_dst", [1, GE], i32, c)
            dst_i = sb("dst_i", [128, NG, SUB], i32, c)
            src_r = sb("src_r", [128, NCT, LANES], i32, c)
            dst_r = sb("dst_r", [128, NCT, LANES], i32, c)
            next_i = sb("next_i", [128, NCT], i32, c)
            next_f = sb("next_f", [128, NCT], fp32, c)
            first_f = sb("first_f", [128, NCT], fp32, c)
            lane_r = sb("lane_r", [128, NCT, LANES], fp32, c)
            key_r = sb("key_r", [128, NCT, LANES], fp32, c)
            rel_r = sb("rel_r", [128, NCT, LANES], fp32, c)
            starts = sb("starts", [1, NC], i32, c)
            starts_f = sb("starts_f", [1, NC], fp32, c)
            rows_ready, rows_turned = sem("rows_ready"), sem("rows_turned")
            ps_r = [c.enter_context(nc.psum_tensor(f"prep_r{k}", [128, 512], fp32)) for k in range(8)]
            base_row = sb("base_row", [1, NG], fp32, c)
            base_f = sb("base_f", [128, NG], fp32, c)
            outside = sb("outside", [128, 4], fp32, c)
            hop_f = sb("hop_f", [1, NG], fp32, c)
            part_i = sb("part_i", [128, NCT, LANES], i32, c)
            tmp_r = sb("tmp_r", [128, NCT, LANES], fp32, c)
            czero = sb("czero", [128, 64 * HI], bf16, c)
            outside_ready, outside_all = sem("outside_ready"), sem("outside_all")
            zeros = sb("zeros", [128, GE], fp32, c)
            block = c.enter_context(stage_block(own))
            loads = [
                (w_ab[:, 0, :], P["L0_gnn_W_m1"][0:D, :]), (w_ab[:, 1, :], P["L0_gnn_W_m1"][D:2 * D, :]),
                (w_m2[0:H, :], P["L0_gnn_W_m2"]), (w_m2[H:H + 1, :], P["L0_gnn_b_m2"].unsqueeze(0)),
                (b_m1[:, :], P["L0_gnn_b_m1"].unsqueeze(1)),
                (w_c1x[:, :], P["L0_gnn_W_c1"][0:D, :]), (w_c1a[1:D + 1, :], P["L0_gnn_W_c1"][D:2 * D, :]),
                (b_c1[:, :], P["L0_gnn_b_c1"].unsqueeze(1)),
                (w_c2[0:HC, :], P["L0_gnn_W_c2"]), (w_c2[HC:HC + 1, :], P["L0_gnn_b_c2"].unsqueeze(0)),
                (w_g1[:, :], P["L1_gnn_W1"]), (b_g1[:, :], P["L1_gnn_b1"].unsqueeze(1)), (w_g2[:, :], P["L1_gnn_W2"]),
                (b_g2[:, :], P["L1_gnn_b2"].unsqueeze(0).to_broadcast([128, D])),
                (w_e1x[:, :], P["L2_gnn_W1"][0:D, :]), (w_e1e[:, :], P["L2_gnn_W1"][D:2 * D, :]),
                (row_b1[:, :], P["L2_gnn_b1"].unsqueeze(0).to_broadcast([128, D])),
                (row_g1[:, :], P["L2_gnn_g1"].unsqueeze(0).to_broadcast([128, D])),
                (row_be1[:, :], P["L2_gnn_be1"].unsqueeze(0).to_broadcast([128, D])),
                (w_n2x[:, 0:D], P["L2_gnn_W2"][0:D, :]), (w_n2a[:, 0:D], P["L2_gnn_W2"][D:2 * D, :]),
                (col_n2[:, 0:1], P["L2_gnn_b2"].unsqueeze(1)), (col_n2[:, 1:2], P["L2_gnn_g2"].unsqueeze(1)),
                (col_n2[:, 2:3], P["L2_gnn_be2"].unsqueeze(1)),
                (w_3[0:D, :], P["L3_gnn_W_t"]), (w_3[D:D + 1, :], P["L3_gnn_b"].unsqueeze(0)),
                (x_nm[:, 0:NFULL].rearrange("p t j f -> p t (j f)"),
                 P["x"][0:NFULL * GE, :].rearrange("(t p j) f -> p t (j f)", p=LANES, j=SUB)),
                (x_nm[0:NREST, NFULL].rearrange("p j f -> p (j f)"),
                 P["x"][NFULL * GE:NFULL * GE + NREST * SUB, :].rearrange("(p j) f -> p (j f)", j=SUB)),
                (x_nm[NREST:NREST + 1, NFULL, 0:NLEFT].rearrange("p j f -> p (j f)"),
                 P["x"][N - NLEFT:N, :].rearrange("(p j) f -> p (j f)", j=NLEFT)),
            ]

            @block.sync
            def _(sp):
                sp.dma_start(src_pad[0:E], P["src"]).then_inc(s_padded, 16)
                sp.dma_start(dst_pad[0:E], P["dst"]).then_inc(s_padded, 16)
                sp.wait_ge(pads_set, 2)
                sp.dma_start(src_pad[E:NG * GE].unsqueeze(0), pad_src[:, 0:NG * GE - E]).then_inc(s_padded, 16)
                sp.dma_start(dst_pad[E:NG * GE].unsqueeze(0), pad_dst[:, 0:NG * GE - E]).then_inc(s_padded, 16)
                sp.wait_ge(clears, 8)
                for to, of in loads:
                    sp.dma_start(to, of).then_inc(s_load, 16)
                sp.wait_ge(s_padded, 64)
                sp.dma_start(dst_i[:, :, :], groups(dst_pad).rearrange("g p s -> p g s")).then_inc(s_idx, 16)
                for to, of in ((src_r, src_pad), (dst_r, dst_pad)):
                    chunks = of.rearrange("(c e) -> c e", e=LANES)
                    sp.dma_start(to[:, 0:NCT - 1, :], chunks[0:(NCT - 1) * LANES, :].rearrange("(m q) e -> q m e", q=LANES)).then_inc(s_idx, 16)
                    sp.dma_start(to[0:CREST, NCT - 1, :], chunks[(NCT - 1) * LANES:NC, :]).then_inc(s_idx, 16)
                firsts = dst_pad.rearrange("(c e) -> c e", e=LANES)[:, 0]
                sp.dma_start(next_i[:, 0:NCT - 1], firsts[1:(NCT - 1) * LANES + 1].rearrange("(m q) -> q m", q=LANES)).then_inc(s_idx, 16)
                sp.dma_start(next_i[0:CREST - 1, NCT - 1:NCT], firsts[(NCT - 1) * LANES + 1:NC].unsqueeze(1)).then_inc(s_idx, 16)
                sp.dma_start(starts[:, :], firsts.unsqueeze(0)).then_inc(s_idx, 16)
                sp.dma_start(base[:, :], dst_pad.rearrange("(a g e) -> a g e", a=1, e=GE)[:, :, 0]).then_inc(s_idx, 16)
                sp.wait_ge(consts, 2)
                for tab in (tab_a, tab_y1, tab_y2, tab_t2):
                    sp.dma_start(tab[NP:NP + 1, :], zeros[0:1, 0:tab.shape[1]]).then_inc(s_zero, 16)
                for tab in (tab_b, tab_x3):
                    sp.dma_start(tab[NP:NP + W, :], zeros[0:W, 0:tab.shape[1]]).then_inc(s_zero, 16)
                for d in range(N + 1, NDB * DB, 64):
                    rows_ = min(64, NDB * DB - d)
                    sp.dma_start(counts[:, d:d + rows_, :].rearrange("p d h -> p (d h)"), czero[:, 0:rows_ * HI]).then_inc(s_zero, 16)
                sp.wait_ge(s_zero, (6 + -(-(NDB * DB - N - 1) // 64)) * 16)
                sp.wait_ge(s_load, len(loads) * 16)

            @block.gpsimd
            def _(pool):
                pool.memset(pad_src[:, :], NP).then_inc(pads_set, 1)
                pool.memset(pad_dst[:, :], N).then_inc(pads_set, 1)
                pool.memset(src_r[:, NCT - 1, :], 0).then_inc(clears, 1)
                pool.memset(dst_r[:, NCT - 1, :], 0).then_inc(clears, 1)
                pool.memset(next_i[:, :], NP).then_inc(clears, 1)
                pool.memset(x_nm[:, NT - 1], 0.0).then_inc(clears, 1)
                pool.memset(w_c1a[0:1, :], 0.0).then_inc(clears, 1)
                pool.memset(acc[:, :], 0.0).then_inc(clears, 1)
                pool.memset(w_n2x[:, D:2 * D], 0.0).then_inc(clears, 1)
                pool.memset(w_n2a[:, D:2 * D], 0.0).then_inc(clears, 1)
                pool.memset(zeros[:, :], 0.0).then_inc(consts, 1)
                pool.memset(czero[:, :], 0.0).then_inc(consts, 1)
                pool.memset(ones_sq[:, :], 1.0).then_inc(consts, 1)
                pool.memset(ident[:, :], 0.0).then_inc(consts, 1)
                pool.wait_ge(consts, 4)
                pool.affine_select(out=ident[:, :], in_=ident[:, :], compare_op=ALU.not_equal, fill=1.0,
                                   base=0, pattern=[[-1, 128]], channel_multiplier=1).then_inc(consts, 1)
                pool.wait_ge(consts, 5)
                pool.tensor_copy(ident_b[:, :], ident[:, :]).then_inc(consts, 1)
                pool.iota(iota_w[:, :, :], pattern=[[0, SUB], [1, W]], base=0, channel_multiplier=0,
                          allow_small_or_imprecise_dtypes=True).then_inc(consts, 1)
                pool.iota(iota_n[:, :], pattern=[[1, GE]], base=0, channel_multiplier=0,
                          allow_small_or_imprecise_dtypes=True).then_inc(consts, 1)
                pool.wait_ge(base_ready, 1)
                pool.partition_broadcast(base_f[:, :], base_row[:, :], 128).then_inc(base_spread, 1)
                pool.wait_ge(outside_ready, 1)
                pool.partition_all_reduce(outside[:, :], outside[:, :], 128, bass.bass_isa.ReduceOp.max).then_inc(outside_all, 1)

            @block.vector
            def _(dve):
                dve.wait_ge(s_idx, 9 * 16)
                nc.vector.tensor_copy(base_row[:, :], base[:, :]).then_inc(base_ready, 1)
                link = linker(dve, vchain)
                link(nc.vector.tensor_scalar(part_i[:, :, :], src_r[:, :, :], 2, 127, ALU.logical_shift_right, ALU.bitwise_and))
                link(nc.vector.tensor_copy(lane_r[:, :, :], part_i[:, :, :]))
                link(nc.vector.tensor_scalar(part_i[:, :, :], src_r[:, :, :], 3, None, ALU.bitwise_and))
                link(nc.vector.tensor_copy(key_r[:, :, :], part_i[:, :, :]))
                link(nc.vector.tensor_scalar(part_i[:, :, :], src_r[:, :, :], 7, 124, ALU.logical_shift_right, ALU.bitwise_and))
                link(nc.vector.tensor_copy(tmp_r[:, :, :], part_i[:, :, :]))
                link(nc.vector.tensor_tensor(key_r[:, :, :], key_r[:, :, :], tmp_r[:, :, :], ALU.add))
                link(nc.vector.tensor_scalar(tmp_r[:, :, :], key_r[:, :, :], HI - 0.5, 4096.0, ALU.is_gt, ALU.mult))
                link(nc.vector.tensor_tensor(key_r[:, :, :], key_r[:, :, :], tmp_r[:, :, :], ALU.add))
                link(nc.vector.tensor_copy(next_f[:, :], next_i[:, :]))
                link(nc.vector.tensor_copy(rel_r[:, :, :], dst_r[:, :, :]))
                link(nc.vector.tensor_copy(first_f[:, :], rel_r[:, :, 0]))
                link(nc.vector.tensor_tensor(tmp_r[:, :, :], rel_r[:, :, :], bc_last(next_f[:, :], LANES), ALU.subtract))
                link(nc.vector.tensor_tensor(rel_r[:, :, :], rel_r[:, :, :], bc_last(first_f[:, :], LANES), ALU.subtract))
                nc.vector.scalar_tensor_tensor(out=key_r[:, :, :], in0=rel_r[:, :, :], scalar=float(HI), in1=key_r[:, :, :], op0=ALU.mult, op1=ALU.add).then_inc(rows_ready, 1)
                link(nc.vector.tensor_copy(rel[:, :, :], dst_i[:, :, :]))
                dve.wait_ge(base_spread, 1)
                link(nc.vector.tensor_tensor(rel[:, :, :], rel[:, :, :], bc_last(base_f[:, :], SUB), ALU.subtract))
                def all_of(ap):
                    return ap.rearrange("p g s -> p (g s)")
                link(nc.vector.tensor_reduce(outside[:, 0:1], all_of(rel[:, :, :]), AX.X, ALU.max))
                link(nc.vector.tensor_reduce(outside[:, 1:2], all_of(rel_r[:, :, :]), AX.X, ALU.min))
                link(nc.vector.tensor_reduce(outside[:, 2:3], all_of(tmp_r[:, :, :]), AX.X, ALU.max))
                link(nc.vector.tensor_reduce(outside[:, 3:4], all_of(rel_r[:, :, :]), AX.X, ALU.max))
                link(nc.vector.tensor_scalar(outside[:, 0:1], outside[:, 0:1], float(W - 1), None, ALU.subtract))
                link(nc.vector.tensor_scalar(outside[:, 3:4], outside[:, 3:4], float(WC - 1), None, ALU.subtract))
                link(nc.vector.tensor_scalar(outside[:, 1:2], outside[:, 1:2], -1.0, None, ALU.mult))
                link(nc.vector.tensor_copy(starts_f[:, :], starts[:, :]))
                per_chunk = starts_f[:, :].rearrange("a (g s) -> a g s", s=SUB)
                link(nc.vector.tensor_tensor(per_chunk, per_chunk, bc_last(base_row[:, :], SUB), ALU.subtract))
                link(nc.vector.tensor_scalar(starts_f[:, :], starts_f[:, :], float(HI), None, ALU.mult))
                link(nc.vector.tensor_copy(moves[:, :, 0:SUB - 1], per_chunk[:, :, 1:SUB]))
                link(nc.vector.memset(moves[:, NG - 1:NG, SUB:SUB + 1], 0))
                link(nc.vector.memset(starts_2[:, 0:LAG, :], 0))
                link(nc.vector.tensor_copy(starts_2[:, :, 0], base[:, :]))
                link(nc.vector.tensor_copy(starts_2[:, LAG:NG, 1], base[:, 0:NG - LAG]))
                link(nc.vector.tensor_copy(moves[:, 0:NG - 1, SUB], base[:, 1:NG]))
                link(nc.vector.tensor_copy(hop_f[:, 0:1], base_row[:, 0:1]))
                link(nc.vector.tensor_tensor(hop_f[:, 1:NG], base_row[:, 1:NG], base_row[:, 0:NG - 1], ALU.subtract))
                link(nc.vector.tensor_reduce(flag_f[:, :], hop_f[:, :], AX.X, ALU.max))
                link(nc.vector.tensor_scalar(flag_f[:, :], flag_f[:, :], float(W - 1), None, ALU.subtract))
                link(nc.vector.tensor_tensor(flag_f[:, :], flag_f[:, :], base_row[:, 0:1], ALU.max))
                link(nc.vector.tensor_scalar(hop_f[:, :], hop_f[:, :], float(HI), None, ALU.mult))
                link(nc.vector.tensor_copy(moves[:, :, SUB - 1], hop_f[:, :]))
                link(nc.vector.tensor_tensor(outside[:, 3:4], outside[:, 3:4], outside[:, 2:3], ALU.max))
                nc.vector.tensor_tensor(outside[:, 0:1], outside[:, 0:1], outside[:, 3:4], ALU.max).then_inc(outside_ready, 1)
                dve.wait_ge(outside_all, 1)
                link(nc.vector.tensor_tensor(outside[0:1, 0:1], outside[0:1, 0:1], outside[0:1, 1:2], ALU.max))
                link(nc.vector.tensor_tensor(flag_f[:, :], flag_f[:, :], outside[0:1, 0:1], ALU.max))
                link(nc.vector.tensor_scalar(flag_f[:, :], flag_f[:, :], 0.0, None, ALU.is_gt))
                nc.vector.tensor_copy(flag[:, :], flag_f[:, :])

            banks = [(which, m) for which in range(2) for m in range(0, NCT, SUB)]

            @block.tensor
            def _(pe):
                pe.wait_ge(consts, 5)
                pe.wait_ge(rows_ready, 1)
                for n, (which, m) in enumerate(banks):
                    for r in range(m, min(m + SUB, NCT)):
                        last = nc.tensor.transpose(ps_r[n][:, (r - m) * LANES:(r - m + 1) * LANES], (lane_r, key_r)[which][:, r, :], ident[:, :])
                    last.then_inc(rows_turned, 1)

            @block.scalar
            def _(act):
                for n, (which, m) in enumerate(banks):
                    width = min(SUB, NCT - m) * LANES
                    act.wait_ge(rows_turned, n + 1)
                    nc.scalar.copy(lane_key[:, which, m * LANES:m * LANES + width], ps_r[n][:, 0:width])

        def general_path(c, sem, name, width, target, tabs, message_tile, ps, after=()):
            class gen:
                pass
            gen.begun, gen.loaded, gen.message, gen.hot, gen.summed, gen.added, gen.turn, gen.lowered = (
                sem(f"gen_{n}") for n in ("begun", "loaded", "message", "hot", "summed", "added", "turn", "lowered"))
            gen.gathered = gather_sem(f"{name}_gen_gathered") if tabs else gen.loaded
            target_i = sb(f"{name}_gen_target_i", [128, SUB], i32, c)
            target_f = sb(f"{name}_gen_target_f", [128, SUB], ctx=c)
            index = [sb(f"{name}_gen_index{n}", [128, SUB], i32, c) for n in range(len(tabs))]
            onehot = sb(f"{name}_gen_onehot", [128, SUB, GE], ctx=c)
            gen.per_group = (1 + len(tabs)) * 16

            def each_group(eng, step):
                with eng.Fori(0, NG - 1) as g:
                    step(g)
                step(NG - 1)
            gen.each_group = each_group

            def sync(sp, load=None):
                def step(g):
                    g = sp.snap(g) if not isinstance(g, int) else g
                    sp.wait_ge(gen.begun, g + 1)
                    sp.dma_start(target_i[:, :], group_rows(target.unsqueeze(1), g)).then_inc(gen.loaded, 16)
                    for n, (_, indices, _) in enumerate(tabs):
                        sp.dma_start(index[n][:, :], group_rows(indices.unsqueeze(1), g)).then_inc(gen.loaded, 16)
                    if load is not None:
                        load(g)
                each_group(sp, step)
            gen.sync = sync

            def gpsimd(pool):
                def step(g):
                    pool.wait_ge(gen.loaded, (g + 1) * gen.per_group)
                    pool.sem_inc(gen.turn, 1)
                    for n, (tab, _, to) in enumerate(tabs):
                        for s in range(SUB):
                            nc.gpsimd.indirect_dma_start(
                                out=to[:, s, :], out_offset=None, in_=tab,
                                in_offset=bass.IndirectOffsetOnAxis(ap=index[n][:, s:s + 1], axis=0)).then_inc(gen.gathered, 16)
                each_group(pool, step)
            gen.gpsimd = gpsimd
            gen.rows_in = len(tabs) * SUB * 16

            def vector(dve, make=None):
                dve.sem_inc(gen.begun, 1)

                def step(g):
                    dve.wait_ge(gen.loaded, (g + 1) * gen.per_group)
                    nc.vector.tensor_copy(target_f[:, :], target_i[:, :]).then_inc(gen.lowered, 1)
                    if make is not None:
                        make(g)

                    def block(v):
                        dve.wait_ge(gen.lowered, (g * (NT + 1) + v) + 1)
                        nc.vector.tensor_tensor(onehot[:, :, :], iota_n[:, :].unsqueeze(1).to_broadcast([128, SUB, GE]),
                                                bc_last(target_f[:, :], GE), ALU.is_equal).then_inc(gen.hot, 1)
                        dve.wait_ge(gen.hot, (g * NT + v) + 1)
                        nc.vector.tensor_scalar(target_f[:, :], target_f[:, :], float(GE), None, ALU.subtract).then_inc(gen.lowered, 1)
                        dve.wait_ge(gen.summed, (g * NT + v) + 1)
                        nc.vector.tensor_tensor(acc[0:width, bass.ds(v * GE, GE)], acc[0:width, bass.ds(v * GE, GE)], ps[0:width, :], ALU.add).then_inc(gen.added, 1)
                    with dve.Fori(0, NT) as v:
                        block(v)
                    dve.wait_ge(gen.lowered, (g + 1) * (NT + 1))
                    dve.wait_ge(gen.added, (g + 1) * NT)
                    dve.sem_inc(gen.begun, 1)
                each_group(dve, step)
            gen.vector = vector

            def tensor(pe, make=None):
                def step(g):
                    if make is not None:
                        make(g)

                    def block(v):
                        if make is not None or not tabs:
                            pe.wait_ge(gen.message, g + 1)
                        else:
                            pe.wait_ge(gen.gathered, (g + 1) * gen.rows_in)
                        pe.wait_ge(gen.hot, (g * NT + v) + 1)
                        pe.sem_inc(gen.turn_pe, 1)
                        for s in range(SUB):
                            last = nc.tensor.matmul(ps[0:width, :], message_tile[:, s, 0:width], onehot[:, s, :], start=s == 0, stop=s == SUB - 1)
                        last.then_inc(gen.summed, 1)
                    with pe.Fori(0, NT) as v:
                        block(v)
                each_group(pe, step)
            gen.turn_pe = sem("gen_turn_pe")
            gen.tensor = tensor
            return gen

        def group_of(tile, g):
            return tile[:, :, 0:NC].rearrange("p q (g s) -> p q g s", s=SUB)[:, :, bass.ds(g, 1), :].rearrange("p q a s -> p q (a s)")

        def by_flag(eng, general, windows):
            outside_some = eng.value_load(flag[0:1, 0:1], min_val=0, max_val=1)
            with eng.If(outside_some):
                general()
            with eng.Else():
                windows()

        with ExitStack() as c:
            sem, own = stage_semaphores(c, "")
            staged, turned, turned_sb, product, tables_sb = (sem(f"ta_{n}") for n in ("staged", "turned", "turned_sb", "product", "tables_sb"))
            s_store = [sem(f"ta_store{k}") for k in range(2)]
            stored, pe_turn = sem("ta_stored"), sem("ta_pe_turn")
            xs = sb("xs", [128, 2, SUB, D], ctx=c)
            xts = sb("xts", [D, 2, GE], ctx=c)
            tabs = sb("tabs", [128, 2, 2, SUB * H], ctx=c)
            ps_t = [c.enter_context(nc.psum_tensor(f"ta_t{k}", [128, 512], fp32)) for k in range(2)]
            ps_p = [c.enter_context(nc.psum_tensor(f"ta_p{k}", [128, 512], fp32)) for k in range(4)]
            block = c.enter_context(stage_block(own))

            @block.vector
            def _(dve):
                dve.sem_inc(staged, CR)
                dve.sem_inc(tables_sb, CR)

                def stage_x(i, k):
                    i, k = i + k // 2, k % 2
                    t = i * 2 + k
                    dve.wait_ge(turned, done(t - 2))
                    nc.vector.tensor_copy(xs[:, k], x_nm[:, bass.ds(t, 1)].rearrange("p a j f -> p (a j) f")).then_inc(staged, 1)
                stage_x(0, 0)

                def step(i, k):
                    t = i * 2 + k
                    if not isinstance(i, int) or t + 1 < NT:
                        stage_x(i, k + 1)
                    dve.wait_ge(stored, done(t - 2))
                    dve.wait_ge(product, done(t))
                    nc.vector.tensor_copy(tabs[:, k, 0, :], ps_p[2 * k][:, 0:SUB * H])
                    nc.vector.tensor_copy(tabs[:, k, 1, :], ps_p[2 * k + 1][:, 0:SUB * H]).then_inc(tables_sb, 1)
                rounds(dve, step, NT, 2)

            @block.tensor
            def _(pe):
                pe.sem_inc(turned, CR)
                pe.sem_inc(product, CR)

                def turn(i, k):
                    i, k = i + k // 2, k % 2
                    t = i * 2 + k
                    pe.wait_ge(staged, done(t))
                    pe.wait_ge(turned_sb, done(t - 2))
                    pe.sem_inc(pe_turn, 1)
                    for j in range(SUB):
                        last = nc.tensor.transpose(ps_t[k][0:D, j * 128:(j + 1) * 128], xs[:, k, j, :], ident[:, :])
                    last.then_inc(turned, 1)
                turn(0, 0)

                def step(i, k):
                    t = i * 2 + k
                    if not isinstance(i, int) or t + 1 < NT:
                        turn(i, k + 1)
                    pe.wait_ge(turned_sb, done(t))
                    pe.wait_ge(tables_sb, done(t - 2))
                    for q in range(2):
                        for j in range(SUB):
                            last = nc.tensor.matmul(ps_p[2 * k + q][:, j * H:(j + 1) * H], xts[:, k, j * 128:(j + 1) * 128],
                                                    w_ab[:, q, :], start=True, stop=True)
                    last.then_inc(product, 1)
                rounds(pe, step, NT, 2)

            @block.scalar
            def _(act):
                act.sem_inc(turned_sb, CR)

                def step(i, k):
                    t = i * 2 + k
                    act.wait_ge(turned, done(t))
                    act.wait_ge(product, done(t - 2))
                    nc.scalar.copy(xts[:, k, :], ps_t[k][0:D, :]).then_inc(turned_sb, 1)
                rounds(act, step, NT, 2)

            @block.sync
            def _(sp):
                sp.sem_inc(stored, CR)

                def step(i, k):
                    t = sp.snap(i * 2 + k) if not isinstance(i, int) else i * 2 + k
                    sp.wait_ge(tables_sb, done(t))
                    sp.dma_start(group_rows(tab_a, t), tabs[:, k, 0, :]).then_inc(s_store[k], 16)
                    sp.dma_start(group_rows(tab_b, t), tabs[:, k, 1, :]).then_inc(s_store[k], 16)
                    sp.wait_ge(s_store[k], (i + 1) * 32)
                    sp.sem_inc(stored, 1)
                rounds(sp, step, NT, 2)

        with ExitStack() as c:
            sem, own = stage_semaphores(c, "")
            s_idx = [sem(f"l0_idx{k}") for k in range(4)]
            s_att = [sem(f"l0_att{k}") for k in range(4)]
            s_win = [sem(f"l0_win{k}") for k in range(4)]
            pe_turn = sem("l0_pe_turn")
            s_rows = [gather_sem(f"l0_rows{k}") for k in range(4)]
            pool_turn = sem("l0_pool_turn")
            combined, turned, turned_sb, hidden, hidden_sb, message, message_sb, summed, added = (
                sem(f"l0_{n}") for n in ("combined", "turned", "turned_sb", "hidden", "hidden_sb", "message", "message_sb", "summed", "added"))
            cleared, w_loaded = sem("l0_cleared"), sem("l0_w_loaded")
            idx = sb("l0_idx_t", [128, 4, SUB], i32, c)
            att = sb("l0_att_t", [128, 4, SUB, DE], ctx=c)
            rows = sb("l0_rows_t", [128, 4, SUB, H], ctx=c)
            comb = sb("l0_comb", [128, 4, SUB, DE + W], ctx=c)
            comb_t = sb("l0_comb_t", [DE + W, 2, GE], ctx=c)
            w_ew = sb("l0_w_ew", [DE + W, 4, H], ctx=c)
            hid = sb("l0_hid", [128, 2, GE], ctx=c)
            msg = sb("l0_msg", [128, 2, SUB, 1 + D], ctx=c)
            ps_t = [c.enter_context(nc.psum_tensor(f"l0_ps_t{k}", [128, 512], fp32)) for k in range(2)]
            ps_h = [c.enter_context(nc.psum_tensor(f"l0_ps_h{k}", [128, 512], fp32)) for k in range(2)]
            ps_m = c.enter_context(nc.psum_tensor("l0_ps_m", [128, 512], fp32))
            ps_s = c.enter_context(nc.psum_tensor("l0_ps_s", [128, 512], fp32))
            ps_c = c.enter_context(nc.psum_tensor("l0_ps_c", [128, 2, 512], fp32))
            s_counts = [sem(f"l0_counts{k}") for k in range(4)]
            keys_set, keys_hot, counted, counted_sb, piled, iota_set, sp_turn = (
                sem(f"l0_{n}") for n in ("keys_set", "keys_hot", "counted", "counted_sb", "piled", "iota_set", "sp_turn"))
            PILES = SUB + 1
            iota_k = sb("l0_iota_k", [128, KEYS], fp16, c)
            keys = sb("l0_keys", [128, 2, 2, SUB], ctx=c)
            hot_lane = sb("l0_hot_lane", [128, 2, SUB, LANES], bf16, c)
            hot_key = sb("l0_hot_key", [128, 2, SUB, KEYS], bf16, c)
            chunk_counts = sb("l0_chunk_counts", [128, 4, SUB - 1, KEYS], bf16, c)
            win_counts = sb("l0_win_counts", [128, 4, (W + WC) * HI], bf16, c)
            gen = general_path(c, sem, "l0", 1 + D, dst_pad, [(tab_a, src_pad, rows[:, 0]), (tab_b, dst_pad, rows[:, 1])], msg[:, 0], ps_s)
            gen_att, gen_turned, gen_turned_sb, gen_hidden, gen_hidden_sb, gen_product = (
                sem(f"l0_gen_{n}") for n in ("att", "turned", "turned_sb", "hidden", "hidden_sb", "product"))
            block = c.enter_context(stage_block(own))
            att_dram = P["edge_attr_32"]

            @block.sync
            def _(sp):
                for k in range(4):
                    sp.dma_start(w_ew[0:DE, k, :], P["L0_gnn_W_m1"][2 * D:2 * D + DE, :]).then_inc(w_loaded, 16)

                def general():
                    def load(g):
                        if isinstance(g, int):
                            sp.dma_start(att[0:TROWS, 0], att_dram[(NG - 1) * GE:E - TLEFT, :].rearrange("(p s) f -> p s f", s=SUB)).then_inc(gen_att, 16)
                            sp.dma_start(att[TROWS:TROWS + 1, 0, 0:TLEFT], att_dram[E - TLEFT:E, :].unsqueeze(0)).then_inc(gen_att, 16)
                        else:
                            sp.dma_start(att[:, 0].rearrange("p s f -> p (s f)"), group_rows(att_dram, g)).then_inc(gen_att, 16)
                    gen.sync(sp, load)

                def windows():
                    def step(i, k):
                        g = i * 4 + k
                        _, (start, start_write) = nc.values_load_multi_w_load_instructions(
                            starts_2[0:1, bass.ds(g, 1), :].rearrange("a g s -> a (g s)"), engines=[mybir.EngineType.SP],
                            min_val=0, max_val=N, skip_runtime_bounds_check_because=SAFE)
                        g = sp.snap(g) if not isinstance(g, int) else g
                        sp.wait_ge(hidden, done(g - 4))
                        sp.dma_start(idx[:, k, :], group_rows(src_pad.unsqueeze(1), g)).then_inc(s_idx[k], 16)
                        if isinstance(i, int) and g == NG - 1:
                            sp.dma_start(att[0:TROWS, k], att_dram[(NG - 1) * GE:E - TLEFT, :].rearrange("(p s) f -> p s f", s=SUB)).then_inc(s_att[k], 16)
                            sp.dma_start(att[TROWS:TROWS + 1, k, 0:TLEFT], att_dram[E - TLEFT:E, :].unsqueeze(0)).then_inc(s_att[k], 16)
                        else:
                            sp.dma_start(att[:, k].rearrange("p s f -> p (s f)"), group_rows(att_dram, g)).then_inc(s_att[k], 16)
                        sp.dma_start(w_ew[DE:DE + W, k, :], tab_b[bass.ds(start, W), :]).then_inc(s_win[k], 16)
                        if not isinstance(g, int) or g >= LAG:
                            write(i - 1 - (LAG - 1 - k) // 4, (k - LAG) % 4, start_write)

                    def write(i, k, start=None):
                        if start is None:
                            start = sp.value_load(base[0:1, bass.ds(i * 4 + k, 1)], min_val=0, max_val=N)
                        sp.wait_ge(piled, (i * 4 + k) * PILES + PILES)
                        if not isinstance(i, int) or i or k:
                            sp.sem_inc(sp_turn, 1)
                            sp.wait_ge(s_counts[(k - 1) % 4], (i + 1 if k else i) * 16)
                        sp.dma_start(counts[:, bass.ds(start, W), :].rearrange("p d h -> p (d h)"), win_counts[:, k, 0:W * HI]).then_inc(s_counts[k], 16)
                    for i in range(3):
                        for k in range(4):
                            step(i, k)
                    with sp.Fori(3, NG // 4) as i:
                        for k in range(4):
                            step(i, k)
                    for k in range(NG % 4):
                        step(NG // 4, k)
                    for g in range(NG - LAG, NG):
                        write(g // 4, g % 4)
                    sp.wait_ge(s_counts[(NG - 1) % 4], ((NG - 1) // 4 + 1) * 16)

                by_flag(sp, general, windows)

            @block.gpsimd
            def _(pool):
                pool.memset(win_counts[:, :, :], 0.0).then_inc(iota_set, 1)
                pool.iota(iota_k[:, :], pattern=[[1, KEYS]], base=0, channel_multiplier=0,
                          allow_small_or_imprecise_dtypes=True).then_inc(iota_set, 1)

                def general():
                    gen.gpsimd(pool)

                def windows():
                    def step(i, k):
                        pool.wait_ge(s_idx[k], (i + 1) * 16)
                        pool.sem_inc(pool_turn, 1)
                        for s in range(SUB):
                            nc.gpsimd.indirect_dma_start(
                                out=rows[:, k, s, :], out_offset=None, in_=tab_a,
                                in_offset=bass.IndirectOffsetOnAxis(ap=idx[:, k, s:s + 1], axis=0)).then_inc(s_rows[k], 16)
                    rounds(pool, step, NG, 4)

                by_flag(pool, general, windows)

            @block.vector
            def _(dve):
                nc.vector.memset(msg[:, :, :, 0:1], 1.0)
                nc.vector.memset(hid[64:128, :, :], 1.0).then_inc(cleared, 1)
                def general():
                    gen.vector(dve)

                def windows():
                    for s_ in (combined, added, keys_set, keys_hot):
                        dve.sem_inc(s_, CR)
                    dve.wait_ge(iota_set, 2)

                    def combine(i, k):
                        i, k = i + k // 4, k % 4
                        g = i * 4 + k
                        nc.vector.tensor_tensor(comb[:, k, :, DE:DE + W], iota_w[:, :, :],
                                                bc_last(rel[:, bass.ds(g, 1), :].rearrange("p a s -> p (a s)"), W), ALU.is_equal)
                        last = isinstance(i, int) and g == NG - 1
                        dve.wait_ge(s_att[k], (i + 1 + last) * 16)
                        nc.vector.tensor_copy(comb[:, k, :, 0:DE], att[:, k]).then_inc(combined, 1)

                    def take_keys(i, k):
                        i, k = i + k // 4, k % 4
                        g = i * 4 + k
                        if not isinstance(g, int) or g >= 2:
                            dve.wait_ge(counted, done((g - 1) * 2 - 1))
                        nc.vector.tensor_copy(keys[:, k % 2], group_of(lane_key, g)).then_inc(keys_set, 1)

                    def heat(i, k, s):
                        i, k = i + k // 4, k % 4
                        g = i * 4 + k
                        if s == 0:
                            dve.wait_ge(keys_set, done(g))
                        nc.vector.tensor_scalar(hot_lane[:, k % 2, s, :], iota_k[:, 0:LANES], keys[:, k % 2, 0, s:s + 1], None, ALU.is_equal)
                        last = nc.vector.tensor_scalar(hot_key[:, k % 2, s, :], iota_k[:, :], keys[:, k % 2, 1, s:s + 1], None, ALU.is_equal)
                        if s == SUB - 1:
                            last.then_inc(keys_hot, 1)

                    def moves_of(g):
                        _, values = nc.values_load_multi_w_load_instructions(
                            moves[0:1, bass.ds(g, 1), :].rearrange("a g s -> a (g s)"), engines=[mybir.EngineType.DVE],
                            min_val=0, max_val=max(N, (W - 1) * HI), skip_runtime_bounds_check_because=SAFE)
                        in_window = [nc.s_assert_within(v, 0, (W - 1) * HI, skip_runtime_bounds_check_because=SAFE) for v in values[0:SUB]]
                        return in_window[0:SUB - 1], in_window[SUB - 1], nc.s_assert_within(values[SUB], 0, N, skip_runtime_bounds_check_because=SAFE)

                    def clear(i, k):
                        g = i * 4 + k
                        if not isinstance(i, int) or i:
                            dve.wait_ge(s_counts[k], i * 16)
                        nc.vector.memset(win_counts[:, k, KEYS:W * HI], 0.0).then_inc(piled, 1)

                    def pile(i, k, s, moved):
                        g = i * 4 + k
                        if s == 1:
                            dve.wait_ge(counted_sb, done(g * 2 + 1))
                        dve.wait_ge(piled, g * PILES + s)
                        if s < SUB:
                            to = win_counts[:, k, bass.ds(moved[0][s - 1], KEYS)]
                            nc.vector.tensor_tensor(to, to, chunk_counts[:, k, s - 1, :], ALU.add).then_inc(piled, 1)
                        elif isinstance(g, int) and g == 0:
                            dve.sem_inc(piled, 1)
                        else:
                            nc.vector.tensor_tensor(win_counts[:, k, 0:HI], win_counts[:, k, 0:HI],
                                                    win_counts[:, (k - 1) % 4, bass.ds(moved[1], HI)], ALU.add).then_inc(piled, 1)

                    def step(i, k):
                        g = i * 4 + k
                        loop = not isinstance(i, int)
                        before = (i, k - 1) if k else (i - 1, 3)
                        pile_up, next_one = loop or g >= 1, loop or g + 1 < NG
                        if next_one:
                            take_keys(i, k + 1)
                        if pile_up:
                            clear(*before)
                            moved = moves_of(g - 1)
                            start = moved[2]
                        else:
                            start = dve.value_load(base[0:1, 0:1], min_val=0, max_val=N)
                        dve.wait_ge(summed, done(g))
                        nc.vector.tensor_tensor(acc[:, bass.ds(start, W)], acc[:, bass.ds(start, W)], ps_s[0:D + 1, 0:W], ALU.add).then_inc(added, 1)
                        if loop or g + 4 < NG:
                            combine(i, k + 4)
                        for s in range(SUB):
                            if next_one:
                                heat(i, k + 1, s)
                            if pile_up:
                                pile(*before, s + 1, moved)

                    for k in range(4):
                        combine(0, k)
                    take_keys(0, 0)
                    for s in range(SUB):
                        heat(0, 0, s)
                    for i in range(2):
                        for k in range(4):
                            step(i, k)
                    with dve.Fori(2, (NG - 4) // 4) as i:
                        for k in range(4):
                            step(i, k)
                    for k in range(NG - (NG - 4) // 4 * 4):
                        step((NG - 4) // 4 + k // 4, k % 4)
                    moved = moves_of(NG - 1)
                    clear((NG - 1) // 4, (NG - 1) % 4)
                    for s in range(SUB):
                        pile((NG - 1) // 4, (NG - 1) % 4, s + 1, moved)

                by_flag(dve, general, windows)

            @block.tensor
            def _(pe):
                pe.wait_ge(w_loaded, 64)
                pe.wait_ge(cleared, 1)
                def general():
                    def make(g):
                        pe.wait_ge(gen_att, (g + 1 + isinstance(g, int)) * 16)
                        pe.sem_inc(pe_turn, 1)
                        for s in range(SUB):
                            last = nc.tensor.transpose(ps_t[0][0:DE, s * 128:(s + 1) * 128], att[:, 0, s, :], ident[:, :])
                        last.then_inc(gen_turned, 1)
                        pe.wait_ge(gen_turned_sb, g + 1)
                        pe.wait_ge(gen.gathered, (g + 1) * gen.rows_in)
                        pe.sem_inc(pe_turn, 1)
                        nc.tensor.matmul(ps_h[0][0:H, :], w_ew[0:DE, 0, :], comb_t[0:DE, 0, :], start=True, stop=False)
                        for n in range(2):
                            for s in range(SUB):
                                last = nc.tensor.matmul(ps_h[0][0:H, s * 128:(s + 1) * 128], rows[:, n, s, :], ident[:, :],
                                                        start=False, stop=n == 1 and s == SUB - 1)
                        last.then_inc(gen_hidden, 1)
                        pe.wait_ge(gen_hidden_sb, g + 1)
                        for s in range(SUB):
                            last = nc.tensor.matmul(ps_m[:, s * D:(s + 1) * D], hid[0:H + 1, 0, s * 128:(s + 1) * 128],
                                                    w_m2[:, :], start=True, stop=True)
                        last.then_inc(gen_product, 1)
                    gen.tensor(pe, make)

                def windows():
                    for s_ in (turned, hidden, message, summed, counted):
                        pe.sem_inc(s_, CR)

                    def count(i, k, half):
                        g = i * 4 + k
                        if half == 0:
                            pe.wait_ge(keys_hot, done(g))
                        pe.wait_ge(counted_sb, done(g * 2 + half - 1))
                        for s in range(2):
                            last = nc.tensor.matmul(ps_c[:, s, 0:KEYS], hot_lane[:, k % 2, half * 2 + s, :], hot_key[:, k % 2, half * 2 + s, :], start=True, stop=True)
                        last.then_inc(counted, 1)

                    def turn(i, k):
                        i, k = i + k // 4, k % 4
                        g = i * 4 + k
                        pe.wait_ge(combined, done(g))
                        pe.wait_ge(turned_sb, done(g - 2))
                        pe.sem_inc(pe_turn, 1)
                        for s in range(SUB):
                            last = nc.tensor.transpose(ps_t[k % 2][0:DE + W, s * 128:(s + 1) * 128], comb[:, k, s, :], ident[:, :])
                        last.then_inc(turned, 1)

                    def hide(i, k, between=lambda: None):
                        i, k = i + k // 4, k % 4
                        g = i * 4 + k
                        pe.wait_ge(turned_sb, done(g))
                        pe.wait_ge(hidden_sb, done(g - 2))
                        pe.wait_ge(s_win[k], (i + 1) * 16)
                        nc.tensor.matmul(ps_h[k % 2][0:H, :], w_ew[:, k, :], comb_t[:, k % 2, :], start=True, stop=False)
                        between()
                        pe.wait_ge(s_rows[k], (i + 1) * 64)
                        for s in range(SUB):
                            last = nc.tensor.matmul(ps_h[k % 2][0:H, s * 128:(s + 1) * 128], rows[:, k, s, :], ident[:, :],
                                                    start=False, stop=s == SUB - 1)
                        last.then_inc(hidden, 1)

                    def messages(i, k):
                        i, k = i + k // 4, k % 4
                        g = i * 4 + k
                        pe.wait_ge(hidden_sb, done(g))
                        pe.wait_ge(message_sb, done(g - 1))
                        for s in range(SUB):
                            last = nc.tensor.matmul(ps_m[:, s * D:(s + 1) * D], hid[0:H + 1, k % 2, s * 128:(s + 1) * 128],
                                                    w_m2[:, :], start=True, stop=True)
                        last.then_inc(message, 1)

                    def sums(i, k):
                        g = i * 4 + k
                        pe.wait_ge(message_sb, done(g))
                        pe.wait_ge(added, done(g - 1))
                        for s in range(SUB):
                            last = nc.tensor.matmul(ps_s[0:D + 1, 0:W], msg[:, k % 2, s, :], comb[:, k, s, DE:DE + W],
                                                    start=s == 0, stop=s == SUB - 1)
                        last.then_inc(summed, 1)

                    for n in range(3):
                        turn(0, n)
                        if n >= 1:
                            hide(0, n - 1)
                        if n >= 2:
                            messages(0, n - 2)

                    def step(i, k):
                        g = i * 4 + k
                        loop = not isinstance(i, int)
                        sums(i, k)
                        count(i, k, 0)
                        if loop or g + 1 < NG:
                            messages(i, k + 1)
                        if loop or g + 2 < NG:
                            hide(i, k + 2, lambda: count(i, k, 1))
                        else:
                            count(i, k, 1)
                        if loop or g + 3 < NG:
                            turn(i, k + 3)
                    rounds(pe, step, NG, 4)

                by_flag(pe, general, windows)

            @block.scalar
            def _(act):
                act.wait_ge(cleared, 1)
                def general():
                    def step(g):
                        act.wait_ge(gen_turned, g + 1)
                        nc.scalar.copy(comb_t[0:DE, 0, :], ps_t[0][0:DE, :]).then_inc(gen_turned_sb, 1)
                        act.wait_ge(gen_hidden, g + 1)
                        nc.scalar.activation(hid[0:H, 0, :], ps_h[0][0:H, :], ACT.Gelu, bias=b_m1[:, :]).then_inc(gen_hidden_sb, 1)
                        act.wait_ge(gen_product, g + 1)
                        nc.scalar.activation(msg[:, 0, :, 1:1 + D], ps_m[:, 0:SUB * D].rearrange("p (s f) -> p s f", s=SUB),
                                             ACT.Gelu).then_inc(gen.message, 1)
                    gen.each_group(act, step)

                def windows():
                    for s_ in (turned_sb, hidden_sb, message_sb, counted_sb):
                        act.sem_inc(s_, CR)

                    def copy_counts(i, k, half):
                        g = i * 4 + k
                        act.wait_ge(counted, done(g * 2 + half))
                        if half == 0:
                            if not isinstance(g, int) or g >= 4:
                                act.wait_ge(s_counts[k], i * 16)
                                act.wait_ge(piled, (g - 3) * PILES + PILES)
                            nc.scalar.copy(win_counts[:, k, 0:KEYS], ps_c[:, 0, 0:KEYS])
                            nc.scalar.copy(chunk_counts[:, k, 0, :], ps_c[:, 1, 0:KEYS]).then_inc(counted_sb, 1)
                        else:
                            nc.scalar.copy(chunk_counts[:, k, 1:SUB - 1, :], ps_c[:, :, 0:KEYS]).then_inc(counted_sb, 1)

                    def copy_turned(i, k):
                        g = i * 4 + k
                        act.wait_ge(turned, done(g))
                        act.wait_ge(hidden, done(g - 2))
                        nc.scalar.copy(comb_t[:, k % 2, :], ps_t[k % 2][0:DE + W, :]).then_inc(turned_sb, 1)

                    def gelu_hidden(i, k):
                        g = i * 4 + k
                        act.wait_ge(hidden, done(g))
                        act.wait_ge(message, done(g - 2))
                        nc.scalar.activation(hid[0:H, k % 2, :], ps_h[k % 2][0:H, :], ACT.Gelu, bias=b_m1[:, :]).then_inc(hidden_sb, 1)

                    def gelu_message(i, k):
                        g = i * 4 + k
                        act.wait_ge(message, done(g))
                        act.wait_ge(summed, done(g - 2))
                        nc.scalar.activation(msg[:, k % 2, :, 1:1 + D], ps_m[:, 0:SUB * D].rearrange("p (s f) -> p s f", s=SUB),
                                             ACT.Gelu).then_inc(message_sb, 1)

                    for n in range(3):
                        copy_turned(0, n)
                        if n >= 1:
                            gelu_hidden(0, n - 1)
                        if n >= 2:
                            gelu_message(0, n - 2)

                    def step(i, k):
                        g = i * 4 + k
                        loop = not isinstance(i, int)
                        copy_counts(i, k, 0)
                        if loop or g + 1 < NG:
                            gelu_message(i, k + 1)
                        copy_counts(i, k, 1)
                        if loop or g + 2 < NG:
                            gelu_hidden(i, k + 2)
                        if loop or g + 3 < NG:
                            copy_turned(i, k + 3)
                    peeled(act, step, NG, 4)

                by_flag(act, general, windows)

        def layer_norm(dve, act_done, act_turn, link, z, mid, sums, squares):
            link(nc.vector.tensor_reduce(sums, z, AX.X, ALU.add))
            link(nc.vector.tensor_scalar(sums, sums, 1.0 / D, None, ALU.mult))
            link(nc.vector.tensor_tensor(z, z, bc_last(sums, D), ALU.subtract))
            link(nc.vector.tensor_tensor(mid, z, z, ALU.mult))
            link(nc.vector.tensor_reduce(squares, mid, AX.X, ALU.add))
            nc.vector.tensor_scalar(squares, squares, 1.0 / D, EPS, ALU.mult, ALU.add).then_inc(act_turn, 1)
            dve.wait_ge(act_done, 1)
            link(nc.vector.reciprocal(squares, squares))
            link(nc.vector.tensor_tensor(z, z, bc_last(squares, D), ALU.mult))

        def flat(ap):
            return ap.rearrange("p t j f -> p (t j) f")

        def block_of(ap, t):
            return ap[:, bass.ds(t, 1)].rearrange("p a j f -> p (a j) f")

        def per_node(ap, t):
            return ap[:, bass.ds(t, 1)].rearrange("p a j -> p (a j)")

        def strided(ap):
            return ap.rearrange("r (p j) -> r j p", j=SUB)

        def halves(ap):
            return ap.rearrange("r (j p) -> r j p", j=SUB)

        with ExitStack() as c:
            sem, own = stage_semaphores(c, "n0_")
            staged, turned, turned_sb, hidden, hidden_sb, product, product_sb, summed = (
                sem(n) for n in ("staged", "turned", "turned_sb", "hidden", "hidden_sb", "product", "product_sb", "summed"))
            pe_turn, ones_set, chain, root_in, root_out, s_cnt = sem("pe_turn"), sem("ones_set"), sem("chain"), sem("root_in"), sem("root_out"), sem("cnt")
            top_lanes, top_all = sem("top_lanes"), sem("top_all")
            top = sb("n0_top", [128, 1], ctx=c)
            xs = sb("n0_xs", [128, 2, SUB, D], ctx=c)
            xts = sb("n0_xts", [D, 2, GE], ctx=c)
            hid = sb("n0_hid", [HC + 1, 2, GE], ctx=c)
            comb = sb("n0_comb", [128, 2, SUB, D], ctx=c)
            sums, squares = sb("n0_sums", [128, NT * SUB], ctx=c), sb("n0_squares", [128, NT * SUB], ctx=c)
            mid = sb("n0_mid", [128, NT * SUB, D], ctx=c)
            ps_t = [c.enter_context(nc.psum_tensor(f"n0_t{k}", [128, 512], fp32)) for k in range(2)]
            ps_h = [c.enter_context(nc.psum_tensor(f"n0_h{k}", [128, 512], fp32)) for k in range(2)]
            ps_p = [c.enter_context(nc.psum_tensor(f"n0_p{k}", [128, 512], fp32)) for k in range(2)]
            block = c.enter_context(stage_block(own))

            @block.sync
            def _(sp):
                sp.dma_start(cnt_dram.unsqueeze(0), acc[0:1, :]).then_inc(s_cnt, 16)
                sp.wait_ge(s_cnt, 16)
                sp.dma_start(cnt_nm[:, :, :], cnt_dram.rearrange("(t p j) -> p t j", p=LANES, j=SUB)).then_inc(s_cnt, 16)
                sp.wait_ge(s_cnt, 32)

            @block.tensor
            def _(pe):
                for s_ in (turned, hidden, product):
                    pe.sem_inc(s_, CR)
                pe.wait_ge(ones_set, 1)

                def turn(i, k):
                    i, k = i + k // 2, k % 2
                    t = i * 2 + k
                    pe.wait_ge(staged, done(t))
                    pe.wait_ge(turned_sb, done(t - 2))
                    pe.sem_inc(pe_turn, 1)
                    for j in range(SUB):
                        last = nc.tensor.transpose(ps_t[k][0:D, j * 128:(j + 1) * 128], xs[:, k, j, :], ident[:, :])
                    last.then_inc(turned, 1)
                turn(0, 0)

                def step(i, k):
                    t = i * 2 + k
                    if not isinstance(i, int) or t + 1 < NT:
                        turn(i, k + 1)
                    pe.wait_ge(hidden_sb, done(t - 2))
                    nc.tensor.matmul(ps_h[k][0:HC, :], w_c1a[:, :], strided(acc[:, bass.ds(t * GE, GE)]), start=True, stop=False)
                    pe.wait_ge(turned_sb, done(t))
                    nc.tensor.matmul(ps_h[k][0:HC, :], w_c1x[:, :], xts[:, k, :], start=False, stop=True).then_inc(hidden, 1)
                    pe.wait_ge(hidden_sb, done(t))
                    pe.wait_ge(product_sb, done(t - 2))
                    for j in range(SUB):
                        last = nc.tensor.matmul(ps_p[k][:, j * D:(j + 1) * D], hid[:, k, j * 128:(j + 1) * 128], w_c2[:, :], start=True, stop=True)
                    last.then_inc(product, 1)
                rounds(pe, step, NT, 2)

            @block.scalar
            def _(act):
                for s_ in (turned_sb, hidden_sb, product_sb):
                    act.sem_inc(s_, CR)

                def copy_turned(i, k):
                    i, k = i + k // 2, k % 2
                    t = i * 2 + k
                    act.wait_ge(turned, done(t))
                    act.wait_ge(hidden, done(t - 2))
                    nc.scalar.copy(xts[:, k, :], ps_t[k][0:D, :]).then_inc(turned_sb, 1)
                copy_turned(0, 0)

                def step(i, k):
                    t = i * 2 + k
                    if not isinstance(i, int) or t + 1 < NT:
                        copy_turned(i, k + 1)
                    act.wait_ge(hidden, done(t))
                    act.wait_ge(product, done(t - 2))
                    nc.scalar.activation(hid[0:HC, k, :], ps_h[k][0:HC, :], ACT.Gelu, bias=b_c1[:, :]).then_inc(hidden_sb, 1)
                    act.wait_ge(product, done(t))
                    act.wait_ge(summed, done(t - 2))
                    nc.scalar.activation(comb[:, k].rearrange("p j f -> p (j f)"), ps_p[k][:, 0:SUB * D], ACT.Gelu).then_inc(product_sb, 1)
                rounds(act, step, NT, 2)
                act.wait_ge(root_in, 1)
                nc.scalar.activation(squares[:, :], squares[:, :], ACT.Sqrt).then_inc(root_out, 1)
                act.wait_ge(root_in, 2)
                nc.scalar.activation(dinv_nm[:, :, :], dinv_nm[:, :, :], ACT.Sqrt).then_inc(root_out, 1)

            @block.vector
            def _(dve):
                link = linker(dve, chain)
                nc.vector.memset(hid[HC:HC + 1, :, :], 1.0).then_inc(ones_set, 1)
                dve.sem_inc(staged, CR)
                dve.sem_inc(summed, CR)

                def stage_x(i, k):
                    i, k = i + k // 2, k % 2
                    t = i * 2 + k
                    dve.wait_ge(turned, done(t - 2))
                    nc.vector.tensor_copy(xs[:, k], block_of(x_nm, t)).then_inc(staged, 1)
                stage_x(0, 0)

                def step(i, k):
                    t = i * 2 + k
                    if not isinstance(i, int) or t + 1 < NT:
                        stage_x(i, k + 1)
                    dve.wait_ge(product_sb, done(t))
                    nc.vector.scalar_tensor_tensor(out=block_of(z_nm, t), in0=block_of(x_nm, t), scalar=2.0, in1=comb[:, k],
                                                   op0=ALU.mult, op1=ALU.add).then_inc(summed, 1)
                rounds(dve, step, NT, 2)
                dve.wait_ge(summed, done(NT - 1))
                layer_norm(dve, root_out, root_in, link, flat(z_nm), mid[:, :, :], sums[:, :], squares[:, :])
                dve.wait_ge(s_cnt, 32)
                nc.vector.tensor_scalar(dinv_nm[:, :, :], cnt_nm[:, :, :], 1.0, None, ALU.add).then_inc(root_in, 1)
                dve.wait_ge(root_out, 2)
                link(nc.vector.reciprocal(dinv_nm[:, :, :], dinv_nm[:, :, :]))
                nc.vector.tensor_reduce(top[:, :], cnt_nm[:, :, :].rearrange("p t j -> p (t j)"), AX.X, ALU.max).then_inc(top_lanes, 1)
                dve.wait_ge(top_all, 1)
                link(nc.vector.tensor_scalar(top[:, :], top[:, :], float(DEG_MAX), None, ALU.is_gt))
                link(nc.vector.tensor_tensor(flag_f[:, :], flag_f[:, :], top[0:1, :], ALU.max))
                nc.vector.tensor_copy(flag[:, :], flag_f[:, :])

            @block.gpsimd
            def _(pool):
                pool.wait_ge(top_lanes, 1)
                pool.partition_all_reduce(top[:, :], top[:, :], 128, bass.bass_isa.ReduceOp.max).then_inc(top_all, 1)

        dinv_ctx = ExitStack()
        whole.enter_context(dinv_ctx)
        dinv_bc = sb("dinv_bc", [128, NP], ctx=dinv_ctx)
        with ExitStack() as c:
            sem, own = stage_semaphores(c, "g1_")
            made, turned, in_acc, stored, pe_turn = (sem(n) for n in ("made", "turned", "in_acc", "stored", "pe_turn"))
            s_store = [sem(f"store{k}") for k in range(2)]
            s_cnt, deg_ready, root = sem("cnt"), sem("deg_ready"), sem("root")
            ys = sb("g1_ys", [128, 2, SUB, D], ctx=c)
            ps_y = [c.enter_context(nc.psum_tensor(f"g1_y{k}", [128, 512], fp32)) for k in range(2)]
            block = c.enter_context(stage_block(own))

            @block.sync
            def _(sp):
                sp.sem_inc(stored, CR)
                sp.dma_start(dinv_bc[:, :], cnt_dram.unsqueeze(0).to_broadcast([128, NP])).then_inc(s_cnt, 16)

                def step(i, k):
                    t = sp.snap(i * 2 + k) if not isinstance(i, int) else i * 2 + k
                    sp.wait_ge(made, done(t))
                    sp.dma_start(group_rows(tab_y1, t), ys[:, k].rearrange("p j f -> p (j f)")).then_inc(s_store[k], 16)
                    sp.wait_ge(s_store[k], (i + 1) * 16)
                    sp.sem_inc(stored, 1)
                rounds(sp, step, NT, 2)

            @block.vector
            def _(dve):
                dve.sem_inc(made, CR)

                def step(i, k):
                    t = i * 2 + k
                    dve.wait_ge(turned, done(t - 2))
                    dve.wait_ge(stored, done(t - 2))
                    nc.vector.tensor_tensor(ys[:, k], block_of(z_nm, t), bc_last(per_node(dinv_nm, t), D), ALU.mult).then_inc(made, 1)
                rounds(dve, step, NT, 2)
                dve.wait_ge(s_cnt, 16)
                nc.vector.tensor_scalar(dinv_bc[:, :], dinv_bc[:, :], 1.0, None, ALU.add).then_inc(deg_ready, 1)
                dve.wait_ge(root, 1)
                nc.vector.reciprocal(dinv_bc[:, :], dinv_bc[:, :])

            @block.tensor
            def _(pe):
                pe.sem_inc(turned, CR)

                def step(i, k):
                    t = i * 2 + k
                    pe.wait_ge(made, done(t))
                    pe.wait_ge(in_acc, done(t - 2))
                    pe.sem_inc(pe_turn, 1)
                    for j in range(SUB):
                        last = nc.tensor.transpose(ps_y[k][0:D, j * 128:(j + 1) * 128], ys[:, k, j, :], ident[:, :])
                    last.then_inc(turned, 1)
                rounds(pe, step, NT, 2)

            @block.scalar
            def _(act):
                act.sem_inc(in_acc, CR)

                def step(i, k):
                    t = i * 2 + k
                    act.wait_ge(turned, done(t))
                    nc.scalar.copy(strided(acc[0:D, bass.ds(t * GE, GE)]), halves(ps_y[k][0:D, :])).then_inc(in_acc, 1)
                rounds(act, step, NT, 2)
                act.wait_ge(deg_ready, 1)
                nc.scalar.activation(dinv_bc[:, :], dinv_bc[:, :], ACT.Sqrt).then_inc(root, 1)

        def split(link, whole_, parts, rest):
            link(nc.vector.tensor_copy(parts[0], whole_))
            link(nc.vector.tensor_tensor(rest, whole_, parts[0], ALU.subtract))
            link(nc.vector.tensor_copy(parts[1], rest))
            link(nc.vector.tensor_tensor(rest, rest, parts[1], ALU.subtract))
            link(nc.vector.tensor_copy(parts[2], rest))

        def gcn_sums(name, tab, half):
            with ExitStack() as c:
                sem, own = stage_semaphores(c, f"{name}_")
                s_y, split_done, chain, summed, added, reduced = (sem(n) for n in ("s_y", "split_done", "chain", "summed", "added", "reduced"))
                s_block = [sem(f"block{k}") for k in range(2)]
                y_top = sb(f"{name}_y_top", [128, HI, 2, D], bf16, c)
                y_low = sb(f"{name}_y_low", [128, HI, D], bf16, c)
                middle = sb(f"{name}_middle", [D, 2, DB], ctx=c)
                block_counts = sb(f"{name}_block_counts", [128, 2, DB, HI], bf16, c)
                block_deg = sb(f"{name}_block_deg", [128, HI], ctx=c)
                rows = sb(f"{name}_rows", [128, SUB, D], ctx=c)
                ps = [c.enter_context(nc.psum_tensor(f"{name}_ps{k}", [128, 512], fp32)) for k in range(2)]
                ps_low = [c.enter_context(nc.psum_tensor(f"{name}_ps_low{k}", [128, 512], fp32)) for k in range(2)]
                middle_sb, partly, sp_turn = sem("middle_sb"), sem("partly"), sem("sp_turn")
                gen = general_path(c, sem, name, D, dst_pad, [(tab, src_pad, rows[:, :, :])], rows, ps[0])
                block = c.enter_context(stage_block(own))

                @block.sync
                def _(sp):
                    def general():
                        gen.sync(sp)

                    def dense():
                        sp.sem_inc(s_y, 1)
                        sp.dma_start(x_nm[:, :, :, :].rearrange("p t j f -> p t (j f)"),
                                     tab[0:NP, :].rearrange("(t p j) f -> p t (j f)", p=LANES, j=SUB)).then_inc(s_y, 16)

                        def step(i, k):
                            b = sp.snap(i * 2 + k) if not isinstance(i, int) else i * 2 + k
                            sp.wait_ge(summed, done(b - 2))
                            sp.sem_inc(sp_turn, 1)
                            sp.wait_ge(reduced, done(b - 2))
                            sp.dma_start(block_counts[:, k].rearrange("p d h -> p (d h)"),
                                         destinations(b, DB)).then_inc(s_block[k], 16)
                        rounds(sp, step, NDB, 2)

                    by_flag(sp, general, dense)

                @block.gpsimd
                def _(pool):
                    by_flag(pool, lambda: gen.gpsimd(pool), lambda: pool.sem_inc(gen.turn, 1))

                @block.vector
                def _(dve):
                    def general():
                        gen.vector(dve)

                    def dense():
                        link = linker(dve, chain)
                        for s_ in (added, reduced):
                            dve.sem_inc(s_, CR)
                        if half == 0:
                            link(nc.vector.memset(deg_nm[:, :], 0.0))
                        dve.wait_ge(s_y, 17)
                        y = flat(x_nm)
                        split(link, y, [y_top[:, :, 0, :], y_top[:, :, 1, :], y_low[:, :, :]], y)
                        dve.sem_inc(split_done, 1)

                        def step(i, k):
                            b = i * 2 + k
                            reduce(i, k)
                            dve.wait_ge(summed, done(b))
                            at = acc[0:D, bass.ds(b * DB, DB)]
                            nc.vector.tensor_tensor(at, at, ps[k][0:D, 0:DB], ALU.add).then_inc(partly, 1)
                            dve.wait_ge(partly, 2 * b + 1)
                            nc.vector.tensor_tensor(at, at, ps_low[k][0:D, 0:DB], ALU.add).then_inc(partly, 1)
                            dve.wait_ge(middle_sb, done(b))
                            dve.wait_ge(partly, 2 * b + 2)
                            nc.vector.tensor_tensor(at, at, middle[:, k, :], ALU.add).then_inc(added, 1)
                            dve.wait_ge(added, done(b))

                        def reduce(i, k):
                            dve.wait_ge(s_block[k], (i + 1) * 16)
                            nc.vector.tensor_reduce(block_deg[:, :], block_counts[:, k, half * (DB // 2):(half + 1) * (DB // 2)].rearrange("p d h -> p h d"), AX.X, ALU.add).then_inc(reduced, 1)
                            dve.wait_ge(reduced, done(i * 2 + k))
                            nc.vector.tensor_tensor(deg_nm[:, :], deg_nm[:, :], block_deg[:, :], ALU.add)
                        rounds(dve, step, NDB, 2)

                    by_flag(dve, general, dense)

                @block.scalar
                def _(act):
                    def general():
                        act.sem_inc(middle_sb, 1)

                    def dense():
                        act.sem_inc(middle_sb, CR)

                        def step(i, k):
                            b = i * 2 + k
                            act.wait_ge(summed, done(b))
                            act.wait_ge(added, done(b - 2))
                            nc.scalar.copy(middle[:, k, :], ps[k][D:2 * D, 0:DB]).then_inc(middle_sb, 1)
                        rounds(act, step, NDB, 2)

                    by_flag(act, general, dense)

                @block.tensor
                def _(pe):
                    def general():
                        gen.tensor(pe)

                    def dense():
                        pe.sem_inc(summed, CR)
                        pe.wait_ge(split_done, 1)

                        def step(i, k):
                            b = i * 2 + k
                            pe.wait_ge(added, done(b - 2))
                            pe.wait_ge(s_block[k], (i + 1) * 16)
                            for h in range(HI):
                                nc.tensor.matmul(ps[k][:, 0:DB], y_top[:, h].rearrange("p q f -> p (q f)"), block_counts[:, k, :, h],
                                                 start=h == 0, stop=h == HI - 1)
                                last = nc.tensor.matmul(ps_low[k][0:D, 0:DB], y_low[:, h, :], block_counts[:, k, :, h],
                                                        start=h == 0, stop=h == HI - 1)
                            last.then_inc(summed, 1)
                        rounds(pe, step, NDB, 2)

                    by_flag(pe, general, dense)


        gcn_sums("gs1", tab_y1, 0)

        with ExitStack() as c:
            sem, own = stage_semaphores(c, "g2_")
            wide, scaled, hidden, product, made, turned, in_acc, stored, pe_turn = (
                sem(n) for n in ("wide", "scaled", "hidden", "product", "made", "turned", "in_acc", "stored", "pe_turn"))
            s_store = [sem(f"store{k}") for k in range(2)]
            us = sb("g2_us", [H1, 2, GE], ctx=c)
            hid = sb("g2_hid", [H1, 2, GE], ctx=c)
            ys = sb("g2_ys", [128, 2, SUB, D], ctx=c)
            ps_u = [c.enter_context(nc.psum_tensor(f"g2_u{k}", [128, 512], fp32)) for k in range(2)]
            ps_p = [c.enter_context(nc.psum_tensor(f"g2_p{k}", [128, 512], fp32)) for k in range(2)]
            ps_y = [c.enter_context(nc.psum_tensor(f"g2_y{k}", [128, 512], fp32)) for k in range(2)]
            block = c.enter_context(stage_block(own))

            @block.tensor
            def _(pe):
                for s_ in (wide, product, turned):
                    pe.sem_inc(s_, CR)

                def step(i, k):
                    t = i * 2 + k
                    pe.wait_ge(scaled, done(t - 2))
                    nc.tensor.matmul(ps_u[k][0:H1, :], w_g1[:, :], acc[0:D, bass.ds(t * GE, GE)], start=True, stop=True).then_inc(wide, 1)
                    pe.wait_ge(hidden, done(t))
                    pe.wait_ge(made, done(t - 2))
                    for j in range(SUB):
                        last = nc.tensor.matmul(ps_p[k][:, j * D:(j + 1) * D], strided(hid[:, k, :])[:, j, :], w_g2[:, :], start=True, stop=True)
                    last.then_inc(product, 1)
                    pe.wait_ge(made, done(t))
                    pe.wait_ge(in_acc, done(t - 2))
                    pe.sem_inc(pe_turn, 1)
                    for j in range(SUB):
                        last = nc.tensor.transpose(ps_y[k][0:D, j * 128:(j + 1) * 128], ys[:, k, j, :], ident[:, :])
                    last.then_inc(turned, 1)
                rounds(pe, step, NT, 2)

            @block.vector
            def _(dve):
                dve.sem_inc(scaled, CR)
                dve.sem_inc(made, CR)

                def step(i, k):
                    t = i * 2 + k
                    dve.wait_ge(wide, done(t))
                    dve.wait_ge(hidden, done(t - 2))
                    nc.vector.tensor_tensor(us[:, k, :], ps_u[k][0:H1, :], dinv_bc[0:H1, bass.ds(t * GE, GE)], ALU.mult).then_inc(scaled, 1)
                    dve.wait_ge(product, done(t))
                    dve.wait_ge(turned, done(t - 2))
                    dve.wait_ge(stored, done(t - 2))
                    nc.vector.tensor_tensor(ys[:, k], ps_p[k][:, 0:SUB * D].rearrange("p (j f) -> p j f", j=SUB),
                                            bc_last(per_node(dinv_nm, t), D), ALU.mult).then_inc(made, 1)
                rounds(dve, step, NT, 2)

            @block.scalar
            def _(act):
                act.sem_inc(hidden, CR)
                act.sem_inc(in_acc, CR)

                def step(i, k):
                    t = i * 2 + k
                    act.wait_ge(scaled, done(t))
                    act.wait_ge(product, done(t - 2))
                    nc.scalar.activation(hid[:, k, :], us[:, k, :], ACT.Relu, bias=b_g1[:, :]).then_inc(hidden, 1)
                    act.wait_ge(turned, done(t))
                    nc.scalar.copy(strided(acc[0:D, bass.ds(t * GE, GE)]), halves(ps_y[k][0:D, :])).then_inc(in_acc, 1)
                rounds(act, step, NT, 2)

            @block.sync
            def _(sp):
                sp.sem_inc(stored, CR)

                def step(i, k):
                    t = sp.snap(i * 2 + k) if not isinstance(i, int) else i * 2 + k
                    sp.wait_ge(made, done(t))
                    sp.dma_start(group_rows(tab_y2, t), ys[:, k].rearrange("p j f -> p (j f)")).then_inc(s_store[k], 16)
                    sp.wait_ge(s_store[k], (i + 1) * 16)
                    sp.sem_inc(stored, 1)
                rounds(sp, step, NT, 2)

        gcn_sums("gs2", tab_y2, 1)

        with ExitStack() as c:
            sem, own = stage_semaphores(c, "g3_")
            scaled, turned, summed, pe_turn, chain, root_in, root_out = (
                sem(n) for n in ("scaled", "turned", "summed", "pe_turn", "chain", "root_in", "root_out"))
            us = sb("g3_us", [D, 2, GE], ctx=c)
            sums, squares = sb("g3_sums", [128, NT * SUB], ctx=c), sb("g3_squares", [128, NT * SUB], ctx=c)
            mid = sb("g3_mid", [128, NT * SUB, D], ctx=c)
            ps_z = [c.enter_context(nc.psum_tensor(f"g3_z{k}", [128, 512], fp32)) for k in range(2)]
            block = c.enter_context(stage_block(own))

            @block.vector
            def _(dve):
                link = linker(dve, chain)
                dve.sem_inc(scaled, CR)
                dve.sem_inc(summed, CR)

                def step(i, k):
                    t = i * 2 + k
                    dve.wait_ge(turned, done(t - 2))
                    nc.vector.tensor_tensor(us[:, k, :], acc[0:D, bass.ds(t * GE, GE)], dinv_bc[0:D, bass.ds(t * GE, GE)], ALU.mult).then_inc(scaled, 1)
                    dve.wait_ge(turned, done(t))
                    nc.vector.tensor_tensor(block_of(x_nm, t), ps_z[k][:, 0:SUB * D].rearrange("p (j f) -> p j f", j=SUB), block_of(z_nm, t), ALU.add).then_inc(summed, 1)
                rounds(dve, step, NT, 2)
                dve.wait_ge(summed, done(NT - 1))
                link(nc.vector.tensor_tensor(flat(x_nm), flat(x_nm), b_g2[:, :].unsqueeze(1).to_broadcast([128, NT * SUB, D]), ALU.add))
                layer_norm(dve, root_out, root_in, link, flat(x_nm), mid[:, :, :], sums[:, :], squares[:, :])

            @block.tensor
            def _(pe):
                pe.sem_inc(turned, CR)

                def step(i, k):
                    t = i * 2 + k
                    pe.wait_ge(scaled, done(t))
                    pe.wait_ge(summed, done(t - 2))
                    pe.sem_inc(pe_turn, 1)
                    for j in range(SUB):
                        last = nc.tensor.transpose(ps_z[k][:, j * D:(j + 1) * D], strided(us[:, k, :])[:, j, :], ident[0:D, 0:D])
                    last.then_inc(turned, 1)
                rounds(pe, step, NT, 2)

            @block.scalar
            def _(act):
                act.wait_ge(root_in, 1)
                nc.scalar.activation(squares[:, :], squares[:, :], ACT.Sqrt).then_inc(root_out, 1)
        dinv_ctx.close()

        x_t = sb("x_t", [D, NP])
        with ExitStack() as c:
            sem, own = stage_semaphores(c, "e0_")
            staged, turned, turned_sb, product, made, stored, pe_turn = (
                sem(n) for n in ("staged", "turned", "turned_sb", "product", "made", "stored", "pe_turn"))
            s_store = [sem(f"store{k}") for k in range(2)]
            xs = sb("e0_xs", [128, 2, SUB, D], ctx=c)
            xts = sb("e0_xts", [D, 2, GE], ctx=c)
            ys = sb("e0_ys", [128, 2, SUB, D], ctx=c)
            ps_t = [c.enter_context(nc.psum_tensor(f"e0_t{k}", [128, 512], fp32)) for k in range(2)]
            ps_p = [c.enter_context(nc.psum_tensor(f"e0_p{k}", [128, 512], fp32)) for k in range(2)]
            block = c.enter_context(stage_block(own))

            @block.vector
            def _(dve):
                dve.sem_inc(staged, CR)
                dve.sem_inc(made, CR)
                nc.vector.memset(acc[:, :], 0.0)

                def stage_x(i, k):
                    i, k = i + k // 2, k % 2
                    t = i * 2 + k
                    dve.wait_ge(turned, done(t - 2))
                    nc.vector.tensor_copy(xs[:, k], block_of(x_nm, t)).then_inc(staged, 1)
                stage_x(0, 0)

                def step(i, k):
                    t = i * 2 + k
                    if not isinstance(i, int) or t + 1 < NT:
                        stage_x(i, k + 1)
                    dve.wait_ge(product, done(t))
                    dve.wait_ge(stored, done(t - 2))
                    nc.vector.tensor_copy(ys[:, k].rearrange("p j f -> p (j f)"), ps_p[k][:, 0:SUB * D]).then_inc(made, 1)
                rounds(dve, step, NT, 2)

            @block.tensor
            def _(pe):
                pe.sem_inc(turned, CR)
                pe.sem_inc(product, CR)

                def turn(i, k):
                    i, k = i + k // 2, k % 2
                    t = i * 2 + k
                    pe.wait_ge(staged, done(t))
                    pe.wait_ge(turned_sb, done(t - 2))
                    pe.sem_inc(pe_turn, 1)
                    for j in range(SUB):
                        last = nc.tensor.transpose(ps_t[k][0:D, j * 128:(j + 1) * 128], xs[:, k, j, :], ident[:, :])
                    last.then_inc(turned, 1)
                turn(0, 0)

                def step(i, k):
                    t = i * 2 + k
                    if not isinstance(i, int) or t + 1 < NT:
                        turn(i, k + 1)
                    pe.wait_ge(turned_sb, done(t))
                    pe.wait_ge(made, done(t - 2))
                    for j in range(SUB):
                        last = nc.tensor.matmul(ps_p[k][:, j * D:(j + 1) * D], xts[:, k, j * 128:(j + 1) * 128], w_e1x[:, :], start=True, stop=True)
                    last.then_inc(product, 1)
                rounds(pe, step, NT, 2)

            @block.scalar
            def _(act):
                act.sem_inc(turned_sb, CR)

                def step(i, k):
                    t = i * 2 + k
                    act.wait_ge(turned, done(t))
                    act.wait_ge(product, done(t - 2))
                    nc.scalar.copy(strided(x_t[:, bass.ds(t * GE, GE)]), halves(ps_t[k][0:D, :]))
                    nc.scalar.copy(xts[:, k, :], ps_t[k][0:D, :]).then_inc(turned_sb, 1)
                rounds(act, step, NT, 2)

            @block.sync
            def _(sp):
                sp.sem_inc(stored, CR)

                def step(i, k):
                    t = sp.snap(i * 2 + k) if not isinstance(i, int) else i * 2 + k
                    sp.wait_ge(made, done(t))
                    sp.dma_start(group_rows(tab_t2, t), ys[:, k].rearrange("p j f -> p (j f)")).then_inc(s_store[k], 16)
                    sp.wait_ge(s_store[k], (i + 1) * 16)
                    sp.sem_inc(stored, 1)
                rounds(sp, step, NT, 2)

        with ExitStack() as c:
            sem, own = stage_semaphores(c, "e1_")
            s_idx = [sem(f"idx{k}") for k in range(4)]
            s_att = [sem(f"att{k}") for k in range(4)]
            s_rows = [gather_sem(f"e1_rows{k}") for k in range(4)]
            s_out = [sem(f"out{k}") for k in range(4)]
            turned, turned_sb, product, made, squared, counted, pool_turn, pe_turn, written, cleared, adds, squares_added = (
                sem(n) for n in ("turned", "turned_sb", "product", "made", "squared", "counted", "pool_turn", "pe_turn", "written", "cleared", "adds", "squares_added"))
            chain, moments, root_in, root_out = sem("chain"), sem("moments"), sem("root_in"), sem("root_out")
            idx = sb("e1_idx_t", [128, 4, SUB], i32, c)
            att = sb("e1_att_t", [128, 4, SUB, D], ctx=c)
            att_end = sb("e1_att_end", [128, SUB, D], ctx=c)
            rows = sb("e1_rows_t", [128, 4, SUB, D], ctx=c)
            att_t = sb("e1_att_tt", [D, 2, GE], ctx=c)
            h = sb("e1_h", [128, 4, SUB * D], ctx=c)
            sq = sb("e1_sq", [128, 2, SUB * D], ctx=c)
            sum_h, sum_q = sb("e1_sum_h", [128, SUB * D], ctx=c), sb("e1_sum_q", [128, SUB * D], ctx=c)
            mean, var = sb("e1_mean", [128, D], ctx=c), sb("e1_var", [128, D], ctx=c)
            tmp = sb("e1_tmp", [128, D], ctx=c)
            ps_t = [c.enter_context(nc.psum_tensor(f"e1_t{k}", [128, 512], fp32)) for k in range(2)]
            ps_p = [c.enter_context(nc.psum_tensor(f"e1_p{k}", [128, 512], fp32)) for k in range(2)]
            ps_q = c.enter_context(nc.psum_tensor("e1_q", [128, 512], fp32))
            block = c.enter_context(stage_block(own))
            att_dram = P["edge_attr_64"]

            def att_of(i, k):
                return att_end[:, :, :] if isinstance(i, int) and i * 4 + k == NG - 1 else att[:, k % 4]

            @block.sync
            def _(sp):
                sp.sem_inc(written, CR)

                def load(i, k):
                    i, k = i + k // 4, k % 4
                    g = sp.snap(i * 4 + k) if not isinstance(i, int) else i * 4 + k
                    sp.wait_ge(made, done(g - 4))
                    sp.dma_start(idx[:, k, :], group_rows(src_pad.unsqueeze(1), g)).then_inc(s_idx[k], 16)
                    if isinstance(i, int) and g == NG - 1:
                        sp.wait_ge(cleared, 1)
                        sp.dma_start(att_end[0:TROWS], att_dram[(NG - 1) * GE:E - TLEFT, :].rearrange("(p s) f -> p s f", s=SUB)).then_inc(s_att[k], 16)
                        sp.dma_start(att_end[TROWS:TROWS + 1, 0:TLEFT], att_dram[E - TLEFT:E, :].unsqueeze(0)).then_inc(s_att[k], 16)
                    else:
                        sp.dma_start(att[:, k].rearrange("p s f -> p (s f)"), group_rows(att_dram, g)).then_inc(s_att[k], 16)

                for k in range(2):
                    load(0, k)

                def step(i, k):
                    g = sp.snap(i * 4 + k) if not isinstance(i, int) else i * 4 + k
                    if not isinstance(i, int) or g + 2 < NG:
                        load(i, k + 2)
                    sp.wait_ge(made, done(g))
                    sp.dma_start(group_rows(h_edges, g), h[:, k, :]).then_inc(s_out[k], 16)
                rounds(sp, step, NG, 4)
                for k in range(4):
                    sp.wait_ge(s_out[k], (NG + 3 - k) // 4 * 16)

            @block.gpsimd
            def _(pool):
                pool.memset(att_end[:, :, :], 0.0).then_inc(cleared, 1)

                def step(i, k):
                    pool.wait_ge(s_idx[k], (i + 1) * 16)
                    pool.sem_inc(pool_turn, 1)
                    for s in range(SUB):
                        nc.gpsimd.indirect_dma_start(
                            out=rows[:, k, s, :], out_offset=None, in_=tab_t2,
                            in_offset=bass.IndirectOffsetOnAxis(ap=idx[:, k, s:s + 1], axis=0)).then_inc(s_rows[k], 16)
                rounds(pool, step, NG, 4)

            @block.tensor
            def _(pe):
                pe.sem_inc(turned, CR)
                pe.sem_inc(product, CR)

                def turn(i, k):
                    i, k = i + k // 4, k % 4
                    g = i * 4 + k
                    last_group = isinstance(i, int) and g == NG - 1
                    pe.wait_ge(s_att[k], (i + 1 + last_group) * 16)
                    pe.wait_ge(turned_sb, done(g - 2))
                    pe.sem_inc(pe_turn, 1)
                    for s in range(SUB):
                        last = nc.tensor.transpose(ps_t[k % 2][0:D, s * 128:(s + 1) * 128], att_of(i, k)[:, s, :], ident[:, :])
                    last.then_inc(turned, 1)
                turn(0, 0)

                def step(i, k):
                    g = i * 4 + k
                    if not isinstance(i, int) or g + 1 < NG:
                        turn(i, k + 1)
                    pe.wait_ge(turned_sb, done(g))
                    pe.wait_ge(made, done(g - 2))
                    for s in range(SUB):
                        last = nc.tensor.matmul(ps_p[k % 2][:, s * D:(s + 1) * D], att_t[:, k % 2, s * 128:(s + 1) * 128], w_e1e[:, :], start=True, stop=True)
                    last.then_inc(product, 1)
                rounds(pe, step, NG, 4)
                pe.wait_ge(adds, done(NG - 1))
                pe.wait_ge(squares_added, done(NG - 1))
                nc.tensor.matmul(ps_q[:, 0:SUB * D], ones_sq[:, :], sum_h[:, :], start=True, stop=True)
                nc.tensor.matmul(ps_q[:, SUB * D:2 * SUB * D], ones_sq[:, :], sum_q[:, :], start=True, stop=True).then_inc(moments, 1)

            @block.scalar
            def _(act):
                act.sem_inc(turned_sb, CR)
                act.sem_inc(squared, CR)

                def copy_turned(i, k):
                    i, k = i + k // 4, k % 4
                    g = i * 4 + k
                    act.wait_ge(turned, done(g))
                    act.wait_ge(product, done(g - 2))
                    nc.scalar.copy(att_t[:, k % 2, :], ps_t[k % 2][0:D, :]).then_inc(turned_sb, 1)
                copy_turned(0, 0)

                def step(i, k):
                    g = i * 4 + k
                    if not isinstance(i, int) or g + 1 < NG:
                        copy_turned(i, k + 1)
                    act.wait_ge(made, done(g))
                    act.wait_ge(squares_added, done(g - 2))
                    nc.scalar.activation(sq[:, k % 2, :], h[:, k, :], ACT.Square).then_inc(squared, 1)
                rounds(act, step, NG, 4)
                act.wait_ge(root_in, 1)
                nc.scalar.activation(var[:, :], var[:, :], ACT.Sqrt).then_inc(root_out, 1)

            @block.vector
            def _(dve):
                link = linker(dve, chain)
                link(nc.vector.memset(sum_h[:, :], 0.0))
                link(nc.vector.memset(sum_q[:, :], 0.0))
                for s_ in (made, adds, squares_added):
                    dve.sem_inc(s_, CR)

                def step(i, k, previous=True):
                    g = i * 4 + k
                    dve.wait_ge(product, done(g))
                    dve.wait_ge(squared, done(g - 4))
                    if not isinstance(i, int) or i > 0:
                        dve.wait_ge(s_out[k], i * 16)
                    dve.wait_ge(s_rows[k], (i + 1) * 64)
                    nc.vector.tensor_tensor(h[:, k, :], ps_p[k % 2][:, 0:SUB * D], rows[:, k].rearrange("p s f -> p (s f)"), ALU.add).then_inc(made, 1)
                    if previous:
                        dve.wait_ge(squared, done(g - 1))
                        dve.wait_ge(squares_added, done(g - 2))
                        nc.vector.tensor_tensor(sum_q[:, :], sum_q[:, :], sq[:, (k + 1) % 2, :], ALU.add).then_inc(squares_added, 1)
                    dve.wait_ge(made, done(g))
                    dve.wait_ge(adds, done(g - 1))
                    nc.vector.tensor_tensor(sum_h[:, :], sum_h[:, :], h[:, k, :], ALU.add).then_inc(adds, 1)
                for k in range(4):
                    step(0, k, k > 0)
                with dve.Fori(1, NG // 4) as i:
                    for k in range(4):
                        step(i, k)
                for k in range(NG % 4):
                    step(NG // 4, k)
                dve.wait_ge(squared, done(NG - 1))
                dve.wait_ge(squares_added, done(NG - 2))
                nc.vector.tensor_tensor(sum_q[:, :], sum_q[:, :], sq[:, (NG - 1) % 2, :], ALU.add).then_inc(squares_added, 1)
                dve.wait_ge(moments, 1)
                by_sub = lambda o: ps_q[:, o:o + SUB * D].rearrange("p (s f) -> p f s", s=SUB)
                link(nc.vector.tensor_reduce(mean[:, :], by_sub(0), AX.X, ALU.add))
                link(nc.vector.tensor_reduce(var[:, :], by_sub(SUB * D), AX.X, ALU.add))
                link(nc.vector.tensor_scalar(mean[:, :], mean[:, :], 1.0 / E, None, ALU.mult))
                link(nc.vector.tensor_tensor(tmp[:, :], mean[:, :], mean[:, :], ALU.mult))
                link(nc.vector.tensor_scalar(var[:, :], var[:, :], 1.0 / E, EPS, ALU.mult, ALU.add))
                nc.vector.tensor_tensor(var[:, :], var[:, :], tmp[:, :], ALU.subtract).then_inc(root_in, 1)
                dve.wait_ge(root_out, 1)
                link(nc.vector.reciprocal(var[:, :], var[:, :]))
                link(nc.vector.tensor_tensor(bn_scale[:, :], var[:, :], row_g1[:, :], ALU.mult))
                link(nc.vector.tensor_tensor(mean[:, :], mean[:, :], row_b1[:, :], ALU.add))
                link(nc.vector.tensor_tensor(mean[:, :], row_b1[:, :], mean[:, :], ALU.subtract))
                link(nc.vector.tensor_tensor(mean[:, :], mean[:, :], bn_scale[:, :], ALU.mult))
                nc.vector.tensor_tensor(bn_shift[:, :], mean[:, :], row_be1[:, :], ALU.add)

        with ExitStack() as c:
            PAIRS, TURN = (NG + 1) // 2, 8
            sem, own = stage_semaphores(c, "e2_")
            s_h = [sem(f"h{k}") for k in range(4)]
            scaled, shifted, message, hot, summed, added = (sem(n) for n in ("scaled", "shifted", "message", "hot", "summed", "added"))
            h = sb("e2_h", [128, 4, 2 * SUB, D], ctx=c)
            hs = sb("e2_hs", [128, 4, 2 * SUB, D], ctx=c)
            msg = sb("e2_msg", [128, 2, 2 * SUB, D], ctx=c)
            onehot = sb("e2_onehot", [128, 4, 2 * SUB, W], ctx=c)
            ps_s = [c.enter_context(nc.psum_tensor(f"e2_s{k}", [128, 512], fp32)) for k in range(2)]
            gen = general_path(c, sem, "e2", D, dst_pad, [], msg[:, 0, 0:SUB], ps_s[0])
            gen_h, gen_shifted, gen_scaled = sem("gen_h"), sem("gen_shifted"), sem("gen_scaled")
            block = c.enter_context(stage_block(own))
            scale_bc = bn_scale[:, :].unsqueeze(1).to_broadcast([128, 2 * SUB, D])
            shift_bc = bn_shift[:, :].unsqueeze(1).to_broadcast([128, 2 * SUB, D])

            def groups_of(p):
                return 1 if isinstance(p, int) and 2 * p + 1 == NG else 2

            @block.sync
            def _(sp):
                def general():
                    gen.sync(sp, lambda g: sp.dma_start(h[:, 0, 0:SUB].rearrange("p s f -> p (s f)"), group_rows(h_edges, g)).then_inc(gen_h, 16))

                def windows():
                    def step(i, k):
                        p = sp.snap(i * TURN + k) if not isinstance(i, int) else i * TURN + k
                        sp.wait_ge(scaled, done(p - 4))
                        if groups_of(p) == 2:
                            pair = h_edges[0:(NG // 2) * 2 * GE, :].rearrange("(x q p s) f -> x p q (s f)", q=2, p=LANES, s=SUB)
                            sp.dma_start(h[:, k % 4].rearrange("p (q s) f -> p q (s f)", q=2), pair[bass.ds(p, 1)].rearrange("a p q r -> (a p) q r")).then_inc(s_h[k % 4], 16)
                        else:
                            sp.dma_start(h[:, k % 4, 0:SUB].rearrange("p s f -> p (s f)"), group_rows(h_edges, NG - 1)).then_inc(s_h[k % 4], 16)
                    rounds(sp, step, PAIRS, TURN)

                by_flag(sp, general, windows)

            @block.gpsimd
            def _(pool):
                def general():
                    pool.sem_inc(scaled, 1)

                def windows():
                    pool.sem_inc(scaled, CR)

                    def step(i, k):
                        p = i * TURN + k
                        n = groups_of(p) * SUB
                        pool.wait_ge(s_h[k % 4], (i * (TURN // 4) + k // 4 + 1) * 16)
                        pool.wait_ge(message, done(p - 4))
                        nc.gpsimd.tensor_tensor(hs[:, k % 4, 0:n], h[:, k % 4, 0:n], scale_bc[:, 0:n], ALU.mult).then_inc(scaled, 1)
                    rounds(pool, step, PAIRS, TURN)

                by_flag(pool, general, windows)

            @block.vector
            def _(dve):
                def general():
                    def make(g):
                        dve.wait_ge(gen_h, (g + 1) * 16)
                        nc.vector.tensor_tensor(hs[:, 0, 0:SUB], h[:, 0, 0:SUB], scale_bc[:, 0:SUB], ALU.mult).then_inc(gen_scaled, 1)
                        dve.wait_ge(gen_scaled, g + 1)
                        nc.vector.tensor_tensor(hs[:, 0, 0:SUB], hs[:, 0, 0:SUB], shift_bc[:, 0:SUB], ALU.add).then_inc(gen_shifted, 1)
                    gen.vector(dve, make)

                def windows():
                    for s_ in (hot, shifted):
                        dve.sem_inc(s_, CR)
                    dve.sem_inc(added, 1)
                    iota_pair = iota_w[:, 0:1, :].to_broadcast([128, 2 * SUB, W])

                    def heat(i, k):
                        i, k = i + k // TURN, k % TURN
                        p = i * TURN + k
                        n = groups_of(p)
                        here = rel[:, bass.ds(p * 2, n), :].rearrange("p a s -> p (a s)")
                        nc.vector.tensor_tensor(onehot[:, k % 4, 0:n * SUB], iota_pair[:, 0:n * SUB], bc_last(here, W), ALU.is_equal).then_inc(hot, 1)

                    def shift(i, k):
                        i, k = i + k // TURN, k % TURN
                        p = i * TURN + k
                        n = groups_of(p)
                        dve.wait_ge(scaled, done(p))
                        nc.vector.tensor_tensor(hs[:, k % 4, 0:n * SUB], hs[:, k % 4, 0:n * SUB], shift_bc[:, 0:n * SUB], ALU.add).then_inc(shifted, 1)
                    for k in range(2):
                        heat(0, k)
                        shift(0, k)

                    def step(i, k):
                        p = i * TURN + k
                        n = groups_of(p)
                        ahead = not isinstance(i, int) or p + 2 < PAIRS
                        if ahead:
                            heat(i, k + 2)
                        _, starts = nc.values_load_multi_w_load_instructions(
                            base[0:1, bass.ds(p * 2, n)], engines=[mybir.EngineType.DVE], min_val=0, max_val=N,
                            skip_runtime_bounds_check_because=SAFE)
                        dve.wait_ge(summed, done(p))
                        for q in range(n):
                            dve.wait_ge(added, p * 2 + q + 1)
                            nc.vector.tensor_tensor(acc[0:D, bass.ds(starts[q], W)], acc[0:D, bass.ds(starts[q], W)],
                                                    ps_s[k % 2][0:D, q * W:(q + 1) * W], ALU.add).then_inc(added, 1)
                            if q == 0 and ahead:
                                shift(i, k + 2)
                    turns = (PAIRS - 3) // TURN
                    with dve.Fori(0, turns) as i:
                        for k in range(TURN):
                            step(i, k)
                    for k in range(PAIRS - turns * TURN):
                        step(turns + k // TURN, k % TURN)

                by_flag(dve, general, windows)

            @block.scalar
            def _(act):
                def general():
                    def step(g):
                        act.wait_ge(gen_shifted, g + 1)
                        nc.scalar.activation(msg[:, 0, 0:SUB], hs[:, 0, 0:SUB], ACT.Silu).then_inc(gen.message, 1)
                    gen.each_group(act, step)

                def windows():
                    act.sem_inc(message, CR)

                    def step(i, k):
                        p = i * TURN + k
                        n = groups_of(p) * SUB
                        act.wait_ge(shifted, done(p))
                        act.wait_ge(summed, done(p - 2))
                        nc.scalar.activation(msg[:, k % 2, 0:n], hs[:, k % 4, 0:n], ACT.Silu).then_inc(message, 1)
                    rounds(act, step, PAIRS, TURN)

                by_flag(act, general, windows)

            @block.tensor
            def _(pe):
                def general():
                    gen.tensor(pe)

                def windows():
                    pe.sem_inc(summed, CR)

                    def step(i, k):
                        p = i * TURN + k
                        pe.wait_ge(hot, done(p))
                        if not isinstance(p, int) or p >= 2:
                            pe.wait_ge(added, 2 * (p - 1) + 1)
                        pe.wait_ge(message, done(p))
                        for q in range(groups_of(p)):
                            for s in range(SUB):
                                last = nc.tensor.matmul(ps_s[k % 2][0:D, q * W:(q + 1) * W], msg[:, k % 2, q * SUB + s, :], onehot[:, k % 4, q * SUB + s, :],
                                                        start=s == 0, stop=s == SUB - 1)
                        last.then_inc(summed, 1)
                    peeled(pe, step, PAIRS, TURN)

                by_flag(pe, general, windows)

        with ExitStack() as c:
            sem, own = stage_semaphores(c, "e3_")
            ready, product, copied, chain, centre, root_in, root_out, silu_out, staged, turned, summed, pe_turn, s_cnt = (
                sem(n) for n in ("ready", "product", "copied", "chain", "centre", "root_in", "root_out", "silu_out", "staged", "turned", "summed", "pe_turn", "s_cnt"))
            s_tab = sem("tab")
            h_t = sb("e3_h_t", [D, NP], ctx=c)
            sq_t = sb("e3_sq_t", [D, NP], ctx=c)
            hs = sb("e3_hs", [D, 2, GE], ctx=c)
            col = sb("e3_col", [D, 6], ctx=c)
            sums, squares = sb("e3_sums", [128, NT * SUB], ctx=c), sb("e3_squares", [128, NT * SUB], ctx=c)
            mid = sb("e3_mid", [128, NT * SUB, D], ctx=c)
            ps_p = [c.enter_context(nc.psum_tensor(f"e3_p{k}", [128, 512], fp32)) for k in range(2)]
            ps_z = [c.enter_context(nc.psum_tensor(f"e3_z{k}", [128, 512], fp32)) for k in range(2)]
            block = c.enter_context(stage_block(own))

            @block.sync
            def _(sp):
                sp.dma_start(sq_t[:, :], cnt_dram.unsqueeze(0).to_broadcast([D, NP])).then_inc(s_cnt, 16)
                sp.wait_ge(root_in, 4)
                sp.dma_start(tab_x3[0:NP, :].rearrange("(t p j) f -> p t (j f)", p=LANES, j=SUB),
                             z_nm[:, :, :, :].rearrange("p t j f -> p t (j f)")).then_inc(s_tab, 16)
                sp.wait_ge(s_tab, 16)

            @block.tensor
            def _(pe):
                pe.sem_inc(product, CR)
                pe.sem_inc(turned, CR)
                pe.wait_ge(ready, 1)

                def multiply(i, k):
                    t = i * 2 + k
                    pe.wait_ge(copied, done(t - 2))
                    nc.tensor.matmul(ps_p[k][:, :], w_n2x[:, :], x_t[:, bass.ds(t * GE, GE)], start=True, stop=False)
                    nc.tensor.matmul(ps_p[k][:, :], w_n2a[:, :], acc[0:D, bass.ds(t * GE, GE)], start=False, stop=True).then_inc(product, 1)
                rounds(pe, multiply, NT, 2)

                def turn(i, k):
                    t = i * 2 + k
                    pe.wait_ge(staged, done(t))
                    pe.wait_ge(summed, done(t - 2))
                    pe.sem_inc(pe_turn, 1)
                    for j in range(SUB):
                        last = nc.tensor.transpose(ps_z[k][:, j * D:(j + 1) * D], strided(hs[:, k, :])[:, j, :], ident[0:D, 0:D])
                    last.then_inc(turned, 1)
                rounds(pe, turn, NT, 2)

            @block.scalar
            def _(act):
                act.sem_inc(copied, CR)
                act.sem_inc(staged, CR)

                def copy_product(i, k):
                    t = i * 2 + k
                    act.wait_ge(product, done(t))
                    nc.scalar.copy(h_t[:, bass.ds(t * GE, GE)], ps_p[k][0:D, :]).then_inc(copied, 1)
                rounds(act, copy_product, NT, 2)
                act.wait_ge(root_in, 1)
                nc.scalar.activation(col[:, 1:2], col[:, 1:2], ACT.Sqrt).then_inc(root_out, 1)
                act.wait_ge(root_in, 2)

                def finish(i, k):
                    t = i * 2 + k
                    act.wait_ge(turned, done(t - 2))
                    nc.scalar.activation(hs[:, k, :], h_t[:, bass.ds(t * GE, GE)], ACT.Silu, bias=col[:, 3:4], scale=col[:, 2:3]).then_inc(staged, 1)
                rounds(act, finish, NT, 2)
                act.wait_ge(root_in, 3)
                nc.scalar.activation(squares[:, :], squares[:, :], ACT.Sqrt).then_inc(root_out, 1)

            @block.vector
            def _(dve):
                link = linker(dve, chain)
                dve.sem_inc(summed, CR)
                dve.wait_ge(s_cnt, 16)
                link(nc.vector.tensor_scalar(sq_t[:, :], sq_t[:, :], 1.0, None, ALU.max))
                link(nc.vector.reciprocal(sq_t[:, :], sq_t[:, :]))
                nc.vector.tensor_tensor(acc[0:D, :], acc[0:D, :], sq_t[:, :], ALU.mult).then_inc(ready, 1)
                dve.wait_ge(ready, 1)
                dve.wait_ge(copied, done(NT - 1))
                link(nc.vector.tensor_reduce(col[:, 0:1], h_t[:, 0:N], AX.X, ALU.add))
                link(nc.vector.tensor_scalar(col[:, 0:1], col[:, 0:1], 1.0 / N, None, ALU.mult))
                link(nc.vector.tensor_scalar(h_t[:, :], h_t[:, :], col[:, 0:1], None, ALU.subtract))
                link(nc.vector.tensor_tensor(sq_t[:, 0:N], h_t[:, 0:N], h_t[:, 0:N], ALU.mult))
                link(nc.vector.tensor_reduce(col[:, 1:2], sq_t[:, 0:N], AX.X, ALU.add))
                nc.vector.tensor_scalar(col[:, 1:2], col[:, 1:2], 1.0 / N, EPS, ALU.mult, ALU.add).then_inc(root_in, 1)
                dve.wait_ge(root_out, 1)
                link(nc.vector.reciprocal(col[:, 1:2], col[:, 1:2]))
                link(nc.vector.tensor_tensor(col[:, 2:3], col[:, 1:2], col_n2[:, 1:2], ALU.mult))
                link(nc.vector.tensor_tensor(col[:, 4:5], col[:, 0:1], col_n2[:, 0:1], ALU.add))
                link(nc.vector.tensor_tensor(col[:, 5:6], col[:, 0:1], col_n2[:, 0:1], ALU.add))
                link(nc.vector.tensor_tensor(col[:, 4:5], col[:, 4:5], col[:, 5:6], ALU.subtract))
                link(nc.vector.tensor_tensor(col[:, 4:5], col[:, 4:5], col[:, 2:3], ALU.mult))
                nc.vector.tensor_tensor(col[:, 3:4], col[:, 4:5], col_n2[:, 2:3], ALU.add).then_inc(root_in, 1)

                def step(i, k):
                    t = i * 2 + k
                    dve.wait_ge(turned, done(t))
                    nc.vector.tensor_tensor(block_of(z_nm, t), ps_z[k][:, 0:SUB * D].rearrange("p (j f) -> p j f", j=SUB), block_of(x_nm, t), ALU.add).then_inc(summed, 1)
                rounds(dve, step, NT, 2)
                dve.wait_ge(summed, done(NT - 1))
                z, mid_ = flat(z_nm), mid[:, :, :]
                link(nc.vector.tensor_reduce(sums[:, :], z, AX.X, ALU.add))
                link(nc.vector.tensor_scalar(sums[:, :], sums[:, :], 1.0 / D, None, ALU.mult))
                link(nc.vector.tensor_tensor(z, z, bc_last(sums[:, :], D), ALU.subtract))
                link(nc.vector.tensor_tensor(mid_, z, z, ALU.mult))
                link(nc.vector.tensor_reduce(squares[:, :], mid_, AX.X, ALU.add))
                nc.vector.tensor_scalar(squares[:, :], squares[:, :], 1.0 / D, EPS, ALU.mult, ALU.add).then_inc(root_in, 1)
                dve.wait_ge(root_out, 2)
                link(nc.vector.reciprocal(squares[:, :], squares[:, :]))
                nc.vector.tensor_tensor(z, z, bc_last(squares[:, :], D), ALU.mult).then_inc(root_in, 1)

        total = sb("total", [128, NT, SUB, D + 1])
        with ExitStack() as c:
            sem, own = stage_semaphores(c, "r1_")
            s_x, chain, split_done, zero_set, finished, ones_set, gen_zero, gen_out, pe_turn = (
                sem(n) for n in ("s_x", "chain", "split_done", "zero_set", "finished", "ones_set", "gen_zero", "gen_out", "pe_turn"))
            turned, turned_sb, multiplied = ([sem(f"{n}{q}") for q in range(2)] for n in ("turned", "turned_sb", "multiplied"))
            SLOTS = 2
            s_block = [sem(f"block{k}") for k in range(SLOTS)]
            SIZES = (8, 4)
            batches, h0 = [], 0
            while h0 < HI:
                kind = len(batches) % 2
                batches.append((kind, h0, min(SIZES[kind], HI - h0)))
                h0 += batches[-1][2]
            COUNT = [sum(kind == q for kind, _, _ in batches) for q in range(2)]
            LAST = batches[-1][1]
            assert len(batches) % 2 and LAST * D == 512 * (HI * D // 512)
            rest = lane_key[:, 0, 0:(HI - LAST) * D]
            rest_added = sem("rest_added")

            def plan(blocks):
                numbers, steps = [0, 0], []
                for k in range(blocks):
                    for kind, first, size in batches:
                        steps.append((k, kind, numbers[kind], first, size))
                        numbers[kind] += 1
                return steps
            x_rows = sb("r1_x_rows", [128, NDL, D], ctx=c)
            x_parts = sb("r1_x_parts", [128, 3, NDL, D], bf16, c)
            block_counts = sb("r1_block_counts", [128, SLOTS, LANES, HI], bf16, c)
            turned_counts = [sb(f"r1_turned_counts{q}", [128, 2, SIZES[q], LANES], bf16, c) for q in range(2)]
            zero_b = sb("r1_zero_b", [128, 512], bf16, c)
            rows = sb("r1_rows", [128, SUB, D + 1], ctx=c)
            PER_BANK = 512 // D
            BANKS = -(-HI // PER_BANK)
            x_now = sb("r1_x_now", [128, SLOTS, 3, D], bf16, c)
            x_set = sem("x_set")
            ps_sum = [c.enter_context(nc.psum_tensor(f"r1_sum{k}", [128, 512], fp32)) for k in range(BANKS)]
            ps_half = ps_sum[-1][:, 512 - SIZES[1] * LANES // 2:512].bitcast(bf16).rearrange("p (n e) -> p n e", n=SIZES[1])
            ps_t = [c.enter_context(nc.psum_tensor("r1_t", [128, SIZES[0], LANES], bf16)), ps_half]
            gen = general_path(c, sem, "r1", D + 1, src_pad, [(tab_x3, dst_pad, rows[:, :, 0:D])], rows, ps_sum[0])
            block = c.enter_context(stage_block(own))

            @block.sync
            def _(sp):
                def general():
                    gen.sync(sp)
                    sp.wait_ge(gen.begun, NG + 1)
                    for t in range(NT):
                        sp.dma_start(sums_dram[t * GE:(t + 1) * GE, :].rearrange("n f -> f n"), acc[:, t * GE:(t + 1) * GE],
                                     allow_slow_non_contiguous=True).then_inc(gen_out, 16)
                    sp.wait_ge(gen_out, NT * 16)
                    sp.dma_start(total[:, :, :, :].rearrange("p t j f -> p t (j f)"),
                                 sums_dram.rearrange("(t p j) f -> p t (j f)", p=LANES, j=SUB)).then_inc(gen_out, 16)
                    sp.wait_ge(gen_out, (NT + 1) * 16)

                def dense():
                    sp.sem_inc(s_x, 1)
                    sp.dma_start(x_rows[:, :, :], tab_x3[0:NDL * LANES, :].rearrange("(b p) f -> p b f", p=LANES)).then_inc(s_x, 16)

                    def step(i, k):
                        b = sp.snap(i * 2 + k) if not isinstance(i, int) else i * 2 + k
                        if not isinstance(b, int) or b >= 2:
                            sp.wait_ge(turned[0], done((b - 1) * COUNT[0] - 1))
                        sp.dma_start(block_counts[:, k].rearrange("p d h -> p (d h)"),
                                     destinations(b, LANES)).then_inc(s_block[k], 16)
                    peeled(sp, step, NDL, 2)

                by_flag(sp, general, dense)

            @block.gpsimd
            def _(pool):
                by_flag(pool, lambda: gen.gpsimd(pool), lambda: pool.sem_inc(gen.turn, 1))

            @block.vector
            def _(dve):
                nc.vector.memset(rows[:, :, D:D + 1], 1.0).then_inc(ones_set, 1)

                def general():
                    nc.vector.memset(acc[:, :], 0.0).then_inc(gen_zero, 1)
                    dve.wait_ge(gen_zero, 1)
                    gen.vector(dve)

                def dense():
                    link = linker(dve, chain)
                    nc.vector.memset(zero_b[:, :], 0.0).then_inc(zero_set, 1)
                    dve.sem_inc(x_set, CR)
                    dve.wait_ge(s_x, 17)
                    split(link, x_rows[:, :, :], [x_parts[:, q] for q in range(3)], x_rows[:, :, :])

                    dve.sem_inc(turned_sb[1], CR)
                    dve.sem_inc(rest_added, CR)
                    link(nc.vector.memset(rest, 0.0))

                    def pair(i, blocks=2):
                        for k, kind, number, first, size in plan(blocks):
                            b = i * 2 + k
                            if first == 0:
                                if not isinstance(b, int) or b >= 2:
                                    dve.wait_ge(multiplied[0], done((b - 1) * COUNT[0] - 1))
                                nc.vector.tensor_copy(x_now[:, k], x_parts[:, :, bass.ds(b, 1), :].rearrange("p q a f -> p (q a) f")).then_inc(x_set, 1)
                            if kind == 1:
                                at = i * (2 * COUNT[1]) + number
                                dve.wait_ge(turned[1], done(at))
                                dve.wait_ge(multiplied[1], done(at - 2))
                                nc.vector.tensor_copy(turned_counts[1][:, number % 2, 0:size], ps_t[1][:, 0:size]).then_inc(turned_sb[1], 1)
                            if first == LAST:
                                dve.wait_ge(multiplied[0], done(i * (2 * COUNT[0]) + number))
                                dve.wait_ge(rest_added, done(b - 1))
                                nc.vector.tensor_tensor(rest, rest, ps_sum[-1][:, 0:size * D], ALU.add).then_inc(rest_added, 1)
                    pair(0)
                    with dve.Fori(1, NDL // 2) as i:
                        pair(i)
                    if NDL % 2:
                        pair(NDL // 2, 1)
                    for q in range(2):
                        dve.wait_ge(multiplied[q], done(NDL * COUNT[q] - 1))
                    tot = total[:, :, :, :].rearrange("p t j f -> p (t j) f")
                    nc.vector.tensor_copy(tot[:, :, D], deg_nm[:, :])
                    dve.wait_ge(rest_added, done(NDL - 1))
                    nc.vector.tensor_copy(tot[:, LAST:HI, 0:D], rest.rearrange("p (h f) -> p h f", f=D))
                    for n in range(0, BANKS - 1, 2):
                        cols = min(PER_BANK, HI - n * PER_BANK)
                        nc.vector.tensor_copy(tot[:, n * PER_BANK:n * PER_BANK + cols, 0:D],
                                              ps_sum[n][:, 0:cols * D].rearrange("p (h f) -> p h f", f=D))

                by_flag(dve, general, dense)

            @block.tensor
            def _(pe):
                def general():
                    pe.wait_ge(ones_set, 1)
                    gen.tensor(pe)

                def dense():
                    for s_ in turned + multiplied:
                        pe.sem_inc(s_, CR)
                    pe.wait_ge(zero_set, 1)
                    for n in range(BANKS - 1):
                        nc.tensor.matmul(ps_sum[n][:, :], zero_b[:, 0:128], zero_b[:, :], start=True, stop=True)

                    def turn(i, k, kind, number, first, size):
                        if first == 0:
                            pe.wait_ge(s_block[k], (i + 1) * 16)
                        if first == batches[1][1]:
                            pe.wait_ge(rest_added, done(i * 2 + k - 1))
                        pe.wait_ge(turned_sb[kind], done(i * (2 * COUNT[kind]) + number - 1))
                        pe.sem_inc(pe_turn, 1)
                        for n in range(size):
                            last = nc.tensor.transpose(ps_t[kind][:, n, :], block_counts[:, k, :, first + n], ident_b[:, :])
                        last.then_inc(turned[kind], 1)

                    def multiply(i, k, kind, number, first, size):
                        if first == 0:
                            pe.wait_ge(x_set, done(i * 2 + k))
                        pe.wait_ge(turned_sb[kind], done(i * (2 * COUNT[kind]) + number))
                        for n in range(size):
                            h = first + n
                            for part in range(3):
                                last = nc.tensor.matmul(ps_sum[h // PER_BANK][:, h % PER_BANK * D:(h % PER_BANK + 1) * D],
                                                        turned_counts[kind][:, number % 2, n, :], x_now[:, k, part, :], start=h == LAST and part == 0, stop=True, skip_group_check=True)
                        last.then_inc(multiplied[kind], 1)

                    def pair(i, blocks=2):
                        steps = plan(blocks)
                        for n in range(len(steps) + 2):
                            product_first = n >= 2 and steps[n - 2][3:] == batches[-1][1:]
                            if product_first:
                                multiply(i, *steps[n - 2])
                            if n < len(steps):
                                turn(i, *steps[n])
                            if n >= 2 and not product_first:
                                multiply(i, *steps[n - 2])
                    with pe.Fori(0, NDL // 2) as i:
                        pair(i)
                    if NDL % 2:
                        pair(NDL // 2, 1)

                by_flag(pe, general, dense)

            @block.scalar
            def _(act):
                def general():
                    act.wait_ge(ones_set, 1)

                def dense():
                    act.sem_inc(turned_sb[0], CR)

                    def pair(i, blocks=2):
                        for _, kind, number, first, size in plan(blocks):
                            if kind == 0:
                                at = i * (2 * COUNT[0]) + number
                                act.wait_ge(turned[0], done(at))
                                act.wait_ge(multiplied[0], done(at - 2))
                                nc.scalar.copy(turned_counts[0][:, number % 2, 0:size], ps_t[0][:, 0:size]).then_inc(turned_sb[0], 1)
                    with act.Fori(0, NDL // 2) as i:
                        pair(i)
                    if NDL % 2:
                        pair(NDL // 2, 1)
                    for q in range(2):
                        act.wait_ge(multiplied[q], done(NDL * COUNT[q] - 1))
                    tot = total[:, :, :, :].rearrange("p t j f -> p (t j) f")
                    for n in range(1, BANKS - 1, 2):
                        cols = min(PER_BANK, HI - n * PER_BANK)
                        nc.scalar.copy(tot[:, n * PER_BANK:n * PER_BANK + cols, 0:D],
                                       ps_sum[n][:, 0:cols * D].rearrange("p (h f) -> p h f", f=D))

                by_flag(act, general, dense)

        with ExitStack() as c:
            sem, own = stage_semaphores(c, "r2_")
            chain, staged, turned, turned_sb, product, summed, pe_turn, root_in, root_out, s_out = (
                sem(n) for n in ("chain", "staged", "turned", "turned_sb", "product", "summed", "pe_turn", "root_in", "root_out", "s_out"))
            R = D + 1
            rdeg = sb("r2_rdeg", [128, NT, SUB], ctx=c)
            ss = sb("r2_ss", [128, 2, SUB, R], ctx=c)
            sts = sb("r2_sts", [R, 2, GE], ctx=c)
            ps_t = [c.enter_context(nc.psum_tensor(f"r2_t{k}", [128, 512], fp32)) for k in range(2)]
            ps_p = [c.enter_context(nc.psum_tensor(f"r2_p{k}", [128, 512], fp32)) for k in range(2)]
            sums, squares = sb("r2_sums", [128, NT * SUB], ctx=c), sb("r2_squares", [128, NT * SUB], ctx=c)
            mid = sb("r2_mid", [128, NT * SUB, D], ctx=c)
            block = c.enter_context(stage_block(own))

            @block.sync
            def _(sp):
                sp.wait_ge(root_in, 2)
                sp.dma_start(out[0:NFULL * GE, :].rearrange("(t p j) f -> p t (j f)", p=LANES, j=SUB),
                             x_nm[:, 0:NFULL].rearrange("p t j f -> p t (j f)")).then_inc(s_out, 16)
                sp.dma_start(out[NFULL * GE:NFULL * GE + NREST * SUB, :].rearrange("(p j) f -> p (j f)", j=SUB),
                             x_nm[0:NREST, NFULL].rearrange("p j f -> p (j f)")).then_inc(s_out, 16)
                sp.dma_start(out[N - NLEFT:N, :].rearrange("(p j) f -> p (j f)", j=NLEFT),
                             x_nm[NREST:NREST + 1, NFULL, 0:NLEFT].rearrange("p j f -> p (j f)")).then_inc(s_out, 16)
                sp.wait_ge(s_out, 48)

            @block.vector
            def _(dve):
                link = linker(dve, chain)
                dve.sem_inc(staged, CR)
                dve.sem_inc(summed, CR)
                link(nc.vector.tensor_scalar(rdeg[:, :, :], total[:, :, :, D], 1.0, None, ALU.max))
                link(nc.vector.reciprocal(rdeg[:, :, :], rdeg[:, :, :]))

                def step(i, k):
                    t = i * 2 + k
                    dve.wait_ge(turned, done(t - 2))
                    nc.vector.tensor_tensor(ss[:, k], block_of(total, t), bc_last(per_node(rdeg, t), R), ALU.mult).then_inc(staged, 1)
                    dve.wait_ge(product, done(t))
                    nc.vector.tensor_tensor(block_of(x_nm, t), ps_p[k][:, 0:SUB * D].rearrange("p (j f) -> p j f", j=SUB), block_of(z_nm, t), ALU.add).then_inc(summed, 1)
                rounds(dve, step, NT, 2)
                dve.wait_ge(summed, done(NT - 1))
                z, mid_ = flat(x_nm), mid[:, :, :]
                link(nc.vector.tensor_reduce(sums[:, :], z, AX.X, ALU.add))
                link(nc.vector.tensor_scalar(sums[:, :], sums[:, :], 1.0 / D, None, ALU.mult))
                link(nc.vector.tensor_tensor(z, z, bc_last(sums[:, :], D), ALU.subtract))
                link(nc.vector.tensor_tensor(mid_, z, z, ALU.mult))
                link(nc.vector.tensor_reduce(squares[:, :], mid_, AX.X, ALU.add))
                nc.vector.tensor_scalar(squares[:, :], squares[:, :], 1.0 / D, EPS, ALU.mult, ALU.add).then_inc(root_in, 1)
                dve.wait_ge(root_out, 1)
                link(nc.vector.reciprocal(squares[:, :], squares[:, :]))
                nc.vector.tensor_tensor(z, z, bc_last(squares[:, :], D), ALU.mult).then_inc(root_in, 1)

            @block.tensor
            def _(pe):
                pe.sem_inc(turned, CR)
                pe.sem_inc(product, CR)

                def step(i, k):
                    t = i * 2 + k
                    pe.wait_ge(staged, done(t))
                    pe.wait_ge(turned_sb, done(t - 2))
                    pe.sem_inc(pe_turn, 1)
                    for j in range(SUB):
                        last = nc.tensor.transpose(ps_t[k][0:R, j * 128:(j + 1) * 128], ss[:, k, j, :], ident[:, :])
                    last.then_inc(turned, 1)
                    pe.wait_ge(turned_sb, done(t))
                    pe.wait_ge(summed, done(t - 2))
                    for j in range(SUB):
                        last = nc.tensor.matmul(ps_p[k][:, j * D:(j + 1) * D], sts[:, k, j * 128:(j + 1) * 128], w_3[:, :], start=True, stop=True)
                    last.then_inc(product, 1)
                rounds(pe, step, NT, 2)

            @block.scalar
            def _(act):
                act.sem_inc(turned_sb, CR)

                def step(i, k):
                    t = i * 2 + k
                    act.wait_ge(turned, done(t))
                    act.wait_ge(product, done(t - 2))
                    nc.scalar.copy(sts[:, k, :], ps_t[k][0:R, :]).then_inc(turned_sb, 1)
                rounds(act, step, NT, 2)
                act.wait_ge(root_in, 1)
                nc.scalar.activation(squares[:, :], squares[:, :], ACT.Sqrt).then_inc(root_out, 1)


_INS = ["x", "src", "dst", "edge_attr_32", "edge_attr_64", "L0_gnn_W_m1", "L0_gnn_b_m1", "L0_gnn_W_m2", "L0_gnn_b_m2",
        "L0_gnn_W_c1", "L0_gnn_b_c1", "L0_gnn_W_c2", "L0_gnn_b_c2", "L1_gnn_W1", "L1_gnn_b1", "L1_gnn_W2", "L1_gnn_b2",
        "L2_gnn_u", "L2_gnn_W1", "L2_gnn_b1", "L2_gnn_g1", "L2_gnn_be1", "L2_gnn_W2", "L2_gnn_b2", "L2_gnn_g2", "L2_gnn_be2",
        "L3_gnn_W", "L3_gnn_b"]


def kernel(**inputs):
    import numpy as np
    import concourse.bacc as bacc
    from concourse import mybir
    from concourse.bass_utils import run_bass_kernel_spmd

    nc = bacc.Bacc("TRN2", target_bir_lowering=False, num_devices=1)
    arrays = {name: np.ascontiguousarray(inputs[name]) for name in _INS if name not in ("L2_gnn_u", "L3_gnn_W")}
    arrays["L3_gnn_W_t"] = np.ascontiguousarray(np.asarray(inputs["L3_gnn_W"]).T)
    params = {n: nc.dram_tensor(f"in_{n}", a.shape, mybir.dt.from_np(a.dtype), kind="ExternalInput").ap() for n, a in arrays.items()}
    shape = arrays["x"].shape
    out = nc.dram_tensor("out", shape, mybir.dt.float32, kind="ExternalOutput").ap()
    build(nc, params, out)
    r = run_bass_kernel_spmd(nc, [{f"in_{n}": a for n, a in arrays.items()}], core_ids=[0])
    return r.results[0]["out"]
```
